# Optimizing a Trainium2 kernel written in Bass

```python
import numpy as np
import jax
import jax.numpy as jnp

def _softmax(x, axis=-1):
    return jax.nn.softmax(x, axis=axis)

def _gelu(x):
    return jax.nn.gelu(x, approximate=True)

def _silu(x):
    return jax.nn.silu(x)

def _sigmoid(x):
    return jax.nn.sigmoid(x)

def _layernorm(x, axis=-1, eps=1e-05):
    m = jnp.mean(x, axis=axis, keepdims=True)
    v = jnp.var(x, axis=axis, keepdims=True)
    return (x - m) / jnp.sqrt(v + eps)

def _scatter_add(tgt, idx, src, axis=0):
    return tgt.at[idx].add(src)

def _segment_sum(src, seg, n):
    return jax.ops.segment_sum(src, seg, n)
kernel_name = 'mk_adj_ffn_d1_adj_r2_e188a3'

def setup_inputs(seed: int=0):
    np.random.seed(seed)
    _w = jnp.asarray

    def _rec_inputs():
        import jax
        import jax.numpy as jnp
        _gk = jax.random.key(seed)
        x = -0.000929 + 1 * jax.random.normal(jax.random.fold_in(_gk, 1), (3327, 128), jnp.float32)
        _a = jax.random.bernoulli(jax.random.fold_in(_gk, 2), 0.00240457, (3327, 3327))
        _a = jnp.logical_or(_a, jnp.swapaxes(_a, -1, -2))
        _a = jnp.logical_or(_a, jnp.eye(3327, dtype=bool))
        _af = _a.astype(jnp.float32)
        _af = _af * jax.random.uniform(jax.random.fold_in(_gk, 3), (3327, 3327), jnp.float32, 0.05, 1)
        adj = _af
        return (x, adj)
    x, adj = _rec_inputs()

    def _L0_gnn_setup():
        import jax, jax.numpy as jnp
        import numpy as np
        N, H, HEADS = (2048, 128, 3)
        ALPHA = 0.2
        NEG_INF = -9000000000000000.0

        def _sign_adj(key, n, density):
            k1, k2 = jax.random.split(key)
            mask = jax.random.uniform(k1, (n, n)) < density
            sign = jnp.where(jax.random.uniform(k2, (n, n)) < 0.5, -1.0, 1.0)
            adj = jnp.where(mask, sign, 0.0).astype(jnp.float32)
            idx = jnp.arange(n)
            return adj.at[idx, idx].set(1.0)

        def _gru_cell(x, hstate, Wih, Whh, bih, bhh):
            gi = x @ Wih.T + bih
            gh = hstate @ Whh.T + bhh
            ir, iz, inn = jnp.split(gi, 3, axis=1)
            hr, hz, hn = jnp.split(gh, 3, axis=1)
            r = jax.nn.sigmoid(ir + hr)
            z = jax.nn.sigmoid(iz + hz)
            n = jnp.tanh(inn + r * hn)
            return (1.0 - z) * n + z * hstate

        def _gat_head(h, node_adj, edge_adj, W, a):
            hW = h @ W
            hp = (node_adj > 0).astype(hW.dtype) @ hW
            hm = (node_adj < 0).astype(hW.dtype) @ hW
            e_plus = jax.nn.leaky_relu(jnp.concatenate([hp, hm], axis=1) @ a, ALPHA)[:, 0]
            e_minus = jax.nn.leaky_relu(jnp.concatenate([hm, hp], axis=1) @ a, ALPHA)[:, 0]
            att = jnp.where(edge_adj > 0, e_plus[None, :], NEG_INF)
            att = jnp.where(edge_adj < 0, e_minus[None, :], att)
            att = jax.nn.softmax(att, axis=1)
            return att * edge_adj @ hW
        key = jax.random.key(seed)
        ks = jax.random.split(key, 16)
        std = 0.01
        gain = 1.414
        return {'h': jax.random.normal(ks[0], (N, H), jnp.float32), 'node_adj': _sign_adj(ks[1], N, 0.005), 'edge_adj': _sign_adj(ks[2], N, 0.005), 'gat_W': jax.random.normal(ks[3], (HEADS, H, H), jnp.float32) * (gain / np.sqrt(H, dtype=np.float32)), 'gat_a': jax.random.normal(ks[4], (HEADS, 2 * H, 1), jnp.float32) * 0.1, 'edge_Wih': jax.random.normal(ks[5], (3 * H, H), jnp.float32) * std, 'edge_Whh': jax.random.normal(ks[6], (3 * H, H), jnp.float32) * std, 'edge_bih': jnp.zeros((3 * H,), jnp.float32), 'edge_bhh': jnp.zeros((3 * H,), jnp.float32), 'node_Wih': jax.random.normal(ks[7], (3 * H, H), jnp.float32) * std, 'node_Whh': jax.random.normal(ks[8], (3 * H, H), jnp.float32) * std, 'node_bih': jnp.zeros((3 * H,), jnp.float32), 'node_bhh': jnp.zeros((3 * H,), jnp.float32)}
    _L0_gnn_all = _L0_gnn_setup()
    _L0_gnn_in = {k: v for k, v in _L0_gnn_all.items() if k in ('gat_W', 'gat_a', 'edge_Wih', 'edge_Whh', 'edge_bih', 'edge_bhh', 'node_Wih', 'node_Whh', 'node_bih', 'node_bhh')}
    del _L0_gnn_all

    def _L0_ffn_setup():
        import jax, jax.numpy as jnp
        import numpy as np
        E = 8
        K = 2
        D = 128
        H = 256
        DOUT = 128
        EPS = 1e-05
        key = jax.random.key(seed)
        ks = jax.random.split(key, 9)
        s = 0.02
        return {'x': jax.random.normal(ks[0], (4, 4096, D), jnp.float32), 'gamma': 1.0 + 0.05 * jax.random.normal(ks[1], (D,), jnp.float32), 'beta': 0.05 * jax.random.normal(ks[2], (D,), jnp.float32), 'Wr': 0.01 * jax.random.normal(ks[3], (D, E), jnp.float32), 'br': jnp.zeros((E,), jnp.float32), 'W1': s * jax.random.normal(ks[4], (E, D, H), jnp.float32), 'b1': s * jax.random.normal(ks[5], (E, H), jnp.float32), 'W2': s * jax.random.normal(ks[6], (E, H, DOUT), jnp.float32), 'b2': s * jax.random.normal(ks[7], (E, DOUT), jnp.float32)}
    _L0_ffn_all = _L0_ffn_setup()
    _L0_ffn_in = {k: v for k, v in _L0_ffn_all.items() if k in ('gamma', 'beta', 'Wr', 'br', 'W1', 'b1', 'W2', 'b2')}
    del _L0_ffn_all
    return {'x': x, 'adj': adj, 'L0_gnn_gat_W': _L0_gnn_in['gat_W'], 'L0_gnn_gat_a': _L0_gnn_in['gat_a'], 'L0_gnn_edge_Wih': _L0_gnn_in['edge_Wih'], 'L0_gnn_edge_Whh': _L0_gnn_in['edge_Whh'], 'L0_gnn_edge_bih': _L0_gnn_in['edge_bih'], 'L0_gnn_edge_bhh': _L0_gnn_in['edge_bhh'], 'L0_gnn_node_Wih': _L0_gnn_in['node_Wih'], 'L0_gnn_node_Whh': _L0_gnn_in['node_Whh'], 'L0_gnn_node_bih': _L0_gnn_in['node_bih'], 'L0_gnn_node_bhh': _L0_gnn_in['node_bhh'], 'L0_ffn_gamma': _L0_ffn_in['gamma'], 'L0_ffn_beta': _L0_ffn_in['beta'], 'L0_ffn_Wr': _L0_ffn_in['Wr'], 'L0_ffn_br': _L0_ffn_in['br'], 'L0_ffn_W1': _L0_ffn_in['W1'], 'L0_ffn_b1': _L0_ffn_in['b1'], 'L0_ffn_W2': _L0_ffn_in['W2'], 'L0_ffn_b2': _L0_ffn_in['b2']}

def reference(x, adj, L0_gnn_gat_W, L0_gnn_gat_a, L0_gnn_edge_Wih, L0_gnn_edge_Whh, L0_gnn_edge_bih, L0_gnn_edge_bhh, L0_gnn_node_Wih, L0_gnn_node_Whh, L0_gnn_node_bih, L0_gnn_node_bhh, L0_ffn_gamma, L0_ffn_beta, L0_ffn_Wr, L0_ffn_br, L0_ffn_W1, L0_ffn_b1, L0_ffn_W2, L0_ffn_b2):
    import jax
    import jax.numpy as jnp

    def _L0_gnn_ref(h, node_adj, edge_adj, gat_W, gat_a, edge_Wih, edge_Whh, edge_bih, edge_bhh, node_Wih, node_Whh, node_bih, node_bhh):
        import jax, jax.numpy as jnp
        import numpy as np
        N, H, HEADS = (2048, 128, 3)
        ALPHA = 0.2
        NEG_INF = -9000000000000000.0

        def _sign_adj(key, n, density):
            k1, k2 = jax.random.split(key)
            mask = jax.random.uniform(k1, (n, n)) < density
            sign = jnp.where(jax.random.uniform(k2, (n, n)) < 0.5, -1.0, 1.0)
            adj = jnp.where(mask, sign, 0.0).astype(jnp.float32)
            idx = jnp.arange(n)
            return adj.at[idx, idx].set(1.0)

        def _gru_cell(x, hstate, Wih, Whh, bih, bhh):
            gi = x @ Wih.T + bih
            gh = hstate @ Whh.T + bhh
            ir, iz, inn = jnp.split(gi, 3, axis=1)
            hr, hz, hn = jnp.split(gh, 3, axis=1)
            r = jax.nn.sigmoid(ir + hr)
            z = jax.nn.sigmoid(iz + hz)
            n = jnp.tanh(inn + r * hn)
            return (1.0 - z) * n + z * hstate

        def _gat_head(h, node_adj, edge_adj, W, a):
            hW = h @ W
            hp = (node_adj > 0).astype(hW.dtype) @ hW
            hm = (node_adj < 0).astype(hW.dtype) @ hW
            e_plus = jax.nn.leaky_relu(jnp.concatenate([hp, hm], axis=1) @ a, ALPHA)[:, 0]
            e_minus = jax.nn.leaky_relu(jnp.concatenate([hm, hp], axis=1) @ a, ALPHA)[:, 0]
            att = jnp.where(edge_adj > 0, e_plus[None, :], NEG_INF)
            att = jnp.where(edge_adj < 0, e_minus[None, :], att)
            att = jax.nn.softmax(att, axis=1)
            return att * edge_adj @ hW
        dn = jnp.diag(node_adj)
        de = jnp.diag(edge_adj)
        idx = jnp.arange(node_adj.shape[0])
        node_adj_norm = node_adj.at[idx, idx].add(-dn)
        edge_adj_norm = edge_adj.at[idx, idx].add(-de)
        node_support = node_adj_norm @ h
        edge_output = _gru_cell(node_support, h, edge_Wih, edge_Whh, edge_bih, edge_bhh)
        edge_support = _gat_head(h, node_adj_norm, edge_adj_norm, gat_W[0], gat_a[0])
        for i in range(1, HEADS):
            edge_support = edge_support + _gat_head(h, node_adj_norm, edge_adj_norm, gat_W[i], gat_a[i])
        edge_support = edge_support / HEADS
        node_output = _gru_cell(edge_support, h, node_Wih, node_Whh, node_bih, node_bhh)
        return de[:, None] * edge_output + dn[:, None] * node_output

    def _L0_ffn_ref(x, gamma, beta, Wr, br, W1, b1, W2, b2):
        import jax, jax.numpy as jnp
        import numpy as np
        E = 8
        K = 2
        D = 128
        H = 256
        DOUT = 128
        EPS = 1e-05
        mu = jnp.mean(x, axis=-1, keepdims=True)
        var = jnp.mean(jnp.square(x - mu), axis=-1, keepdims=True)
        xn = (x - mu) * jax.lax.rsqrt(var + EPS) * gamma + beta
        logits = jnp.einsum('bsd,de->bse', xn, Wr) + br
        top_vals, top_idx = jax.lax.top_k(logits, K)
        w = jax.nn.softmax(top_vals, axis=-1)
        w_full = jnp.einsum('bsk,bske->bse', w, jax.nn.one_hot(top_idx, E, dtype=w.dtype))
        y = jnp.zeros(x.shape[:-1] + (DOUT,), x.dtype)
        for e in range(E):
            h = jax.nn.gelu(jnp.einsum('bsd,dh->bsh', xn, W1[e]) + b1[e], approximate=False)
            y_e = jnp.einsum('bsh,hd->bsd', h, W2[e]) + b2[e]
            y = y + y_e * w_full[..., e, None]
        return y
    x = x + _L0_gnn_ref(_layernorm(x, axis=-1), adj, adj, L0_gnn_gat_W, L0_gnn_gat_a, L0_gnn_edge_Wih, L0_gnn_edge_Whh, L0_gnn_edge_bih, L0_gnn_edge_bhh, L0_gnn_node_Wih, L0_gnn_node_Whh, L0_gnn_node_bih, L0_gnn_node_bhh)
    x = x + _L0_ffn_ref(_layernorm(x, axis=-1)[None], L0_ffn_gamma, L0_ffn_beta, L0_ffn_Wr, L0_ffn_br, L0_ffn_W1, L0_ffn_b1, L0_ffn_W2, L0_ffn_b2)[0]
    return x

_drawn_inputs = setup_inputs


def setup_inputs(seed=0):
    import zlib

    import numpy as np

    out = dict(_drawn_inputs(seed))
    spreads = {'L0_gnn_edge_bih': (0.0, 0.374),
     'L0_gnn_edge_bhh': (0.0, 0.62),
     'L0_gnn_node_bih': (0.0, 0.389),
     'L0_gnn_node_bhh': (0.0, 0.599),
     'L0_ffn_br': (0.0, 0.395)}
    factors = {'L0_gnn_gat_W': 5.708,
     'L0_gnn_gat_a': 6.086,
     'L0_gnn_edge_Whh': 3.781,
     'L0_gnn_node_Wih': 5.685,
     'L0_gnn_node_Whh': 3.707,
     'L0_ffn_gamma': 8.0,
     'L0_ffn_beta': 8.0,
     'L0_ffn_Wr': 5.044,
     'L0_ffn_W1': 3.331,
     'L0_ffn_b1': 8.0,
     'L0_ffn_W2': 3.275,
     'L0_ffn_b2': 6.357}
    for name, (base, spread) in spreads.items():
        noise = np.random.default_rng([zlib.crc32(name.encode()), seed]).standard_normal(out[name].shape)
        drawn = base * np.exp(spread * noise) if base else spread * noise
        out[name] = jnp.asarray(drawn.astype(out[name].dtype))
    for name, factor in factors.items():
        out[name] = (out[name] * factor).astype(out[name].dtype)
    return out
```

```python
from contextlib import ExitStack

import concourse.bass as bass
from concourse import mybir
import numpy as np

N = 3327
H = 128
HEADS = 3
TILES = -(-N // 128)
NP = TILES * 128
CHUNK = 512
CHUNKS = [(c, min(CHUNK, NP - c)) for c in range(0, NP, CHUNK)]
PARTS = ((0, 12), (12, TILES))
ALPHA = 0.2
NEG_INF = -9e15
LOWEST = -3e38
EPS = 1e-5
E = 8
HID = 256
HALVES = HID // 128
BLOCK = 416
BLOCKS = NP // BLOCK
RSPLIT = 4
RT = BLOCK // RSPLIT
SCORES = 2 * HEADS
STAT = 3
UW = 32
HE = H + SCORES
GROWS = STAT * E
FREE = 2


def host_constants():
    ident = np.eye(128, dtype=np.float32)
    sum_parts = np.zeros((32, 32), np.float32)
    for q in range(STAT):
        for r in range(SCORES):
            sum_parts[1 + SCORES * q + r, r] = 1.0
    pick_score = np.zeros((32, SCORES, 128), np.float32)
    for r in range(SCORES):
        pick_score[r, r, :] = 1.0
    pick_expert = np.zeros((32, E, 128), np.float32)
    for q in range(STAT):
        for e in range(E):
            pick_expert[E * q + e, e, :] = 1.0
    iota = np.tile(np.arange(E, dtype=np.float32), (128, 1))
    return ident, sum_parts, pick_score, pick_expert, iota


class InOrder:

    def __init__(self, engine, semaphore):
        self.engine, self.semaphore, self.value = engine, semaphore, 0

    def done(self, instruction):
        instruction.then_inc(self.semaphore, 1)
        self.value = self.value + 1
        self.engine.wait_ge(self.semaphore, self.value)


LAYERS = {
    "gru": {"pe": ["heads", "edge", "node"],
            "act": ["attention", "edge gates", "node gates", "edge tanh", "node tanh"],
            "dve": ["edge candidate", "node candidate", "x"],
            "settled": 10},
    "norm": {"pe": ["mean", "variance", "mean again", "variance again"],
             "act": ["squares", "root", "squares again", "root again"],
             "dve": ["centred", "variance", "normalised", "centred again", "variance again",
                     "experts' input"],
             "settled": 11},
    "router": {"pe": ["logits", "gates"],
               "act": ["weights", "gates"],
               "dve": ["block", "gap", "gates"],
               "settled": 13},
}


def signalled(layer, who, g, steps):
    past = 1
    for name, lists in LAYERS.items():
        each = lists[who] if who == "settled" else len(lists[who])
        if name == layer:
            return g * each + (past + steps)
        past += BLOCKS * each


def apart(engine, waits):
    engine.sem_inc(waits, 1)


class Steps:

    def __init__(self, engine, layer, who, g, own=None):
        self.engine, self.layer, self.who, self.g, self.own = engine, layer, who, g, own
        self.signals, self.chain = [], 0

    def after(self, semaphore, who, name):
        done = LAYERS[self.layer][who].index(name) + 1
        self.engine.wait_ge(semaphore, signalled(self.layer, who, self.g, done))

    def before(self, semaphore, who):
        self.engine.wait_ge(semaphore, signalled(self.layer, who, self.g, 0))

    def step(self, instruction, semaphore, name):
        self.signals.append(name)
        instruction.then_inc(semaphore, 1)

    def settled(self, instruction):
        self.chain += 1
        instruction.then_inc(self.own, 1)
        self.engine.wait_ge(self.own, signalled(self.layer, "settled", self.g, self.chain))

    def end(self):
        assert self.signals == LAYERS[self.layer][self.who], self.signals
        if self.own is not None:
            assert self.chain == LAYERS[self.layer]["settled"], (self.layer, self.chain)


def graph_layer_kernel(nc, x, x_t, adj_rows, adj_cols, diag, ident_in, sum_parts_in, pick_score_in,
                       pick_expert_in, iota_in, gat_w, gat_w_t, gat_a, edge_wih_t, edge_whh_t, edge_bih,
                       edge_bhh, node_wih_t, node_whh_t, node_bih, node_bhh, gamma, beta, wr, br, w1, b1,
                       w2, b2, out_t):
    f32, bf16, i32, u32 = mybir.dt.float32, mybir.dt.bfloat16, mybir.dt.int32, mybir.dt.uint32
    ALU = mybir.AluOpType
    ACT = mybir.ActivationFunctionType
    AX = mybir.AxisListType
    ctx = ExitStack()
    with ctx:
        def sb(name, shape, dt=f32):
            return ctx.enter_context(nc.sbuf_tensor(name, shape, dt))

        def sem(name):
            return ctx.enter_context(nc.semaphore(name))

        bank = [ctx.enter_context(nc.psum_tensor(f"bank{b}", [128, 512], f32)) for b in range(8)]

        h = sb("h", [128, TILES, HE])
        h_t = sb("h_t", [128, NP])
        support = sb("support", [128, NP])
        big = sb("big", [128, TILES * CHUNK])
        rowbuf = sb("rowbuf", [128, HEADS, NP])
        heads = sb("heads", [128, HEADS, NP])
        work = sb("work", [128, 12 * CHUNK])
        h_tile = sb("h_tile", [128, 2, HE])
        u_tile = sb("u_tile", [128, 2, 2 * UW], bf16)
        u_parts = sb("u_parts", [128, TILES, 2 * UW], bf16)
        ident = sb("ident", [128, 128])
        ones = sb("ones", [128, 128])
        off_diag = sb("off_diag", [128, 128])
        zero_bf = sb("zero_bf", [128, 512], bf16)
        stats = sb("stats", [128, 3, TILES])
        neg_max = sb("neg_max", [128, HEADS, TILES])
        denom = sb("denom", [128, HEADS, TILES])
        inv_denom = sb("inv_denom", [128, HEADS, TILES])
        row_max = sb("row_max", [128, 4])
        sum_parts = sb("sum_parts", [32, 32])
        pick_score = sb("pick_score", [32, SCORES, 128])
        att_vec = sb("att_vec", [128, HEADS, 2])
        w_att = sb("w_att", [128, SCORES])
        flag_f = sb("flag_f", [1, 1])
        flag = sb("flag", [1, 1], i32)

        h_feat = h[:, :, 0:H]
        x_nodes = support[:, :].rearrange("p (t f) -> p t f", f=H)
        squares = heads[:, 0, :].rearrange("p (t f) -> p t f", f=H)
        gat_wt_sb = heads[:, 1, 0:HEADS * H].rearrange("p (i f) -> p i f", i=HEADS)
        NU = TILES * SCORES
        u_all = heads[:, 2, 0:NU].rearrange("p (t i s) -> p t i s", i=HEADS, s=2)
        u_f32 = heads[:, 2, NU:2 * NU].rearrange("p (t i s) -> p t i s", i=HEADS, s=2)
        u_part = heads[:, 2, 2 * NU:3 * NU].bitcast(bf16)[:, 0:NU]\
            .rearrange("p (t i s) -> p t i s", i=HEADS, s=2)
        score_parts = heads[0:32, 0, :]
        scores = heads[0:32, 1, :]
        scaled = heads[0:32, 2, 0:2 * CHUNK].rearrange("p (b c) -> p b c", b=2)
        cols = big[:, :].rearrange("p (t c) -> p t c", t=TILES)
        masks = work[:, 0:2 * CHUNK].bitcast(bf16).rearrange("p (b m c) -> p b m c", b=2, m=2)
        row = [big[:, i * NP:(i + 1) * NP] for i in range(2)]
        masked = [big[:, (2 + i) * NP:(3 + i) * NP] for i in range(2)]
        edge_mask = heads[:, 0, :]
        masked_minus = heads[:, 2, :]
        wexp = work[:, 0:6 * CHUNK].rearrange("p (b i c) -> p b i c", b=2, i=HEADS)
        wadj = work[:, 6 * CHUNK:12 * CHUNK].rearrange("p (b i c) -> p b i c", b=2, i=HEADS)
        spread = work[:, 0:8 * 128].rearrange("p (b t c) -> p b t c", b=2, c=128)

        def carve(buffer, widths):
            views, at = [], 0
            for width in widths:
                views.append(buffer[:, at:at + width])
                at += width
            assert at <= buffer.shape[-1], (at, buffer.shape)
            return views

        (x_feat, xn, w1_f, w2_f, wih_e, whh_e, wih_n, whh_n, pick_f) = carve(
            big[:, :], [NP, NP, E * HID, E * HID, 3 * H, 3 * H, 3 * H, 3 * H, E * 128 // 2])
        w1_sb = w1_f.rearrange("p (e f) -> p e f", e=E)
        w2_sb = w2_f.rearrange("p (e a d) -> p e a d", e=E, a=HALVES)
        pick_bf = pick_f.bitcast(bf16).rearrange("p (e c) -> p e c", e=E)
        gru_w = ((wih_e, whh_e), (wih_n, whh_n))
        (diag_bc, gates_t, gates_half, gw_f, bias_in_f, bias_f, gamma_sb, beta_sb, wr_sb, br_bc, b1_f, b2_sb,
         iota, mean_w, logit_f, top_f, topi_f, topn_f, gap, pair_f, gate_f, gate2_f, gparts_f,
         gbf_f) = carve(rowbuf[:, :, :].rearrange("p i n -> p (i n)"),
                        [NP, NP, NP // 2, HEADS * H, 12, 6, 1, 1, E, E, E * HALVES, H, E, 128,
                         RSPLIT * E, RSPLIT * 8, RSPLIT * 8, RSPLIT * 8, RSPLIT, 2 * RSPLIT, RSPLIT * E,
                         RSPLIT * E, RSPLIT * GROWS, RSPLIT * E // 2])
        gates_bf = gates_half.bitcast(bf16)
        gat_w_sb = gw_f.rearrange("p (i f) -> p i f", i=HEADS)
        bias_in = bias_in_f.rearrange("p (g a) -> p g a", g=4)
        bias = bias_f.rearrange("p (g a) -> p g a", g=2)
        b1_sb = b1_f.rearrange("p (e a) -> p e a", e=E)
        logit, top, top_i, top_n, gate, gate2 = (
            v.rearrange("p (j e) -> p j e", j=RSPLIT) for v in (logit_f, top_f, topi_f, topn_f, gate_f, gate2_f))
        top_i = top_i.bitcast(u32)
        pair = pair_f.rearrange("p (s j) -> p s j", s=2)
        gparts = gparts_f.rearrange("p (j q e) -> p j q e", j=RSPLIT, q=STAT)
        gbf = gbf_f.bitcast(bf16).rearrange("p (j e) -> p j e", j=RSPLIT)
        (t0_, t1_, t2_, t3_, t4_, t5_, t6_, t7_, act_f) = carve(work[:, :], [BLOCK] * 8 + [4 * BLOCK])
        pick32 = act_f[:, 0:E * 128].rearrange("p (e c) -> p e c", e=E)
        act_h = act_f.rearrange("p (b a n) -> p b a n", b=2, a=HALVES)
        prod_h = heads[:, 0, 0:4 * BLOCK].rearrange("p (b a n) -> p b a n", b=2, a=HALVES)
        y_sb = heads[:, 1, 0:2 * BLOCK].rearrange("p (b n) -> p b n", b=2)

        x_in, small_in, gatw_in, consts = sem("x_in"), sem("small_in"), sem("gatw_in"), sem("consts")
        dve_order, pool_order = sem("dve_order"), sem("pool_order")
        h_ready, ht_psum, ht_ready = sem("h_ready"), sem("ht_psum"), sem("ht_ready")
        var_ready, root_ready = sem("var_ready"), sem("root_ready")
        v_psum, v_ready, u_psum, u_ready = sem("v_psum"), sem("v_ready"), sem("u_psum"), sem("u_ready")
        a_in = [sem("a_in0"), sem("a_in1")]
        a_tile, a_mask, a_used, a_sums, a_kept = (sem("a_tile"), sem("a_mask"), sem("a_used"), sem("a_sums"),
                                                  sem("a_kept"))
        s_psum, s_scaled, s_ready = sem("s_psum"), sem("s_scaled"), sem("s_ready")
        b_psum, b_ready, c_psum, c_ready, f_ready = (sem("b_psum"), sem("b_ready"), sem("c_psum"),
                                                     sem("c_ready"), sem("f_ready"))
        PATHS = ("plain", "signed")
        r_in = {v: [sem(f"r_in_{v}{i}") for i in range(2)] for v in PATHS}
        r_free, r_max, r_exp, r_order = ({v: sem(f"{n}_{v}") for v in PATHS}
                                         for n in ("r_free", "r_max", "r_exp", "r_order"))
        q_psum, q_ready = sem("q_psum"), sem("q_ready")
        rows_done = sem("rows_done")
        n_spread, n_psum, n_ready = sem("n_spread"), sem("n_psum"), sem("n_ready")
        g_in = [sem("g_in0"), sem("g_in1")]
        g_y, g_e, g_w, g_mm, g_sums, g_kept = (sem("g_y"), sem("g_e"), sem("g_w"), sem("g_mm"),
                                               sem("g_sums"), sem("g_kept"))
        g_order_pool, g_order_dve = sem("g_order_pool"), sem("g_order_dve")
        t_in, t_ready = sem("t_in"), sem("t_ready")
        by_pe, by_act, by_dve, dense_order = sem("by_pe"), sem("by_act"), sem("by_dve"), sem("dense_order")
        m_hid, m_gate, m_act, m_prod, m_used, m_y, m_out = (
            sem(f"m_{n}") for n in ("hid", "gate", "act", "prod", "used", "y", "out"))
        m_stored = [sem("m_stored0"), sem("m_stored1")]

        dve_waits, pool_waits = sem("dve_waits"), sem("pool_waits")

        NCH = len(CHUNKS)
        parities = range(2)
        block = ctx.enter_context(nc.Block())
        WEIGHT_LOADS = 23

        @block.sync
        def _(sp):
            sp.dma_start(x_nodes, x.rearrange("(t p) f -> p t f", p=128)).then_inc(x_in, 16)
            for dst, src in ((ident[:, :], ident_in), (sum_parts[:, :], sum_parts_in),
                             (pick_score[:, :, :], pick_score_in)):
                sp.dma_start(dst, src).then_inc(small_in, 16)
            sp.dma_start(gat_wt_sb, gat_w_t.rearrange("i p f -> p i f")).then_inc(gatw_in, 16)
            for i in range(HEADS):
                sp.dma_start(att_vec[:, i, :], gat_a[i].rearrange("(s p) o -> p (s o)", p=128),
                             allow_slow_non_contiguous=True).then_inc(gatw_in, 16)

            def load_columns(c, arrived, used):
                c0, w = CHUNKS[c]
                for part, (t0, t1) in enumerate(PARTS):
                    if c > 0:
                        sp.wait_ge(used, TILES * (c - 1) + t1 + FREE)
                    src = adj_cols[t0 * 128:t1 * 128, c0:c0 + w].rearrange("(t p) c -> p t c", p=128)
                    sp.dma_start(cols[:, t0:t1, 0:w], src).then_inc(arrived[part], 16)

            def load_rows(v, tiles, offset=0):
                with sp.Fori(0, tiles // 2) as p:
                    for b in parities:
                        sp.wait_ge(r_free[v], 2 * p + b + 1 + offset)
                        sp.dma_start(row[b], adj_rows[bass.ds((2 * p + b) * 128, 128), :])\
                            .then_inc(r_in[v][b], 16)

            for c in range(NCH):
                load_columns(c, a_in, a_used)
            sp.wait_ge(a_used, TILES * NCH + FREE)
            sp.wait_ge(f_ready, 1)
            signed = sp.value_load(flag[0:1, 0:1])
            with sp.If(signed > 0):
                for head in range(HEADS):
                    load_rows("signed", TILES, TILES * head)
            with sp.Else():
                load_rows("plain", TILES)
            sp.wait_ge(rows_done, 1)
            for c in range(NCH):
                load_columns(c, g_in, g_mm)
            sp.wait_ge(g_mm, TILES * NCH + FREE)
            loads = (
                (x_feat, x_t), (w1_sb, w1.rearrange("e d f -> d e f")),
                (w2_sb, w2.rearrange("e (a p) d -> p e a d", p=128)),
                (wih_e, edge_wih_t), (whh_e, edge_whh_t), (wih_n, node_wih_t), (whh_n, node_whh_t),
                (gat_w_sb, gat_w.rearrange("i p f -> p i f")), (diag_bc, diag.partition_broadcast(128)),
                (bias_in[:, 0, :], edge_bih.rearrange("(a p) -> p a", p=128)),
                (bias_in[:, 1, :], edge_bhh.rearrange("(a p) -> p a", p=128)),
                (bias_in[:, 2, :], node_bih.rearrange("(a p) -> p a", p=128)),
                (bias_in[:, 3, :], node_bhh.rearrange("(a p) -> p a", p=128)),
                (gamma_sb, gamma.rearrange("(p a) -> p a", a=1)), (beta_sb, beta.rearrange("(p a) -> p a", a=1)),
                (wr_sb, wr), (br_bc, br.partition_broadcast(128)), (b1_sb, b1.rearrange("e (a p) -> p e a", p=128)),
                (b2_sb[0:E, :], b2), (b2_sb[E:2 * E, :], b2), (b2_sb[2 * E:3 * E, :], b2),
                (pick32[0:32, :, :], pick_expert_in), (iota, iota_in))
            assert len(loads) == WEIGHT_LOADS
            for dst, src in loads:
                sp.dma_start(dst, src, allow_slow_non_contiguous=True).then_inc(t_in, 16)
            with sp.Fori(0, BLOCKS // 2) as g:
                for b in parities:
                    sp.wait_ge(m_out, 2 * g + b + 1 + FREE)
                    sp.dma_start(out_t[:, bass.ds((2 * g + b) * BLOCK, BLOCK)], y_sb[:, b, :])\
                        .then_inc(m_stored[b], 16)
            for b in parities:
                sp.wait_ge(m_stored[b], 16 * (BLOCKS // 2 + 1))

        @block.gpsimd
        def _(pool):
            order = InOrder(pool, pool_order)
            nc.gpsimd.memset(ones[:, :], 1.0).then_inc(consts, 1)
            nc.gpsimd.memset(zero_bf[:, :], 0.0).then_inc(consts, 1)
            order.done(nc.gpsimd.memset(off_diag[:, :], 1.0))
            nc.gpsimd.affine_select(out=off_diag[:, :], in_=off_diag[:, :], compare_op=ALU.not_equal,
                                    fill=0.0, base=0, pattern=[[-1, 128]], channel_multiplier=1)\
                .then_inc(consts, 1)

            def clear_diagonal(c, part):
                c0, w = CHUNKS[c]
                for t in range(*PARTS[part]):
                    if c0 <= t * 128 < c0 + w:
                        crossed = cols[:, t, t * 128 - c0:t * 128 - c0 + 128]
                        order.done(nc.gpsimd.affine_select(
                            out=crossed, in_=crossed, compare_op=ALU.not_equal, fill=0.0, base=0,
                            pattern=[[-1, 128]], channel_multiplier=1))

            pool.wait_ge(h_ready, 1)
            pool.wait_ge(u_ready, 1)
            for c in range(NCH):
                for part, (t0, t1) in enumerate(PARTS):
                    pool.wait_ge(a_in[part], 16 * (c + 1))
                    clear_diagonal(c, part)
                    with pool.Fori(0, (t1 - t0) // 2) as p:
                        for b in parities:
                            t = 2 * p + (t0 + b)
                            pool.wait_ge(a_used, TILES * c + 1 + t)
                            nc.gpsimd.tensor_copy(u_tile[:, b, :], u_parts[:, bass.ds(t, 1), :].squeeze(1))\
                                .then_inc(a_tile, 1)
                            nc.gpsimd.tensor_copy(h_tile[:, b, 0:H], h[:, bass.ds(t, 1), 0:H].squeeze(1))\
                                .then_inc(a_tile, 1)

            pool.wait_ge(f_ready, 1)
            signed = pool.value_load(flag[0:1, 0:1])

            def weights(v):
                signs = 2 if v == "signed" else 1
                for c, (c0, w) in enumerate(CHUNKS):
                    for part, (t0, t1) in enumerate(PARTS):
                        pool.wait_ge(g_in[part], 16 * (c + 1))
                        clear_diagonal(c, part)
                        at = TILES * c + t0
                        with pool.Fori(0, (t1 - t0) // 2) as p:
                            for b in parities:
                                t = 2 * p + (t0 + b)
                                late = 1 if signs == 1 else 2
                                pool.wait_ge(g_mm, 2 * p + (at + b + late))
                                nc.gpsimd.tensor_copy(h_tile[:, b, :], h[:, bass.ds(t, 1), :].squeeze(1))\
                                    .then_inc(g_order_pool, 1)
                                pool.wait_ge(g_order_pool, 2 * p + (at + b + 1))
                                pool.wait_ge(g_w, 2 * p + (at + b + late))
                                apart(pool, pool_waits)
                                for s in range(signs):
                                    for i in range(HEADS):
                                        col = H + HEADS * s + i
                                        last = nc.gpsimd.tensor_scalar(
                                            wexp[:, s if signs == 2 else b, i, 0:w], rowbuf[:, i, c0:c0 + w],
                                            h_tile[:, b, col:col + 1], 0.0, ALU.add, ALU.min)
                                last.then_inc(g_y, 1)

            pool.wait_ge(n_ready, 2 * HEADS * NCH)
            order_base = order.value
            with pool.If(signed > 0):
                weights("signed")
            order.value = order_base
            with pool.Else():
                weights("plain")

        @block.scalar
        def _(act):
            act.wait_ge(var_ready, 1)
            nc.scalar.activation(stats[:, 1, :], stats[:, 0, :], ACT.Sqrt).then_inc(root_ready, 1)
            for q in range(-(-TILES // 4)):
                n = min(4, TILES - 4 * q) * 128
                act.wait_ge(ht_psum, q + 1)
                nc.scalar.activation(h_t[:, q * 512:q * 512 + n], bank[q % 2][:, 0:n], ACT.Copy)\
                    .then_inc(ht_ready, 1)
            for c, (c0, w) in enumerate(CHUNKS):
                act.wait_ge(a_sums, c + 1)
                nc.scalar.activation(support[:, c0:c0 + w], bank[c % 2][:, 0:w], ACT.Copy).then_inc(a_kept, 1)
                nc.scalar.activation(score_parts[:, c0:c0 + w], bank[2 + c % 2][0:32, 0:w], ACT.Copy)\
                    .then_inc(a_kept, 1)
            for c, (c0, w) in enumerate(CHUNKS):
                act.wait_ge(s_psum, c + 1)
                if c >= 2:
                    act.wait_ge(s_ready, c - 1)
                nc.scalar.activation(scaled[:, c % 2, 0:w], bank[4 + c % 2][0:32, 0:w], ACT.Copy, scale=ALPHA)\
                    .then_inc(s_scaled, 1)
            for q in range(HEADS * NCH):
                i, (c0, w) = q % HEADS, CHUNKS[q // HEADS]
                act.wait_ge(b_psum, q + 1)
                nc.scalar.activation(rowbuf[:, i, c0:c0 + w], bank[6 + q % 2][:, 0:w], ACT.Copy)\
                    .then_inc(b_ready, 1)
            act.wait_ge(f_ready, 1)
            signed = act.value_load(flag[0:1, 0:1])

            def denominators(v):
                nc.scalar.nop().then_inc(r_exp[v], FREE)
                if v == "plain":
                    with act.Fori(0, TILES // 2) as p:
                        for b in parities:
                            for i in range(HEADS):
                                k, n = (HEADS * b + i) % 2, HEADS * b + i
                                act.wait_ge(r_max[v], 2 * HEADS * p + (n + 1))
                                nc.scalar.activation(masked[k], masked[k], ACT.Exp,
                                                     bias=neg_max[:, i, bass.ds(2 * p + b, 1)],
                                                     accum_out=denom[:, i, bass.ds(2 * p + b, 1)])\
                                    .then_inc(r_exp[v], 1)
                    act.wait_ge(r_exp[v], HEADS * TILES + FREE)
                    return
                for head in range(HEADS):
                    for q in range(2 * NCH):
                        c0, w = CHUNKS[q // 2]
                        act.wait_ge(q_psum, 2 * NCH * head + q + 1)
                        nc.scalar.activation(rowbuf[:, q % 2, c0:c0 + w], bank[6 + q % 2][:, 0:w], ACT.Copy)\
                            .then_inc(q_ready, 1)
                    with act.Fori(0, TILES // 2) as p:
                        for b in parities:
                            act.wait_ge(r_max[v], 2 * p + (TILES * head + b + 1))
                            nc.scalar.activation(masked[b], masked[b], ACT.Exp,
                                                 bias=neg_max[:, head, bass.ds(2 * p + b, 1)],
                                                 accum_out=denom[:, head, bass.ds(2 * p + b, 1)])\
                                .then_inc(r_exp[v], 1)
                act.wait_ge(r_exp[v], HEADS * TILES + FREE)

            with act.If(signed > 0):
                denominators("signed")
            with act.Else():
                denominators("plain")
            nc.scalar.nop().then_inc(rows_done, 2)

            for q in range(2 * HEADS * NCH):
                i, (c0, w) = q % (2 * HEADS), CHUNKS[q // (2 * HEADS)]
                target = rowbuf[:, i, c0:c0 + w] if i < HEADS else heads[:, i - HEADS, c0:c0 + w]
                act.wait_ge(n_psum, q + 1)
                nc.scalar.activation(target, bank[q % 2][:, 0:w], ACT.Copy).then_inc(n_ready, 1)

            def exponentials(v):
                for c, (c0, w) in enumerate(CHUNKS):
                    with act.Fori(0, TILES // 2) as p:
                        for b in parities:
                            act.wait_ge(g_y, 2 * p + (TILES * c + b + 1))
                            if v == "plain":
                                place = wexp[:, b, :, 0:w]
                            else:
                                place = work[:, 0:6 * CHUNK].rearrange("p (k c) -> p k c", c=CHUNK)[:, :, 0:w]
                            nc.scalar.activation(place, place, ACT.Exp).then_inc(g_e, 1)

            with act.If(signed > 0):
                exponentials("signed")
            with act.Else():
                exponentials("plain")

            act.wait_ge(t_ready, 4)
            nc.scalar.nop().then_inc(by_act, 1)
            with act.Fori(0, BLOCKS) as g:
                at = Steps(act, "gru", "act", g)
                at.after(by_pe, "pe", "heads")
                at.step(nc.scalar.activation(t0_, bank[0][:, 0:BLOCK], ACT.Copy), by_act, "attention")
                at.after(by_pe, "pe", "edge")
                nc.scalar.activation(t1_, bank[1][:, 0:BLOCK], ACT.Sigmoid, bias=bias[:, 0, 0:1])
                at.step(nc.scalar.activation(t2_, bank[2][:, 0:BLOCK], ACT.Sigmoid, bias=bias[:, 0, 1:2]),
                        by_act, "edge gates")
                at.after(by_pe, "pe", "node")
                nc.scalar.activation(t6_, bank[5][:, 0:BLOCK], ACT.Sigmoid, bias=bias[:, 1, 0:1])
                at.step(nc.scalar.activation(t7_, bank[6][:, 0:BLOCK], ACT.Sigmoid, bias=bias[:, 1, 1:2]),
                        by_act, "node gates")
                at.after(by_dve, "dve", "edge candidate")
                at.step(nc.scalar.activation(t3_, t3_, ACT.Tanh), by_act, "edge tanh")
                at.after(by_dve, "dve", "node candidate")
                at.step(nc.scalar.activation(t1_, t1_, ACT.Tanh), by_act, "node tanh")
                at.end()

            with act.Fori(0, BLOCKS) as g:
                at = Steps(act, "norm", "act", g)
                for again, (centred, squared, value, root) in (
                        ("", (t0_, t1_, t6_, t2_)), (" again", (t4_, t5_, t6_, t7_))):
                    at.after(by_dve, "dve", "centred" + again)
                    at.step(nc.scalar.activation(squared, centred, ACT.Square), by_act, "squares" + again)
                    at.after(by_dve, "dve", "variance" + again)
                    at.step(nc.scalar.activation(root, value, ACT.Sqrt), by_act, "root" + again)
                at.end()

            with act.Fori(0, BLOCKS) as g:
                at = Steps(act, "router", "act", g)
                at.after(by_dve, "dve", "gap")
                nc.scalar.activation(pair[0:RT, 0, :], gap[0:RT, :], ACT.Sigmoid)
                at.step(nc.scalar.activation(pair[0:RT, 1, :], gap[0:RT, :], ACT.Sigmoid, scale=-1.0), by_act,
                        "weights")
                at.after(by_pe, "pe", "gates")
                nc.scalar.activation(gates_t[0:GROWS, bass.ds(g * BLOCK, BLOCK)], bank[6][0:GROWS, 0:BLOCK],
                                     ACT.Copy)
                at.step(nc.scalar.activation(gates_bf[0:GROWS, bass.ds(g * BLOCK, BLOCK)],
                                             bank[6][0:GROWS, 0:BLOCK], ACT.Copy), by_act, "gates")
                at.end()

            with act.Fori(0, BLOCKS) as g:
                for e in range(E):
                    b = e % 2
                    act.wait_ge(m_hid, g * E + (e + 1))
                    act.wait_ge(m_prod, g * E + (e + 1))
                    for a in range(HALVES):
                        last = nc.scalar.activation(act_h[:, b, a, :], bank[2 * b + a][:, 0:BLOCK], ACT.Gelu,
                                                    bias=b1_sb[:, e, a:a + 1])
                    last.then_inc(m_act, 1)

        @block.vector
        def _(dve):
            order = InOrder(dve, dve_order)

            def inverse_root(root, value, spare, settled):
                settled(nc.vector.reciprocal(root, root))
                settled(nc.vector.tensor_tensor(spare, root, root, ALU.mult))
                settled(nc.vector.tensor_tensor(spare, spare, value, ALU.mult))
                settled(nc.vector.tensor_scalar(spare, spare, -0.5, 1.5, ALU.mult, ALU.add))
                settled(nc.vector.tensor_tensor(root, root, spare, ALU.mult))

            dve.wait_ge(x_in, 16)
            wide = [128, TILES, H]
            total, inv = stats[:, 0, :], stats[:, 1, :]
            order.done(nc.vector.tensor_reduce(total, x_nodes, AX.X, ALU.add))
            order.done(nc.vector.tensor_scalar(total, total, 1.0 / H, None, ALU.mult))
            order.done(nc.vector.tensor_tensor(x_nodes, x_nodes, total.unsqueeze(2).broadcast_to(wide),
                                               ALU.subtract))
            order.done(nc.vector.tensor_tensor(squares, x_nodes, x_nodes, ALU.mult))
            order.done(nc.vector.tensor_reduce(inv, squares, AX.X, ALU.add))
            order.done(nc.vector.tensor_scalar(inv, inv, 1.0 / H, EPS, ALU.mult, ALU.add))
            nc.vector.tensor_scalar(total, inv, 1.0, None, ALU.mult).then_inc(var_ready, 1)
            dve.wait_ge(root_ready, 1)
            inverse_root(inv, total, stats[:, 2, :], lambda ins: order.done(ins))
            nc.vector.tensor_tensor(h_feat, x_nodes, inv.unsqueeze(2).broadcast_to(wide), ALU.mult)\
                .then_inc(h_ready, 2)
            dve.wait_ge(v_psum, 1)
            nc.vector.tensor_copy(w_att[:, :], bank[2][:, 0:SCORES]).then_inc(v_ready, 1)
            order.done(nc.vector.memset(u_parts[:, :, :], 0.0))
            order.done(nc.vector.memset(u_parts[:, :, UW:UW + 1], 1.0))
            dve.wait_ge(u_psum, 1)
            order.done(nc.vector.tensor_copy(heads[:, 2, 0:NU], bank[3][:, 0:NU]))
            for q in range(STAT):
                order.done(nc.vector.tensor_copy(u_part, u_all))
                for s in range(2):
                    for m in range(2):
                        at = UW * m + 1 + SCORES * q + HEADS * s
                        nc.vector.tensor_copy(u_parts[:, :, at:at + HEADS], u_part[:, :, :, s ^ m])
                order.done(nc.vector.tensor_copy(u_f32, u_part))
                if q < STAT - 1:
                    order.done(nc.vector.tensor_tensor(u_all, u_all, u_f32, ALU.subtract))
            nc.vector.nop().then_inc(u_ready, 1)

            for c, (c0, w) in enumerate(CHUNKS):
                with dve.Fori(0, TILES // 2) as p:
                    for b in parities:
                        n = TILES * c + b
                        dve.wait_ge(a_tile, 4 * p + 2 * (n + 1))
                        dve.wait_ge(a_used, 2 * p + (n + 1))
                        tile = cols[:, bass.ds(2 * p + b, 1), 0:w].squeeze(1)
                        nc.vector.tensor_scalar(masks[:, b, 0, 0:w], tile, 0.0, None, ALU.is_gt)
                        nc.vector.tensor_scalar(masks[:, b, 1, 0:w], tile, 0.0, None, ALU.is_lt)\
                            .then_inc(a_mask, 1)
            for c, (c0, w) in enumerate(CHUNKS):
                dve.wait_ge(s_scaled, c + 1)
                nc.vector.tensor_tensor(scores[:, c0:c0 + w], scaled[:, c % 2, 0:w], bank[4 + c % 2][0:32, 0:w],
                                        ALU.max).then_inc(s_ready, 1)
            order.done(nc.vector.tensor_reduce(flag_f[:, :], score_parts[0:1, :], AX.X, ALU.max))
            nc.vector.tensor_copy(flag[:, :], flag_f[:, :]).then_inc(f_ready, 1)
            dve.wait_ge(f_ready, 1)
            signed = dve.value_load(flag[0:1, 0:1])
            dve.wait_ge(c_psum, 1)
            nc.vector.tensor_copy(h[:, :, H:HE], bank[3][:, 0:NU].rearrange("p (t r) -> p t r", r=SCORES))\
                .then_inc(c_ready, 1)

            def maxima(v):
                step = r_order[v]
                nc.vector.nop().then_inc(r_free[v], FREE)
                if v == "plain":
                    EACH = 2 + HEADS
                    dve.wait_ge(b_ready, HEADS * NCH)
                    with dve.Fori(0, TILES // 2) as p:
                        for b in parities:
                            at = EACH * b
                            dve.wait_ge(r_in[v][b], 16 * p + 16)
                            crossed = row[b][:, bass.ds((2 * p + b) * 128, 128)]
                            nc.vector.tensor_tensor(crossed, crossed, off_diag[:, :], ALU.mult).then_inc(step, 1)
                            dve.wait_ge(step, 2 * EACH * p + (at + 1))
                            nc.vector.tensor_scalar(row[b], row[b], 0.0, NEG_INF, ALU.is_le, ALU.mult)\
                                .then_inc(step, 1)
                            dve.wait_ge(step, 2 * EACH * p + (at + 2))
                            for i in range(HEADS):
                                n = HEADS * b + i
                                dve.wait_ge(r_exp[v], 2 * HEADS * p + (n + 1))
                                apart(dve, dve_waits)
                                nc.vector.tensor_tensor_reduce(
                                    out=masked[n % 2], in0=row[b], in1=rowbuf[:, i, :], scale=1.0,
                                    scalar=LOWEST, op0=ALU.add, op1=ALU.max,
                                    accum_out=row_max[:, i:i + 1]).then_inc(step, 1)
                                dve.wait_ge(step, 2 * EACH * p + (at + 3 + i))
                                nc.vector.tensor_scalar(neg_max[:, i, bass.ds(2 * p + b, 1)],
                                                        row_max[:, i:i + 1], -1.0, None, ALU.mult)\
                                    .then_inc(r_max[v], 1)
                            nc.vector.nop().then_inc(r_free[v], 1)
                    return
                EACH = 7
                for head in range(HEADS):
                    dve.wait_ge(q_ready, 2 * NCH * (head + 1))
                    with dve.Fori(0, TILES // 2) as p:
                        for b in parities:
                            at = EACH * (TILES * head + b)
                            dve.wait_ge(r_in[v][b], 16 * p + 16 * (TILES // 2 * head + 1))
                            crossed = row[b][:, bass.ds((2 * p + b) * 128, 128)]
                            nc.vector.tensor_tensor(crossed, crossed, off_diag[:, :], ALU.mult).then_inc(step, 1)
                            dve.wait_ge(step, 2 * EACH * p + (at + 1))
                            nc.vector.tensor_scalar(edge_mask, row[b], 0.0, NEG_INF, ALU.is_le, ALU.mult)\
                                .then_inc(step, 1)
                            dve.wait_ge(step, 2 * EACH * p + (at + 2))
                            dve.wait_ge(r_exp[v], 2 * p + (TILES * head + b + 1))
                            apart(dve, dve_waits)
                            nc.vector.tensor_tensor_reduce(
                                out=masked[b], in0=edge_mask, in1=rowbuf[:, 0, :], scale=1.0, scalar=LOWEST,
                                op0=ALU.add, op1=ALU.max, accum_out=row_max[:, 0:1]).then_inc(step, 1)
                            dve.wait_ge(step, 2 * EACH * p + (at + 3))
                            nc.vector.tensor_scalar(edge_mask, row[b], 0.0, NEG_INF, ALU.is_ge, ALU.mult)\
                                .then_inc(step, 1)
                            dve.wait_ge(step, 2 * EACH * p + (at + 4))
                            apart(dve, dve_waits)
                            nc.vector.tensor_tensor_reduce(
                                out=masked_minus, in0=edge_mask, in1=rowbuf[:, 1, :], scale=1.0, scalar=LOWEST,
                                op0=ALU.add, op1=ALU.max, accum_out=row_max[:, 1:2]).then_inc(step, 1)
                            dve.wait_ge(step, 2 * EACH * p + (at + 5))
                            nc.vector.tensor_tensor(masked[b], masked[b], masked_minus, ALU.max)\
                                .then_inc(step, 1)
                            nc.vector.tensor_tensor(row_max[:, 2:3], row_max[:, 0:1], row_max[:, 1:2], ALU.max)\
                                .then_inc(step, 1)
                            dve.wait_ge(step, 2 * EACH * p + (at + 7))
                            nc.vector.tensor_scalar(neg_max[:, head, bass.ds(2 * p + b, 1)],
                                                    row_max[:, 2:3], -1.0, None, ALU.mult).then_inc(r_max[v], 1)
                            nc.vector.nop().then_inc(r_free[v], 1)

            with dve.If(signed > 0):
                maxima("signed")
                dve.wait_ge(r_max["signed"], HEADS * TILES)
            with dve.Else():
                maxima("plain")
                dve.wait_ge(r_max["plain"], HEADS * TILES)

            dve.wait_ge(rows_done, 1)
            order.done(nc.vector.tensor_scalar(inv_denom[:, :, :], denom[:, :, :], float(HEADS), None, ALU.mult))
            order.done(nc.vector.reciprocal(inv_denom[:, :, :], inv_denom[:, :, :]))
            for q in range(2 * HEADS * NCH):
                i, (c0, w) = q % (2 * HEADS), CHUNKS[q // (2 * HEADS)]
                source = neg_max if i < HEADS else inv_denom
                t, n = c0 // 128, w // 128
                if q >= 2:
                    dve.wait_ge(n_psum, q - 1)
                nc.vector.tensor_tensor(
                    spread[:, q % 2, 0:n, :], ident[:, :].unsqueeze(1).broadcast_to([128, n, 128]),
                    source[:, i % HEADS, t:t + n].unsqueeze(2).broadcast_to([128, n, 128]), ALU.mult)\
                    .then_inc(n_spread, 1)

            def products(v):
                nc.vector.nop().then_inc(g_w, FREE)
                for c, (c0, w) in enumerate(CHUNKS):
                    with dve.Fori(0, TILES // 2) as p:
                        for b in parities:
                            n = TILES * c + b
                            tile = cols[:, bass.ds(2 * p + b, 1), 0:w].broadcast_to([128, HEADS, w])
                            dve.wait_ge(g_e, 2 * p + (n + 1))
                            if v == "plain":
                                dve.wait_ge(g_mm, 2 * p + (n + 1))
                                nc.vector.tensor_tensor(wadj[:, b, :, 0:w], wexp[:, b, :, 0:w], tile, ALU.mult)\
                                    .then_inc(g_w, 1)
                                continue
                            dve.wait_ge(g_mm, 2 * p + (n + 2))
                            for s, part in enumerate((ALU.max, ALU.min)):
                                for i in range(HEADS):
                                    last = nc.vector.scalar_tensor_tensor(
                                        out=wadj[:, s, i, 0:w], in0=cols[:, bass.ds(2 * p + b, 1), 0:w].squeeze(1),
                                        scalar=0.0, in1=wexp[:, s, i, 0:w], op0=part, op1=ALU.mult)
                            last.then_inc(g_order_dve, 1)
                            dve.wait_ge(g_order_dve, 2 * p + (n + 1))
                            nc.vector.tensor_tensor(wadj[:, 0, :, 0:w], wadj[:, 0, :, 0:w],
                                                    wadj[:, 1, :, 0:w], ALU.add).then_inc(g_w, 1)
                    dve.wait_ge(g_sums, c + 1)
                    for i in range(HEADS):
                        nc.vector.tensor_tensor(heads[:, i, c0:c0 + w], heads[:, i, c0:c0 + w],
                                                bank[3 * (c % 2) + i][:, 0:w], ALU.mult).then_inc(g_kept, 1)

            dve.wait_ge(n_ready, 2 * HEADS * NCH)
            with dve.If(signed > 0):
                products("signed")
            with dve.Else():
                products("plain")

            dve.wait_ge(t_in, 16 * WEIGHT_LOADS)
            nc.vector.tensor_copy(pick_bf[0:32, :, :], pick32[0:32, :, :]).then_inc(t_ready, 1)
            nc.vector.memset(mean_w, 1.0 / H).then_inc(t_ready, 1)
            for c in range(2):
                nc.vector.tensor_tensor(bias[:, c, :], bias_in[:, 2 * c, :], bias_in[:, 2 * c + 1, :], ALU.add)\
                    .then_inc(t_ready, 1)
            nc.vector.nop().then_inc(by_dve, 1)
            nc.vector.nop().then_inc(dense_order, 1)
            with dve.Fori(0, BLOCKS) as g:
                here = bass.ds(g * BLOCK, BLOCK)
                at = Steps(dve, "gru", "dve", g, dense_order)

                def candidate(gru, reset, out, bank_in, bank_hn, name):
                    at.after(by_act, "act", name + " gates")
                    at.settled(nc.vector.scalar_tensor_tensor(
                        out=out, in0=bank_hn[:, 0:BLOCK], scalar=bias_in[:, 2 * gru + 1, 2:3], in1=reset,
                        op0=ALU.add, op1=ALU.mult))
                    at.step(nc.vector.scalar_tensor_tensor(
                        out=out, in0=bank_in[:, 0:BLOCK], scalar=bias_in[:, 2 * gru, 2:3], in1=out,
                        op0=ALU.add, op1=ALU.add), by_dve, name + " candidate")

                def mix(out, update, cand, name):
                    at.after(by_act, "act", name + " tanh")
                    at.settled(nc.vector.tensor_tensor(out, h_t[:, here], cand, ALU.subtract))
                    at.settled(nc.vector.tensor_tensor(out, out, update, ALU.mult))
                    at.settled(nc.vector.tensor_tensor(out, out, cand, ALU.add))

                candidate(0, t1_, t3_, bank[3], bank[4], "edge")
                candidate(1, t6_, t1_, bank[7], bank[0], "node")
                mix(t4_, t2_, t3_, "edge")
                mix(t5_, t7_, t1_, "node")
                at.settled(nc.vector.tensor_tensor(t4_, t4_, t5_, ALU.add))
                at.settled(nc.vector.tensor_tensor(t4_, t4_, diag_bc[:, here], ALU.mult))
                at.step(nc.vector.tensor_tensor(x_feat[:, here], x_feat[:, here], t4_, ALU.add), by_dve, "x")
                at.end()

            with dve.Fori(0, BLOCKS) as g:
                here = bass.ds(g * BLOCK, BLOCK)
                at = Steps(dve, "norm", "dve", g, dense_order)
                for again, (source, centred, value, root, spare, mean_bank, var_bank, out) in (
                        ("", (x_feat[:, here], t0_, t6_, t2_, t3_, bank[1], bank[2], t3_)),
                        (" again", (t3_, t4_, t6_, t7_, t5_, bank[3], bank[4], t4_))):
                    at.after(by_pe, "pe", "mean" + again)
                    at.step(nc.vector.tensor_tensor(centred, source, mean_bank[:, 0:BLOCK], ALU.subtract),
                            by_dve, "centred" + again)
                    at.after(by_pe, "pe", "variance" + again)
                    at.step(nc.vector.tensor_scalar(value, var_bank[:, 0:BLOCK], EPS, None, ALU.add), by_dve,
                            "variance" + again)
                    at.after(by_act, "act", "root" + again)
                    at.after(by_dve, "dve", "variance" + again)
                    inverse_root(root, value, spare, at.settled)
                    result = nc.vector.tensor_tensor(out, centred, root, ALU.mult)
                    if again:
                        at.settled(result)
                    else:
                        at.step(result, by_dve, "normalised")
                        at.after(by_dve, "dve", "normalised")
                at.step(nc.vector.tensor_scalar(xn[:, here], t4_, gamma_sb, beta_sb, ALU.mult, ALU.add), by_dve,
                        "experts' input")
                at.end()

            with dve.Fori(0, BLOCKS) as g:
                here = bass.ds(g * BLOCK, BLOCK)
                at = Steps(dve, "router", "dve", g, dense_order)
                at.step(nc.vector.tensor_copy(t0_, xn[:, here]), by_dve, "block")
                at.after(by_pe, "pe", "logits")
                at.settled(nc.vector.tensor_tensor(
                    logit[0:RT], bank[5][0:RT, 0:RSPLIT * E].rearrange("p (j e) -> p j e", j=RSPLIT),
                    br_bc[0:RT, :].unsqueeze(1).broadcast_to([RT, RSPLIT, E]), ALU.add))
                apart(dve, dve_waits)
                for j in range(RSPLIT):
                    last = nc.vector.max(top[0:RT, j, :], logit[0:RT, j, :])
                at.settled(last)
                apart(dve, dve_waits)
                for j in range(RSPLIT):
                    last = nc.vector.max_index(top_i[0:RT, j, :], top[0:RT, j, :], logit[0:RT, j, :])
                at.settled(last)
                at.settled(nc.vector.tensor_copy(top_n[0:RT], top_i[0:RT]))
                at.step(nc.vector.tensor_tensor(gap[0:RT, :], top[0:RT, :, 0], top[0:RT, :, 1], ALU.subtract),
                        by_dve, "gap")
                at.after(by_act, "act", "weights")
                for s, one in enumerate((gate, gate2)):
                    for j in range(RSPLIT):
                        last = nc.vector.tensor_scalar(one[0:RT, j, :], iota[0:RT, :], top_n[0:RT, j, s:s + 1],
                                                       pair[0:RT, s, j:j + 1], ALU.is_equal, ALU.mult)
                at.settled(last)
                at.settled(nc.vector.tensor_tensor(gate[0:RT], gate[0:RT], gate2[0:RT], ALU.add))
                for q in range(STAT):
                    at.settled(nc.vector.tensor_copy(gbf[0:RT], gate[0:RT]))
                    if q < STAT - 1:
                        at.settled(nc.vector.tensor_copy(gparts[0:RT, :, q, :], gbf[0:RT]))
                        at.settled(nc.vector.tensor_tensor(gate[0:RT], gate[0:RT], gparts[0:RT, :, q, :],
                                                           ALU.subtract))
                at.step(nc.vector.tensor_copy(gparts[0:RT, :, STAT - 1, :], gbf[0:RT]), by_dve, "gates")
                at.end()

            nc.vector.nop().then_inc(m_prod, FREE)
            nc.vector.nop().then_inc(m_out, FREE)
            for b in parities:
                nc.vector.nop().then_inc(m_stored[b], 16)
            with dve.Fori(0, BLOCKS // 2) as gg:
                for gb in parities:
                    for e in range(E):
                        b, n = e % 2, E * gb + e
                        dve.wait_ge(m_act, 2 * E * gg + (n + 1))
                        dve.wait_ge(m_gate, 2 * E * gg + (n + 1))
                        dve.wait_ge(m_used, 2 * E * gg + (n + 1))
                        nc.vector.tensor_tensor(
                            prod_h[:, b, :, :], act_h[:, b, :, :],
                            bank[4 + b][:, 0:BLOCK].unsqueeze(1).broadcast_to([128, HALVES, BLOCK]), ALU.mult)\
                            .then_inc(m_prod, 1)
                    dve.wait_ge(m_y, 2 * gg + (gb + 1))
                    dve.wait_ge(m_stored[gb], 16 * gg + 16)
                    nc.vector.tensor_tensor(y_sb[:, gb, :], bank[6 + gb][:, 0:BLOCK],
                                            x_feat[:, bass.ds((2 * gg + gb) * BLOCK, BLOCK)], ALU.add)\
                        .then_inc(m_out, 1)

        @block.tensor
        def _(pe):
            pe.wait_ge(small_in, 48)
            pe.wait_ge(consts, 3)
            pe.wait_ge(h_ready, 2)
            for t in range(TILES):
                q = t // 4
                if t % 4 == 0 and q >= 2:
                    pe.wait_ge(ht_ready, q - 1)
                last = nc.tensor.transpose(bank[q % 2][:, t % 4 * 128:(t % 4 + 1) * 128], h[:, t, 0:H],
                                           ident[:, :])
                if t % 4 == 3 or t == TILES - 1:
                    last.then_inc(ht_psum, 1)
            pe.wait_ge(gatw_in, 16 * (1 + HEADS))
            for i in range(HEADS):
                last = nc.tensor.matmul(bank[2][:, 2 * i:2 * i + 2], gat_wt_sb[:, i, :], att_vec[:, i, :],
                                        start=True, stop=True)
            last.then_inc(v_psum, 1)
            pe.wait_ge(v_ready, 1)
            pe.wait_ge(ht_ready, -(-TILES // 4))
            for t in range(TILES):
                last = nc.tensor.matmul(bank[3][:, t * SCORES:(t + 1) * SCORES], h_t[:, t * 128:(t + 1) * 128],
                                        w_att[:, :], start=True, stop=True)
            last.then_inc(u_psum, 1)

            def clear(out, free=None):
                m = out.shape[0]
                return nc.tensor.matmul(out, zero_bf[:, 0:m], zero_bf[:, 0:out.shape[1]], start=True, stop=False)

            def close(out):
                m = out.shape[0]
                return nc.tensor.matmul(out, zero_bf[:, 0:m], zero_bf[:, 0:out.shape[1]], start=False, stop=True)

            pe.wait_ge(u_ready, 1)
            for c, (c0, w) in enumerate(CHUNKS):
                if c >= 2:
                    pe.wait_ge(a_kept, 2 * (c - 1))
                sums, parts = bank[c % 2][:, 0:w], bank[2 + c % 2][0:32, 0:w]
                clear(sums)
                last = clear(parts)
                if c == 0:
                    last.then_inc(a_used, FREE)
                with pe.Fori(0, TILES // 2) as p:
                    for b in parities:
                        n = TILES * c + b
                        pe.wait_ge(a_tile, 4 * p + 2 * (n + 1))
                        nc.tensor.matmul(sums, h_tile[:, b, 0:H],
                                         cols[:, bass.ds(2 * p + b, 1), 0:w].squeeze(1), start=False, stop=False)
                        pe.wait_ge(a_mask, 2 * p + (n + 1))
                        nc.tensor.matmul(parts, u_tile[:, b, 0:UW], masks[:, b, 0, 0:w], start=False, stop=False)
                        nc.tensor.matmul(parts, u_tile[:, b, UW:2 * UW], masks[:, b, 1, 0:w], start=False,
                                         stop=False).then_inc(a_used, 1)
                close(sums)
                close(parts).then_inc(a_sums, 1)
            pe.wait_ge(a_kept, 2 * NCH)
            for c, (c0, w) in enumerate(CHUNKS):
                if c >= 2:
                    pe.wait_ge(s_ready, c - 1)
                nc.tensor.matmul(bank[4 + c % 2][0:32, 0:w], sum_parts[:, :], score_parts[:, c0:c0 + w],
                                 start=True, stop=True).then_inc(s_psum, 1)
            pe.wait_ge(s_ready, NCH)
            for q in range(HEADS * NCH):
                i, (c0, w) = q % HEADS, CHUNKS[q // HEADS]
                if q >= 2:
                    pe.wait_ge(b_ready, q - 1)
                nc.tensor.matmul(bank[6 + q % 2][:, 0:w], pick_score[:, i, :], scores[:, c0:c0 + w],
                                 start=True, stop=True).then_inc(b_psum, 1)
            for t in range(TILES):
                last = nc.tensor.matmul(bank[3][:, t * SCORES:(t + 1) * SCORES], scores[:, t * 128:(t + 1) * 128],
                                        ident[0:32, 0:SCORES], start=True, stop=True)
            last.then_inc(c_psum, 1)
            pe.wait_ge(f_ready, 1)
            signed = pe.value_load(flag[0:1, 0:1])
            with pe.If(signed > 0):
                pe.wait_ge(b_ready, HEADS * NCH)
                for head in range(HEADS):
                    if head > 0:
                        pe.wait_ge(r_max["signed"], TILES * head)
                    for q in range(2 * NCH):
                        c0, w = CHUNKS[q // 2]
                        if head > 0 or q >= 2:
                            pe.wait_ge(q_ready, 2 * NCH * head + q - 1)
                        nc.tensor.matmul(bank[6 + q % 2][:, 0:w], pick_score[:, HEADS * (q % 2) + head, :],
                                         scores[:, c0:c0 + w], start=True, stop=True).then_inc(q_psum, 1)
            for q in range(2 * HEADS * NCH):
                w = CHUNKS[q // (2 * HEADS)][1]
                pe.wait_ge(n_spread, q + 1)
                if q >= 2:
                    pe.wait_ge(n_ready, q - 1)
                nc.tensor.matmul(bank[q % 2][:, 0:w], ones[:, :],
                                 spread[:, q % 2, 0:w // 128, :].rearrange("p t c -> p (t c)"),
                                 start=True, stop=True).then_inc(n_psum, 1)
            pe.wait_ge(n_ready, 2 * HEADS * NCH)

            def sum_heads(v):
                for c, (c0, w) in enumerate(CHUNKS):
                    if c >= 2:
                        pe.wait_ge(g_kept, HEADS * (c - 1))
                    sums = [bank[3 * (c % 2) + i][:, 0:w] for i in range(HEADS)]
                    for out in sums:
                        last = clear(out)
                    if c == 0:
                        last.then_inc(g_mm, FREE)
                    with pe.Fori(0, TILES // 2) as p:
                        for b in parities:
                            pe.wait_ge(g_w, 2 * p + (TILES * c + b + 1 + FREE))
                            for i in range(HEADS):
                                last = nc.tensor.matmul(sums[i], h_tile[:, b, 0:H],
                                                        wadj[:, b if v == "plain" else 0, i, 0:w],
                                                        start=False, stop=False)
                            last.then_inc(g_mm, 1)
                    for out in sums:
                        last = close(out)
                    last.then_inc(g_sums, 1)

            with pe.If(signed > 0):
                sum_heads("signed")
            with pe.Else():
                sum_heads("plain")

            nc.tensor.nop().then_inc(by_pe, 1)
            pe.wait_ge(g_kept, HEADS * NCH)
            pe.wait_ge(t_ready, 4)
            with pe.Fori(0, BLOCKS) as g:
                here = bass.ds(g * BLOCK, BLOCK)
                at = Steps(pe, "gru", "pe", g)

                def gates(gru, inp, banks):
                    wih, whh = gru_w[gru]
                    for a in range(2):
                        nc.tensor.matmul(banks[a][:, 0:BLOCK], wih[:, a * H:(a + 1) * H], inp, start=True,
                                         stop=False)
                        nc.tensor.matmul(banks[a][:, 0:BLOCK], whh[:, a * H:(a + 1) * H], h_t[:, here],
                                         start=False, stop=True)
                    nc.tensor.matmul(banks[2][:, 0:BLOCK], wih[:, 2 * H:3 * H], inp, start=True, stop=True)
                    return nc.tensor.matmul(banks[3][:, 0:BLOCK], whh[:, 2 * H:3 * H], h_t[:, here], start=True,
                                            stop=True)

                at.before(by_act, "act")
                at.before(by_dve, "dve")
                for i in range(HEADS):
                    last = nc.tensor.matmul(bank[0][:, 0:BLOCK], gat_w_sb[:, i, :], heads[:, i, here],
                                            start=(i == 0), stop=(i == HEADS - 1))
                at.step(last, by_pe, "heads")
                at.step(gates(0, support[:, here], bank[1:5]), by_pe, "edge")
                at.after(by_act, "act", "attention")
                at.step(gates(1, t0_, [bank[5], bank[6], bank[7], bank[0]]), by_pe, "node")
                at.end()

            with pe.Fori(0, BLOCKS) as g:
                here = bass.ds(g * BLOCK, BLOCK)
                at = Steps(pe, "norm", "pe", g)
                at.before(by_dve, "dve")
                at.step(nc.tensor.matmul(bank[1][:, 0:BLOCK], mean_w, x_feat[:, here], start=True, stop=True),
                        by_pe, "mean")
                at.after(by_act, "act", "squares")
                at.step(nc.tensor.matmul(bank[2][:, 0:BLOCK], mean_w, t1_, start=True, stop=True), by_pe,
                        "variance")
                at.after(by_dve, "dve", "normalised")
                at.step(nc.tensor.matmul(bank[3][:, 0:BLOCK], mean_w, t3_, start=True, stop=True), by_pe,
                        "mean again")
                at.after(by_act, "act", "squares again")
                at.step(nc.tensor.matmul(bank[4][:, 0:BLOCK], mean_w, t5_, start=True, stop=True), by_pe,
                        "variance again")
                at.end()

            with pe.Fori(0, BLOCKS) as g:
                at = Steps(pe, "router", "pe", g)
                at.before(by_act, "act")
                at.after(by_dve, "dve", "block")
                for j in range(RSPLIT):
                    last = nc.tensor.matmul(bank[5][0:RT, j * E:(j + 1) * E], t0_[:, j * RT:(j + 1) * RT], wr_sb,
                                            start=True, stop=True)
                at.step(last, by_pe, "logits")
                at.after(by_dve, "dve", "gates")
                for j in range(RSPLIT):
                    last = nc.tensor.transpose(bank[6][0:GROWS, j * RT:(j + 1) * RT],
                                               gparts[0:RT, j].rearrange("p q e -> p (q e)"), ident[0:RT, 0:RT])
                at.step(last, by_pe, "gates")
                at.end()

            pe.wait_ge(by_act, 1 + BLOCKS * sum(len(layer["act"]) for layer in LAYERS.values()))
            nc.tensor.nop().then_inc(m_used, FREE)
            with pe.Fori(0, BLOCKS // 2) as gg:
                for gb in parities:
                    here = bass.ds((2 * gg + gb) * BLOCK, BLOCK)
                    y = bank[6 + gb][:, 0:BLOCK]
                    pe.wait_ge(m_out, 2 * gg + (gb + 1))
                    nc.tensor.matmul(y, b2_sb[0:GROWS, :], gates_t[0:GROWS, here], start=True, stop=False)

                    def down(e):
                        pe.wait_ge(m_prod, 2 * E * gg + (E * gb + e + 1 + FREE))
                        for a in range(HALVES):
                            last = nc.tensor.matmul(y, w2_sb[:, e, a, :], prod_h[:, e % 2, a, :], start=False,
                                                    stop=False)
                        last.then_inc(m_used, 1)
                        return last

                    for e in range(E):
                        b, n = e % 2, E * gb + e
                        pe.wait_ge(m_prod, 2 * E * gg + (n + 1))
                        for a in range(HALVES):
                            last = nc.tensor.matmul(bank[2 * b + a][:, 0:BLOCK],
                                                    w1_sb[:, e, a * 128:(a + 1) * 128], xn[:, here],
                                                    start=True, stop=True)
                        last.then_inc(m_hid, 1)
                        nc.tensor.matmul(bank[4 + b][:, 0:BLOCK], pick_bf[0:GROWS, e, :], gates_bf[0:GROWS, here],
                                         start=True, stop=True).then_inc(m_gate, 1)
                        if e >= 1:
                            down(e - 1)
                    down(E - 1)
                    close(y).then_inc(m_y, 1)


def kernel(**inputs):
    import concourse.bacc as bacc
    from concourse.bass_utils import run_bass_kernel_spmd

    def arr(name):
        return np.ascontiguousarray(inputs[name])

    x, adj = arr("x"), arr("adj")
    x_pad = np.zeros((NP, H), x.dtype)
    x_pad[:N] = x
    rows = np.zeros((NP, NP), adj.dtype)
    rows[:N, :N] = adj
    ident, sum_parts, pick_score, pick_expert, iota = host_constants()
    data = [("x", x_pad), ("x_t", x_pad.T), ("adj_rows", rows), ("adj_cols", rows.T), ("diag", rows.diagonal()),
            ("ident", ident), ("sum_parts", sum_parts), ("pick_score", pick_score),
            ("pick_expert", pick_expert), ("iota", iota), ("gat_w", arr("L0_gnn_gat_W")),
            ("gat_w_t", arr("L0_gnn_gat_W").transpose(0, 2, 1)), ("gat_a", arr("L0_gnn_gat_a")),
            ("edge_wih_t", arr("L0_gnn_edge_Wih").T), ("edge_whh_t", arr("L0_gnn_edge_Whh").T),
            ("edge_bih", arr("L0_gnn_edge_bih")), ("edge_bhh", arr("L0_gnn_edge_bhh")),
            ("node_wih_t", arr("L0_gnn_node_Wih").T), ("node_whh_t", arr("L0_gnn_node_Whh").T),
            ("node_bih", arr("L0_gnn_node_bih")), ("node_bhh", arr("L0_gnn_node_bhh")),
            ("gamma", arr("L0_ffn_gamma")), ("beta", arr("L0_ffn_beta")), ("wr", arr("L0_ffn_Wr")),
            ("br", arr("L0_ffn_br")), ("w1", arr("L0_ffn_W1")), ("b1", arr("L0_ffn_b1")),
            ("w2", arr("L0_ffn_W2")), ("b2", arr("L0_ffn_b2"))]
    nc = bacc.Bacc("TRN2", target_bir_lowering=False, num_devices=1)
    arrays, args = {}, []
    for name, a in data:
        a = np.ascontiguousarray(a)
        arrays[f"{name}_dram"] = a
        args.append(nc.dram_tensor(f"{name}_dram", a.shape, mybir.dt.from_np(a.dtype),
                                   kind="ExternalInput").ap())
    out = nc.dram_tensor("out_dram", (H, NP), mybir.dt.float32, kind="ExternalOutput").ap()
    graph_layer_kernel(nc, *args, out)
    result = run_bass_kernel_spmd(nc, [arrays], core_ids=[0])
    return np.ascontiguousarray(result.results[0]["out_dram"][:, :N].T)
```

```python
from contextlib import ExitStack

import concourse.bass as bass
from concourse import mybir
import numpy as np

N = 3327
H = 128
HEADS = 3
TILES = -(-N // 128)
NP = TILES * 128
CHUNK = 512
CHUNKS = [(c, min(CHUNK, NP - c)) for c in range(0, NP, CHUNK)]
PARTS = ((0, 12), (12, TILES))
ALPHA = 0.2
NEG_INF = -9e15
LOWEST = -3e38
EPS = 1e-5
E = 8
HID = 256
HALVES = HID // 128
BLOCK = 416
BLOCKS = NP // BLOCK
SCORES = 2 * HEADS
STAT = 3
UW = 32
HE = H + SCORES + HEADS
GROWS = STAT * E
FREE = 2


def host_constants():
    ident = np.eye(128, dtype=np.float32)
    sum_parts = np.zeros((32, 32), np.float32)
    for q in range(STAT):
        for r in range(SCORES):
            sum_parts[1 + SCORES * q + r, r] = 1.0
    pick_score = np.zeros((32, SCORES, 128), np.float32)
    for r in range(SCORES):
        pick_score[r, r, :] = 1.0
    pick_expert = np.zeros((32, E, 128), np.float32)
    for q in range(STAT):
        for e in range(E):
            pick_expert[E * q + e, e, :] = 1.0
    iota = np.tile(np.arange(-E, 0, dtype=np.float32), (128, 1))
    return ident, sum_parts, pick_score, pick_expert, iota


class InOrder:

    def __init__(self, engine, semaphore):
        self.engine, self.semaphore, self.value = engine, semaphore, 0

    def done(self, instruction):
        instruction.then_inc(self.semaphore, 1)
        self.value = self.value + 1
        self.engine.wait_ge(self.semaphore, self.value)


GRU = {
    "pe": ["edge gates", "heads", "edge candidate", "node"],
    "act": ["edge gates", "attention", "node gates", "edge tanh", "node tanh"],
    "dve": ["edge candidate", "node candidate", "x"],
    "settled": 10,
}


START = 10


def signalled(who, g, steps, back=0):
    each = GRU[who] if who == "settled" else len(GRU[who])
    return g * each + (START + steps - back * each)


def apart(engine, waits):
    engine.sem_inc(waits, 1)


class Steps:

    def __init__(self, engine, who, g, own=None):
        self.engine, self.who, self.g, self.own = engine, who, g, own
        self.signals, self.chain = [], 0

    def after(self, semaphore, who, name, back=0):
        self.engine.wait_ge(semaphore, signalled(who, self.g, GRU[who].index(name) + 1, back))

    def step(self, instruction, semaphore, name):
        self.signals.append(name)
        instruction.then_inc(semaphore, 1)

    def settled(self, instruction):
        self.chain += 1
        instruction.then_inc(self.own, 1)
        self.engine.wait_ge(self.own, signalled("settled", self.g, self.chain))

    def end(self):
        assert self.signals == GRU[self.who], self.signals
        assert self.own is None or self.chain == GRU["settled"], self.chain


def graph_layer_kernel(nc, x, x_t, adj_rows, adj_cols, diag, ident_in, sum_parts_in, pick_score_in,
                       pick_expert_in, iota_in, gat_w, gat_w_t, gat_a, edge_wih_t, edge_whh_t, edge_bih,
                       edge_bhh, node_wih_t, node_whh_t, node_bih, node_bhh, gamma, beta, wr, br, w1, b1,
                       w2, b2, out_t):
    f32, bf16, i32, u32 = mybir.dt.float32, mybir.dt.bfloat16, mybir.dt.int32, mybir.dt.uint32
    ALU = mybir.AluOpType
    ACT = mybir.ActivationFunctionType
    AX = mybir.AxisListType
    ctx = ExitStack()
    with ctx:
        def sb(name, shape, dt=f32):
            return ctx.enter_context(nc.sbuf_tensor(name, shape, dt))

        def sem(name):
            return ctx.enter_context(nc.semaphore(name))

        bank = [ctx.enter_context(nc.psum_tensor(f"bank{b}", [128, 512], f32)) for b in range(8)]

        h = sb("h", [128, TILES, HE])
        h_t = sb("h_t", [128, NP])
        support = sb("support", [128, NP])
        big = sb("big", [128, TILES * CHUNK])
        rowbuf = sb("rowbuf", [128, HEADS, NP])
        heads = sb("heads", [128, HEADS, NP])
        work = sb("work", [128, 12 * CHUNK])
        h_tile = sb("h_tile", [128, 2, HE])
        u_tile = sb("u_tile", [128, 2, 2 * UW], bf16)
        u_parts = sb("u_parts", [128, TILES, 2 * UW], bf16)
        ident = sb("ident", [128, 128])
        ones = sb("ones", [128, 128])
        off_diag = sb("off_diag", [128, 128])
        zero_bf = sb("zero_bf", [128, 512], bf16)
        minus_ones = sb("minus_ones", [128, 128])
        bn = sb("bn", [128, TILES, 6])
        stats = sb("stats", [128, 4, TILES])
        neg_max = sb("neg_max", [128, HEADS, TILES])
        denom = sb("denom", [128, HEADS, TILES])
        inv_denom = sb("inv_denom", [128, HEADS, TILES])
        row_max = sb("row_max", [128, 4])
        sum_parts = sb("sum_parts", [32, 32])
        pick_score = sb("pick_score", [32, SCORES, 128])
        att_vec = sb("att_vec", [128, HEADS, 2])
        w_att = sb("w_att", [128, SCORES])
        flag_f = sb("flag_f", [1, 1])
        flag = sb("flag", [1, 1], i32)

        h_feat = h[:, :, 0:H]
        x_nodes = support[:, :].rearrange("p (t f) -> p t f", f=H)
        gat_wt_sb = heads[:, 1, 0:HEADS * H].rearrange("p (i f) -> p i f", i=HEADS)
        NU = TILES * SCORES
        u_all = heads[:, 2, 0:NU].rearrange("p (t i s) -> p t i s", i=HEADS, s=2)
        u_f32 = heads[:, 2, NU:2 * NU].rearrange("p (t i s) -> p t i s", i=HEADS, s=2)
        u_part = heads[:, 2, 2 * NU:3 * NU].bitcast(bf16)[:, 0:NU]\
            .rearrange("p (t i s) -> p t i s", i=HEADS, s=2)
        score_parts = heads[0:32, 0, :]
        scores = heads[0:32, 1, :]
        scaled = heads[0:32, 2, 0:2 * CHUNK].rearrange("p (b c) -> p b c", b=2)
        cols = big[:, :].rearrange("p (t c) -> p t c", t=TILES)
        masks = work[:, 0:2 * CHUNK].bitcast(bf16).rearrange("p (b m c) -> p b m c", b=2, m=2)
        row = [big[:, i * NP:(i + 1) * NP] for i in range(2)]
        masked = [big[:, (2 + i) * NP:(3 + i) * NP] for i in range(2)]
        edge_mask = heads[:, 0, :]
        masked_minus = heads[:, 2, :]
        wexp = work[:, 0:6 * CHUNK].rearrange("p (b i c) -> p b i c", b=2, i=HEADS)
        wadj = work[:, 6 * CHUNK:12 * CHUNK].rearrange("p (b i c) -> p b i c", b=2, i=HEADS)
        spread = work[:, 0:8 * 128].rearrange("p (b t c) -> p b t c", b=2, c=128)

        def carve(buffer, widths):
            views, at = [], 0
            for width in widths:
                views.append(buffer[:, at:at + width])
                at += width
            assert at <= buffer.shape[-1], (at, buffer.shape)
            return views

        (x_feat, xn, w1_f, w2_f, wih_e, whh_e, wih_n, whh_n, pick_f) = carve(
            big[:, :], [NP, NP, E * HID, E * HID, 3 * H, 3 * H, 3 * H, 3 * H, E * 128 // 2])
        w1_sb = w1_f.rearrange("p (e f) -> p e f", e=E)
        w2_sb = w2_f.rearrange("p (e a d) -> p e a d", e=E, a=HALVES)
        pick_bf = pick_f.bitcast(bf16).rearrange("p (e c) -> p e c", e=E)
        gru_w = ((wih_e, whh_e), (wih_n, whh_n))
        (diag_bc, gates_t, gates_half, gw_f, bias_in_f, bias_f, gamma_sb, beta_sb, wr_sb, br_bc, b1_f, b2_sb,
         iota) = carve(rowbuf[:, :, :].rearrange("p i n -> p (i n)"),
                       [NP, NP, NP // 2, HEADS * H, 12, 6, 1, 1, E, E, E * HALVES, H, E])
        gates_bf = gates_half.bitcast(bf16)
        gat_w_sb = gw_f.rearrange("p (i f) -> p i f", i=HEADS)
        bias_in = bias_in_f.rearrange("p (g a) -> p g a", g=4)
        bias = bias_f.rearrange("p (g a) -> p g a", g=2)
        b1_sb = b1_f.rearrange("p (e a) -> p e a", e=E)
        gru_tmp = work[:, 0:2 * 7 * BLOCK].rearrange("p (b k n) -> p b k n", b=2, k=7)
        x_nm = heads[:, 2, :].rearrange("p (t f) -> p t f", f=H)
        RW = TILES * E
        (logit, rest, hot1, hot2, spare_f, gate, gbf_f, gparts_f, small_f) = (
            v for v in carve(work[:, 0:4096], [RW] * 6 + [RW // 2, STAT * RW, 6 * TILES]))
        logit, rest, hot1, hot2, picked, gate = (
            v.rearrange("p (t e) -> p t e", e=E) for v in (logit, rest, hot1, hot2, spare_f, gate))
        gbf = gbf_f.bitcast(bf16).rearrange("p (t e) -> p t e", e=E)
        gparts = gparts_f.rearrange("p (t q e) -> p t q e", q=STAT, e=E)
        first, second, where, gap, w_first, w_second = (small_f[:, k * TILES:(k + 1) * TILES] for k in range(6))
        act_f = work[:, 4096:4096 + 4 * BLOCK]
        pick32 = act_f[:, 0:E * 128].rearrange("p (e c) -> p e c", e=E)
        act_h = act_f.rearrange("p (b a n) -> p b a n", b=2, a=HALVES)
        prod_h = heads[:, 0, 0:4 * BLOCK].rearrange("p (b a n) -> p b a n", b=2, a=HALVES)
        y_sb = heads[:, 1, 0:2 * BLOCK].rearrange("p (b n) -> p b n", b=2)

        x_in, small_in, gatw_in, consts = sem("x_in"), sem("small_in"), sem("gatw_in"), sem("consts")
        dve_order, pool_order = sem("dve_order"), sem("pool_order")
        h_ready, ht_psum, ht_ready = sem("h_ready"), sem("ht_psum"), sem("ht_ready")
        var_ready, root_ready = sem("var_ready"), sem("root_ready")
        v_psum, v_ready, u_psum, u_ready = sem("v_psum"), sem("v_ready"), sem("u_psum"), sem("u_ready")
        a_in = [sem("a_in0"), sem("a_in1")]
        a_tile, a_mask, a_used, a_sums, a_kept = (sem("a_tile"), sem("a_mask"), sem("a_used"), sem("a_sums"),
                                                  sem("a_kept"))
        s_psum, s_scaled, s_ready = sem("s_psum"), sem("s_scaled"), sem("s_ready")
        b_psum, b_ready, c_psum, c_ready, f_ready = (sem("b_psum"), sem("b_ready"), sem("c_psum"),
                                                     sem("c_ready"), sem("f_ready"))
        PATHS = ("plain", "signed")
        r_in = {v: [sem(f"r_in_{v}{i}") for i in range(2)] for v in PATHS}
        r_free, r_max, r_exp, r_order = ({v: sem(f"{n}_{v}") for v in PATHS}
                                         for n in ("r_free", "r_max", "r_exp", "r_order"))
        q_psum, q_ready = sem("q_psum"), sem("q_ready")
        rows_done = sem("rows_done")
        n_spread, n_psum, n_ready = sem("n_spread"), sem("n_psum"), sem("n_ready")
        g_in = [sem("g_in0"), sem("g_in1")]
        g_y, g_e, g_w, g_mm, g_sums, g_kept = (sem("g_y"), sem("g_e"), sem("g_w"), sem("g_mm"),
                                               sem("g_sums"), sem("g_kept"))
        g_relu, g_order_dve, g_tile = sem("g_relu"), sem("g_order_dve"), sem("g_tile")
        t_in, t_ready = sem("t_in"), sem("t_ready")
        by_pe, by_act, by_dve, dense_order = sem("by_pe"), sem("by_act"), sem("by_dve"), sem("dense_order")
        n_turned, n_normed, n_back, n_input = sem("n_turned"), sem("n_normed"), sem("n_back"), sem("n_input")
        l_psum, l_gap, l_weights, l_parts, l_turned, l_gates, l_rows = (
            sem(f"l_{n}") for n in ("psum", "gap", "weights", "parts", "turned", "gates", "rows"))
        m_hid, m_gate, m_act, m_prod, m_used, m_y, m_out = (
            sem(f"m_{n}") for n in ("hid", "gate", "act", "prod", "used", "y", "out"))
        m_stored = [sem("m_stored0"), sem("m_stored1")]

        dve_waits = sem("dve_waits")

        NCH = len(CHUNKS)
        parities = range(2)
        GROUPS = [(q, range(4 * q, min(4 * q + 4, TILES))) for q in range(-(-TILES // 4))]
        block = ctx.enter_context(nc.Block())
        WEIGHT_LOADS = 23

        @block.sync
        def _(sp):
            sp.dma_start(x_nodes, x.rearrange("(t p) f -> p t f", p=128)).then_inc(x_in, 16)
            for dst, src in ((ident[:, :], ident_in), (sum_parts[:, :], sum_parts_in),
                             (pick_score[:, :, :], pick_score_in)):
                sp.dma_start(dst, src).then_inc(small_in, 16)
            sp.dma_start(gat_wt_sb, gat_w_t.rearrange("i p f -> p i f")).then_inc(gatw_in, 16)
            for i in range(HEADS):
                sp.dma_start(att_vec[:, i, :], gat_a[i].rearrange("(s p) o -> p (s o)", p=128),
                             allow_slow_non_contiguous=True).then_inc(gatw_in, 16)

            def load_columns(c, arrived, used):
                c0, w = CHUNKS[c]
                for part, (t0, t1) in enumerate(PARTS):
                    if c > 0:
                        sp.wait_ge(used, TILES * (c - 1) + t1 + FREE)
                    src = adj_cols[t0 * 128:t1 * 128, c0:c0 + w].rearrange("(t p) c -> p t c", p=128)
                    sp.dma_start(cols[:, t0:t1, 0:w], src).then_inc(arrived[part], 16)

            def load_rows(v, tiles, offset=0):
                with sp.Fori(0, tiles // 2) as p:
                    for b in parities:
                        sp.wait_ge(r_free[v], 2 * p + b + 1 + offset)
                        sp.dma_start(row[b], adj_rows[bass.ds((2 * p + b) * 128, 128), :])\
                            .then_inc(r_in[v][b], 16)

            for c in range(NCH):
                load_columns(c, a_in, a_used)
            sp.wait_ge(a_used, TILES * NCH + FREE)
            sp.wait_ge(f_ready, 1)
            signed = sp.value_load(flag[0:1, 0:1])
            with sp.If(signed > 0):
                for head in range(HEADS):
                    load_rows("signed", TILES, TILES * head)
            with sp.Else():
                load_rows("plain", TILES)
            sp.wait_ge(rows_done, 1)
            for c in range(NCH):
                load_columns(c, g_in, g_mm)
            sp.wait_ge(g_mm, TILES * NCH + FREE)
            loads = (
                (x_feat, x_t), (w1_sb, w1.rearrange("e d f -> d e f")),
                (w2_sb, w2.rearrange("e (a p) d -> p e a d", p=128)),
                (wih_e, edge_wih_t), (whh_e, edge_whh_t), (wih_n, node_wih_t), (whh_n, node_whh_t),
                (gat_w_sb, gat_w.rearrange("i p f -> p i f")), (diag_bc, diag.partition_broadcast(128)),
                (bias_in[:, 0, :], edge_bih.rearrange("(a p) -> p a", p=128)),
                (bias_in[:, 1, :], edge_bhh.rearrange("(a p) -> p a", p=128)),
                (bias_in[:, 2, :], node_bih.rearrange("(a p) -> p a", p=128)),
                (bias_in[:, 3, :], node_bhh.rearrange("(a p) -> p a", p=128)),
                (gamma_sb, gamma.rearrange("(p a) -> p a", a=1)), (beta_sb, beta.rearrange("(p a) -> p a", a=1)),
                (wr_sb, wr), (br_bc, br.partition_broadcast(128)), (b1_sb, b1.rearrange("e (a p) -> p e a", p=128)),
                (b2_sb[0:E, :], b2), (b2_sb[E:2 * E, :], b2), (b2_sb[2 * E:3 * E, :], b2),
                (pick32[0:32, :, :], pick_expert_in), (iota, iota_in))
            assert len(loads) == WEIGHT_LOADS
            for dst, src in loads:
                sp.dma_start(dst, src, allow_slow_non_contiguous=True).then_inc(t_in, 16)
            with sp.Fori(0, BLOCKS // 2) as g:
                for b in parities:
                    sp.wait_ge(m_out, 2 * g + b + 1 + FREE)
                    sp.dma_start(out_t[:, bass.ds((2 * g + b) * BLOCK, BLOCK)], y_sb[:, b, :])\
                        .then_inc(m_stored[b], 16)
            for b in parities:
                sp.wait_ge(m_stored[b], 16 * (BLOCKS // 2 + 1))

        @block.gpsimd
        def _(pool):
            order = InOrder(pool, pool_order)
            nc.gpsimd.memset(ones[:, :], 1.0).then_inc(consts, 1)
            nc.gpsimd.memset(minus_ones[:, :], -1.0).then_inc(consts, 1)
            nc.gpsimd.memset(zero_bf[:, :], 0.0).then_inc(consts, 1)
            order.done(nc.gpsimd.memset(off_diag[:, :], 1.0))
            nc.gpsimd.affine_select(out=off_diag[:, :], in_=off_diag[:, :], compare_op=ALU.not_equal,
                                    fill=0.0, base=0, pattern=[[-1, 128]], channel_multiplier=1)\
                .then_inc(consts, 1)

            def clear_diagonal(c, part):
                c0, w = CHUNKS[c]
                for t in range(*PARTS[part]):
                    if c0 <= t * 128 < c0 + w:
                        crossed = cols[:, t, t * 128 - c0:t * 128 - c0 + 128]
                        order.done(nc.gpsimd.affine_select(
                            out=crossed, in_=crossed, compare_op=ALU.not_equal, fill=0.0, base=0,
                            pattern=[[-1, 128]], channel_multiplier=1))

            pool.wait_ge(h_ready, 1)
            pool.wait_ge(u_ready, 1)
            for c in range(NCH):
                for part, (t0, t1) in enumerate(PARTS):
                    pool.wait_ge(a_in[part], 16 * (c + 1))
                    clear_diagonal(c, part)
                    with pool.Fori(0, (t1 - t0) // 2) as p:
                        for b in parities:
                            t = 2 * p + (t0 + b)
                            pool.wait_ge(a_used, TILES * c + 1 + t)
                            nc.gpsimd.tensor_copy(u_tile[:, b, :], u_parts[:, bass.ds(t, 1), :].squeeze(1))\
                                .then_inc(a_tile, 1)
                            nc.gpsimd.tensor_copy(h_tile[:, b, 0:H], h[:, bass.ds(t, 1), 0:H].squeeze(1))\
                                .then_inc(a_tile, 1)

            for c in range(NCH):
                for part, (t0, t1) in enumerate(PARTS):
                    pool.wait_ge(g_in[part], 16 * (c + 1))
                    clear_diagonal(c, part)
                    with pool.Fori(0, (t1 - t0) // 2) as p:
                        for b in parities:
                            t = 2 * p + (t0 + b)
                            pool.wait_ge(g_mm, TILES * c + 1 + t)
                            nc.gpsimd.tensor_copy(h_tile[:, b, 0:H], h[:, bass.ds(t, 1), 0:H].squeeze(1))\
                                .then_inc(g_tile, 1)

        @block.scalar
        def _(act):
            def root(k):
                act.wait_ge(var_ready, k + 1)
                nc.scalar.activation(stats[:, 1, :], stats[:, 0, :], ACT.Sqrt).then_inc(root_ready, 1)

            root(0)
            for q in range(-(-TILES // 4)):
                n = min(4, TILES - 4 * q) * 128
                act.wait_ge(ht_psum, q + 1)
                nc.scalar.activation(h_t[:, q * 512:q * 512 + n], bank[q % 2][:, 0:n], ACT.Copy)\
                    .then_inc(ht_ready, 1)
            for c, (c0, w) in enumerate(CHUNKS):
                act.wait_ge(a_sums, c + 1)
                nc.scalar.activation(support[:, c0:c0 + w], bank[c % 2][:, 0:w], ACT.Copy).then_inc(a_kept, 1)
                nc.scalar.activation(score_parts[:, c0:c0 + w], bank[2 + c % 2][0:32, 0:w], ACT.Copy)\
                    .then_inc(a_kept, 1)
            for c, (c0, w) in enumerate(CHUNKS):
                act.wait_ge(s_psum, c + 1)
                if c >= 2:
                    act.wait_ge(s_ready, c - 1)
                nc.scalar.activation(scaled[:, c % 2, 0:w], bank[4 + c % 2][0:32, 0:w], ACT.Copy, scale=ALPHA)\
                    .then_inc(s_scaled, 1)
            for q in range(HEADS * NCH):
                i, (c0, w) = q % HEADS, CHUNKS[q // HEADS]
                act.wait_ge(b_psum, q + 1)
                nc.scalar.activation(rowbuf[:, i, c0:c0 + w], bank[6 + q % 2][:, 0:w], ACT.Copy)\
                    .then_inc(b_ready, 1)
            act.wait_ge(f_ready, 1)
            signed = act.value_load(flag[0:1, 0:1])

            def denominators(v):
                nc.scalar.nop().then_inc(r_exp[v], FREE)
                if v == "plain":
                    with act.Fori(0, TILES // 2) as p:
                        for b in parities:
                            for i in range(HEADS):
                                k, n = (HEADS * b + i) % 2, HEADS * b + i
                                act.wait_ge(r_max[v], 2 * HEADS * p + (n + 1))
                                nc.scalar.activation(masked[k], masked[k], ACT.Exp,
                                                     bias=neg_max[:, i, bass.ds(2 * p + b, 1)],
                                                     accum_out=denom[:, i, bass.ds(2 * p + b, 1)])\
                                    .then_inc(r_exp[v], 1)
                    act.wait_ge(r_exp[v], HEADS * TILES + FREE)
                    return
                for head in range(HEADS):
                    for q in range(2 * NCH):
                        c0, w = CHUNKS[q // 2]
                        act.wait_ge(q_psum, 2 * NCH * head + q + 1)
                        nc.scalar.activation(rowbuf[:, q % 2, c0:c0 + w], bank[6 + q % 2][:, 0:w], ACT.Copy)\
                            .then_inc(q_ready, 1)
                    with act.Fori(0, TILES // 2) as p:
                        for b in parities:
                            act.wait_ge(r_max[v], 2 * p + (TILES * head + b + 1))
                            nc.scalar.activation(masked[b], masked[b], ACT.Exp,
                                                 bias=neg_max[:, head, bass.ds(2 * p + b, 1)],
                                                 accum_out=denom[:, head, bass.ds(2 * p + b, 1)])\
                                .then_inc(r_exp[v], 1)
                act.wait_ge(r_exp[v], HEADS * TILES + FREE)

            with act.If(signed > 0):
                denominators("signed")
            with act.Else():
                denominators("plain")
            nc.scalar.nop().then_inc(rows_done, 2)

            for q in range(2 * HEADS * NCH):
                i, (c0, w) = q % (2 * HEADS), CHUNKS[q // (2 * HEADS)]
                target = rowbuf[:, i, c0:c0 + w] if i < HEADS else heads[:, i - HEADS, c0:c0 + w]
                act.wait_ge(n_psum, q + 1)
                nc.scalar.activation(target, bank[q % 2][:, 0:w], ACT.Copy).then_inc(n_ready, 1)

            LAST = HEADS - 1

            def exponentials(v):
                for c, (c0, w) in enumerate(CHUNKS):
                    with act.Fori(0, TILES // 2) as p:
                        for b in parities:
                            n = TILES * c + b
                            if v == "signed":
                                place = work[:, 0:6 * CHUNK].rearrange("p (k c) -> p k c", c=CHUNK)[:, :, 0:w]
                                act.wait_ge(g_y, 2 * p + (n + 1))
                                nc.scalar.activation(place, place, ACT.Exp, scale=-1.0).then_inc(g_e, 1)
                                continue
                            act.wait_ge(g_w, 2 * p + (n + 1))
                            place = wexp[:, b, LAST, 0:w]
                            minus_e = h[:, bass.ds(2 * p + b, 1), H + SCORES + LAST]
                            nc.scalar.activation(place, rowbuf[:, LAST, c0:c0 + w], ACT.Relu, bias=minus_e)\
                                .then_inc(g_relu, 1)
                            act.wait_ge(g_y, 2 * p + (n + 1))
                            both = wexp[:, b, 0:LAST, 0:w]
                            nc.scalar.activation(both, both, ACT.Exp, scale=-1.0)
                            act.wait_ge(g_relu, 2 * p + (n + 1))
                            nc.scalar.activation(place, place, ACT.Exp, scale=-1.0).then_inc(g_e, 1)

            with act.If(signed > 0):
                exponentials("signed")
            with act.Else():
                exponentials("plain")

            act.wait_ge(t_ready, 3)
            nc.scalar.nop().then_inc(by_act, START)
            with act.Fori(0, BLOCKS // 2) as gg:
                for b in parities:
                    at = Steps(act, "act", 2 * gg + b)
                    att, e_r, e_z, _, n_r, n_z, _ = (gru_tmp[:, b, k, :] for k in range(7))
                    at.after(by_dve, "dve", "x", back=2)
                    at.after(by_pe, "pe", "edge gates")
                    nc.scalar.activation(e_r, bank[1][:, 0:BLOCK], ACT.Sigmoid, bias=bias[:, 0, 0:1])
                    at.step(nc.scalar.activation(e_z, bank[2][:, 0:BLOCK], ACT.Sigmoid, bias=bias[:, 0, 1:2]),
                            by_act, "edge gates")
                    at.after(by_pe, "pe", "heads")
                    at.step(nc.scalar.activation(att, bank[0][:, 0:BLOCK], ACT.Copy), by_act, "attention")
                    at.after(by_pe, "pe", "node")
                    nc.scalar.activation(n_r, bank[5][:, 0:BLOCK], ACT.Sigmoid, bias=bias[:, 1, 0:1])
                    at.step(nc.scalar.activation(n_z, bank[6][:, 0:BLOCK], ACT.Sigmoid, bias=bias[:, 1, 1:2]),
                            by_act, "node gates")
                    at.after(by_dve, "dve", "edge candidate")
                    at.step(nc.scalar.activation(e_r, e_r, ACT.Tanh), by_act, "edge tanh")
                    at.after(by_dve, "dve", "node candidate")
                    at.step(nc.scalar.activation(n_r, n_r, ACT.Tanh), by_act, "node tanh")
                    at.end()

            root(1)
            root(2)
            for q, tiles in GROUPS:
                w = len(tiles) * 128
                act.wait_ge(n_back, q + 1)
                nc.scalar.activation(xn[:, q * 512:q * 512 + w], bank[q][:, 0:w], ACT.Identity, bias=beta_sb,
                                     scale=gamma_sb).then_inc(n_input, 1)
            act.wait_ge(l_gap, 1)
            nc.scalar.activation(w_first, gap, ACT.Sigmoid)
            nc.scalar.activation(w_second, gap, ACT.Sigmoid, scale=-1.0).then_inc(l_weights, 1)
            for q, tiles in GROUPS:
                w = len(tiles) * 128
                act.wait_ge(l_turned, q + 1)
                nc.scalar.activation(gates_bf[0:GROWS, q * 512:q * 512 + w], bank[q][0:GROWS, 0:w], ACT.Copy)\
                    .then_inc(l_gates, 1)

            with act.Fori(0, BLOCKS) as g:
                for e in range(E):
                    b = e % 2
                    act.wait_ge(m_hid, g * E + (e + 1))
                    act.wait_ge(m_prod, g * E + (e + 1))
                    for a in range(HALVES):
                        last = nc.scalar.activation(act_h[:, b, a, :], bank[2 * b + a][:, 0:BLOCK], ACT.Gelu,
                                                    bias=b1_sb[:, e, a:a + 1])
                    last.then_inc(m_act, 1)

        @block.vector
        def _(dve):
            order = InOrder(dve, dve_order)

            def inverse_root(root, value, spare, settled):
                settled(nc.vector.reciprocal(root, root))
                settled(nc.vector.tensor_tensor(spare, root, root, ALU.mult))
                settled(nc.vector.tensor_tensor(spare, spare, value, ALU.mult))
                settled(nc.vector.tensor_scalar(spare, spare, -0.5, 1.5, ALU.mult, ALU.add))
                settled(nc.vector.tensor_tensor(root, root, spare, ALU.mult))

            def normalise(source, out, k, ready=None):
                for q, tiles in GROUPS:
                    if ready is not None:
                        dve.wait_ge(ready, q + 1)
                    for t in tiles:
                        last = nc.vector.bn_stats(bn[:, t, :], source(t))
                order.done(last)
                mean, inv, value, spare = stats[:, 2, :], stats[:, 1, :], stats[:, 0, :], stats[:, 3, :]
                nc.vector.tensor_tensor(mean, bn[:, :, 1], bn[:, :, 4], ALU.add)
                order.done(nc.vector.tensor_tensor(value, bn[:, :, 2], bn[:, :, 5], ALU.add))
                nc.vector.tensor_tensor(spare, bn[:, :, 1], bn[:, :, 4], ALU.subtract)
                order.done(nc.vector.tensor_scalar(value, value, 1.0 / H, EPS, ALU.mult, ALU.add))
                order.done(nc.vector.tensor_tensor(spare, spare, spare, ALU.mult))
                nc.vector.tensor_scalar(mean, mean, 0.5, None, ALU.mult)
                nc.vector.scalar_tensor_tensor(out=value, in0=spare, scalar=0.25, in1=value, op0=ALU.mult,
                                               op1=ALU.add).then_inc(var_ready, 1)
                dve.wait_ge(root_ready, k + 1)
                inverse_root(inv, value, spare, order.done)
                for t in range(TILES):
                    last = nc.vector.tensor_scalar(out[:, t, :], source(t), mean[:, t:t + 1], inv[:, t:t + 1],
                                                   ALU.subtract, ALU.mult)
                return last

            dve.wait_ge(x_in, 16)
            normalise(lambda t: x_nodes[:, t, :], h_feat, 0).then_inc(h_ready, 2)
            dve.wait_ge(v_psum, 1)
            nc.vector.tensor_copy(w_att[:, :], bank[2][:, 0:SCORES]).then_inc(v_ready, 1)
            order.done(nc.vector.memset(u_parts[:, :, :], 0.0))
            order.done(nc.vector.memset(u_parts[:, :, UW:UW + 1], 1.0))
            dve.wait_ge(u_psum, 1)
            order.done(nc.vector.tensor_copy(heads[:, 2, 0:NU], bank[3][:, 0:NU]))
            for q in range(STAT):
                order.done(nc.vector.tensor_copy(u_part, u_all))
                for s in range(2):
                    for m in range(2):
                        at = UW * m + 1 + SCORES * q + HEADS * s
                        nc.vector.tensor_copy(u_parts[:, :, at:at + HEADS], u_part[:, :, :, s ^ m])
                order.done(nc.vector.tensor_copy(u_f32, u_part))
                if q < STAT - 1:
                    order.done(nc.vector.tensor_tensor(u_all, u_all, u_f32, ALU.subtract))
            nc.vector.nop().then_inc(u_ready, 1)

            for c, (c0, w) in enumerate(CHUNKS):
                with dve.Fori(0, TILES // 2) as p:
                    for b in parities:
                        n = TILES * c + b
                        dve.wait_ge(a_tile, 4 * p + 2 * (n + 1))
                        dve.wait_ge(a_used, 2 * p + (n + 1))
                        tile = cols[:, bass.ds(2 * p + b, 1), 0:w].squeeze(1)
                        nc.vector.tensor_scalar(masks[:, b, 0, 0:w], tile, 0.0, None, ALU.is_gt)
                        nc.vector.tensor_scalar(masks[:, b, 1, 0:w], tile, 0.0, None, ALU.is_lt)\
                            .then_inc(a_mask, 1)
            for c, (c0, w) in enumerate(CHUNKS):
                dve.wait_ge(s_scaled, c + 1)
                nc.vector.tensor_tensor(scores[:, c0:c0 + w], scaled[:, c % 2, 0:w], bank[4 + c % 2][0:32, 0:w],
                                        ALU.max).then_inc(s_ready, 1)
            order.done(nc.vector.tensor_reduce(flag_f[:, :], score_parts[0:1, :], AX.X, ALU.max))
            nc.vector.tensor_copy(flag[:, :], flag_f[:, :]).then_inc(f_ready, 1)
            dve.wait_ge(f_ready, 1)
            signed = dve.value_load(flag[0:1, 0:1])
            dve.wait_ge(c_psum, 1)
            by_node = bank[3][:, 0:NU].rearrange("p (t r) -> p t r", r=SCORES)
            nc.vector.tensor_copy(h[:, :, H:H + SCORES], by_node)
            nc.vector.tensor_scalar(h[:, :, H + SCORES:HE], by_node[:, :, 0:HEADS], -1.0, None, ALU.mult)\
                .then_inc(c_ready, 1)

            def maxima(v):
                step = r_order[v]
                nc.vector.nop().then_inc(r_free[v], FREE)
                if v == "plain":
                    EACH = 2 + HEADS
                    dve.wait_ge(b_ready, HEADS * NCH)
                    with dve.Fori(0, TILES // 2) as p:
                        for b in parities:
                            at = EACH * b
                            dve.wait_ge(r_in[v][b], 16 * p + 16)
                            crossed = row[b][:, bass.ds((2 * p + b) * 128, 128)]
                            nc.vector.tensor_tensor(crossed, crossed, off_diag[:, :], ALU.mult).then_inc(step, 1)
                            dve.wait_ge(step, 2 * EACH * p + (at + 1))
                            nc.vector.tensor_scalar(row[b], row[b], 0.0, NEG_INF, ALU.is_le, ALU.mult)\
                                .then_inc(step, 1)
                            dve.wait_ge(step, 2 * EACH * p + (at + 2))
                            for i in range(HEADS):
                                n = HEADS * b + i
                                dve.wait_ge(r_exp[v], 2 * HEADS * p + (n + 1))
                                apart(dve, dve_waits)
                                nc.vector.tensor_tensor_reduce(
                                    out=masked[n % 2], in0=row[b], in1=rowbuf[:, i, :], scale=1.0,
                                    scalar=LOWEST, op0=ALU.add, op1=ALU.max,
                                    accum_out=row_max[:, i:i + 1]).then_inc(step, 1)
                                dve.wait_ge(step, 2 * EACH * p + (at + 3 + i))
                                nc.vector.tensor_scalar(neg_max[:, i, bass.ds(2 * p + b, 1)],
                                                        row_max[:, i:i + 1], -1.0, None, ALU.mult)\
                                    .then_inc(r_max[v], 1)
                            nc.vector.nop().then_inc(r_free[v], 1)
                    return
                EACH = 7
                for head in range(HEADS):
                    dve.wait_ge(q_ready, 2 * NCH * (head + 1))
                    with dve.Fori(0, TILES // 2) as p:
                        for b in parities:
                            at = EACH * (TILES * head + b)
                            dve.wait_ge(r_in[v][b], 16 * p + 16 * (TILES // 2 * head + 1))
                            crossed = row[b][:, bass.ds((2 * p + b) * 128, 128)]
                            nc.vector.tensor_tensor(crossed, crossed, off_diag[:, :], ALU.mult).then_inc(step, 1)
                            dve.wait_ge(step, 2 * EACH * p + (at + 1))
                            nc.vector.tensor_scalar(edge_mask, row[b], 0.0, NEG_INF, ALU.is_le, ALU.mult)\
                                .then_inc(step, 1)
                            dve.wait_ge(step, 2 * EACH * p + (at + 2))
                            dve.wait_ge(r_exp[v], 2 * p + (TILES * head + b + 1))
                            apart(dve, dve_waits)
                            nc.vector.tensor_tensor_reduce(
                                out=masked[b], in0=edge_mask, in1=rowbuf[:, 0, :], scale=1.0, scalar=LOWEST,
                                op0=ALU.add, op1=ALU.max, accum_out=row_max[:, 0:1]).then_inc(step, 1)
                            dve.wait_ge(step, 2 * EACH * p + (at + 3))
                            nc.vector.tensor_scalar(edge_mask, row[b], 0.0, NEG_INF, ALU.is_ge, ALU.mult)\
                                .then_inc(step, 1)
                            dve.wait_ge(step, 2 * EACH * p + (at + 4))
                            apart(dve, dve_waits)
                            nc.vector.tensor_tensor_reduce(
                                out=masked_minus, in0=edge_mask, in1=rowbuf[:, 1, :], scale=1.0, scalar=LOWEST,
                                op0=ALU.add, op1=ALU.max, accum_out=row_max[:, 1:2]).then_inc(step, 1)
                            dve.wait_ge(step, 2 * EACH * p + (at + 5))
                            nc.vector.tensor_tensor(masked[b], masked[b], masked_minus, ALU.max)\
                                .then_inc(step, 1)
                            nc.vector.tensor_tensor(row_max[:, 2:3], row_max[:, 0:1], row_max[:, 1:2], ALU.max)\
                                .then_inc(step, 1)
                            dve.wait_ge(step, 2 * EACH * p + (at + 7))
                            nc.vector.tensor_scalar(neg_max[:, head, bass.ds(2 * p + b, 1)],
                                                    row_max[:, 2:3], -1.0, None, ALU.mult).then_inc(r_max[v], 1)
                            nc.vector.nop().then_inc(r_free[v], 1)

            with dve.If(signed > 0):
                maxima("signed")
                dve.wait_ge(r_max["signed"], HEADS * TILES)
            with dve.Else():
                maxima("plain")
                dve.wait_ge(r_max["plain"], HEADS * TILES)

            dve.wait_ge(rows_done, 1)
            order.done(nc.vector.tensor_scalar(inv_denom[:, :, :], denom[:, :, :], float(HEADS), None, ALU.mult))
            order.done(nc.vector.reciprocal(inv_denom[:, :, :], inv_denom[:, :, :]))
            for q in range(2 * HEADS * NCH):
                i, (c0, w) = q % (2 * HEADS), CHUNKS[q // (2 * HEADS)]
                source = neg_max if i < HEADS else inv_denom
                t, n = c0 // 128, w // 128
                if q >= 2:
                    dve.wait_ge(n_psum, q - 1)
                nc.vector.tensor_tensor(
                    spread[:, q % 2, 0:n, :], ident[:, :].unsqueeze(1).broadcast_to([128, n, 128]),
                    source[:, i % HEADS, t:t + n].unsqueeze(2).broadcast_to([128, n, 128]), ALU.mult)\
                    .then_inc(n_spread, 1)

            def keep(c):
                c0, w = CHUNKS[c]
                dve.wait_ge(g_sums, c + 1)
                for i in range(HEADS):
                    nc.vector.tensor_tensor(heads[:, i, c0:c0 + w], heads[:, i, c0:c0 + w],
                                            bank[3 * (c % 2) + i][:, 0:w], ALU.mult).then_inc(g_kept, 1)

            def products_signed():
                nc.vector.nop().then_inc(g_w, FREE)
                for c, (c0, w) in enumerate(CHUNKS):
                    with dve.Fori(0, TILES // 2) as p:
                        for b in parities:
                            n, t = TILES * c + b, 2 * p + b
                            dve.wait_ge(g_tile, 2 * p + (n + 1))
                            for s in parities:
                                for i in range(HEADS):
                                    last = nc.vector.tensor_scalar(
                                        wexp[:, s, i, 0:w], rowbuf[:, i, c0:c0 + w],
                                        h[:, bass.ds(t, 1), H + HEADS * s + i], 0.0, ALU.subtract, ALU.max)
                            last.then_inc(g_y, 1)
                            dve.wait_ge(g_e, 2 * p + (n + 1))
                            dve.wait_ge(g_mm, 2 * p + (n + 2))
                            for s, part in enumerate((ALU.max, ALU.min)):
                                for i in range(HEADS):
                                    last = nc.vector.scalar_tensor_tensor(
                                        out=wadj[:, s, i, 0:w], in0=cols[:, bass.ds(t, 1), 0:w].squeeze(1),
                                        scalar=0.0, in1=wexp[:, s, i, 0:w], op0=part, op1=ALU.mult)
                            last.then_inc(g_order_dve, 1)
                            dve.wait_ge(g_order_dve, 2 * p + (n + 1))
                            nc.vector.tensor_tensor(wadj[:, 0, :, 0:w], wadj[:, 0, :, 0:w],
                                                    wadj[:, 1, :, 0:w], ALU.add).then_inc(g_w, 1)
                    keep(c)

            def products_plain():
                nc.vector.nop().then_inc(g_w, FREE)

                def distance(c, t, b):
                    c0, w = CHUNKS[c]
                    dve.wait_ge(g_w, t + (TILES * c + 1))
                    for i in range(HEADS - 1):
                        last = nc.vector.tensor_scalar(wexp[:, b, i, 0:w], rowbuf[:, i, c0:c0 + w],
                                                       h[:, bass.ds(t, 1), H + i], 0.0, ALU.subtract, ALU.max)
                    last.then_inc(g_y, 1)

                def product(c, t, b):
                    c0, w = CHUNKS[c]
                    dve.wait_ge(g_e, t + (TILES * c + 1))
                    dve.wait_ge(g_tile, t + (TILES * c + 1))
                    dve.wait_ge(g_mm, t + (TILES * c + 1))
                    nc.vector.tensor_tensor(wadj[:, b, :, 0:w], wexp[:, b, :, 0:w],
                                            cols[:, bass.ds(t, 1), 0:w].broadcast_to([128, HEADS, w]), ALU.mult)\
                        .then_inc(g_w, 1)

                distance(0, 0, 0)
                for c in range(NCH):
                    with dve.Fori(0, TILES // 2 - 1) as p:
                        distance(c, 2 * p + 1, 1)
                        product(c, 2 * p, 0)
                        distance(c, 2 * p + 2, 0)
                        product(c, 2 * p + 1, 1)
                    distance(c, TILES - 1, 1)
                    product(c, TILES - 2, 0)
                    if c + 1 < NCH:
                        distance(c + 1, 0, 0)
                    product(c, TILES - 1, 1)
                    keep(c)

            dve.wait_ge(n_ready, 2 * HEADS * NCH)
            with dve.If(signed > 0):
                products_signed()
            with dve.Else():
                products_plain()

            dve.wait_ge(t_in, 16 * WEIGHT_LOADS)
            nc.vector.tensor_copy(pick_bf[0:32, :, :], pick32[0:32, :, :]).then_inc(t_ready, 1)
            for c in range(2):
                nc.vector.tensor_tensor(bias[:, c, :], bias_in[:, 2 * c, :], bias_in[:, 2 * c + 1, :], ALU.add)\
                    .then_inc(t_ready, 1)
            nc.vector.nop().then_inc(by_dve, START)
            nc.vector.nop().then_inc(dense_order, START)
            with dve.Fori(0, BLOCKS // 2) as gg:
                for b in parities:
                    here = bass.ds((2 * gg + b) * BLOCK, BLOCK)
                    at = Steps(dve, "dve", 2 * gg + b, dense_order)
                    _, e_r, e_z, e_out, n_r, n_z, n_out = (gru_tmp[:, b, k, :] for k in range(7))

                    def candidate(gru, reset, bank_in, bank_hn, name):
                        at.settled(nc.vector.scalar_tensor_tensor(
                            out=reset, in0=bank_hn[:, 0:BLOCK], scalar=bias_in[:, 2 * gru + 1, 2:3], in1=reset,
                            op0=ALU.add, op1=ALU.mult))
                        at.step(nc.vector.scalar_tensor_tensor(
                            out=reset, in0=bank_in[:, 0:BLOCK], scalar=bias_in[:, 2 * gru, 2:3], in1=reset,
                            op0=ALU.add, op1=ALU.add), by_dve, name + " candidate")

                    def mix(out, update, cand, name):
                        at.after(by_act, "act", name + " tanh")
                        at.settled(nc.vector.tensor_tensor(out, h_t[:, here], cand, ALU.subtract))
                        at.settled(nc.vector.tensor_tensor(out, out, update, ALU.mult))
                        at.settled(nc.vector.tensor_tensor(out, out, cand, ALU.add))

                    at.after(by_act, "act", "edge gates")
                    at.after(by_pe, "pe", "edge candidate")
                    candidate(0, e_r, bank[3], bank[4], "edge")
                    at.after(by_act, "act", "node gates")
                    candidate(1, n_r, bank[7], bank[0], "node")
                    mix(e_out, e_z, e_r, "edge")
                    mix(n_out, n_z, n_r, "node")
                    at.settled(nc.vector.tensor_tensor(e_out, e_out, n_out, ALU.add))
                    at.settled(nc.vector.tensor_tensor(e_out, e_out, diag_bc[:, here], ALU.mult))
                    at.step(nc.vector.tensor_tensor(x_feat[:, here], x_feat[:, here], e_out, ALU.add), by_dve, "x")
                    at.end()

            order.done(normalise(lambda t: bank[t // 4][:, t % 4 * 128:(t % 4 + 1) * 128], x_nm, 1, n_turned))
            normalise(lambda t: x_nm[:, t, :], x_nm, 2).then_inc(n_normed, 1)

            wide = [128, TILES, E]
            codes = iota.unsqueeze(1).broadcast_to(wide)

            def spread_out(value):
                return value.unsqueeze(2).broadcast_to(wide)

            def largest(values, best, hot):
                order.done(nc.vector.tensor_reduce(best, values, AX.X, ALU.max))
                order.done(nc.vector.tensor_tensor(picked, values, spread_out(best), ALU.is_equal))
                order.done(nc.vector.tensor_tensor(picked, picked, codes, ALU.mult))
                order.done(nc.vector.tensor_reduce(where, picked, AX.X, ALU.min))
                order.done(nc.vector.tensor_tensor(hot, codes, spread_out(where), ALU.is_equal))

            dve.wait_ge(l_psum, 1)
            order.done(nc.vector.tensor_tensor(logit, bank[7][:, 0:RW].rearrange("p (t e) -> p t e", e=E),
                                               br_bc.unsqueeze(1).broadcast_to(wide), ALU.add))
            largest(logit, first, hot1)
            order.done(nc.vector.scalar_tensor_tensor(out=rest, in0=hot1, scalar=LOWEST, in1=logit, op0=ALU.mult,
                                                      op1=ALU.add))
            largest(rest, second, hot2)
            nc.vector.tensor_tensor(gap, first, second, ALU.subtract).then_inc(l_gap, 1)
            dve.wait_ge(l_weights, 1)
            nc.vector.tensor_tensor(hot1, hot1, spread_out(w_first), ALU.mult)
            order.done(nc.vector.tensor_tensor(hot2, hot2, spread_out(w_second), ALU.mult))
            order.done(nc.vector.tensor_tensor(gate, hot1, hot2, ALU.add))
            for q in range(STAT):
                order.done(nc.vector.tensor_copy(gbf, gate))
                order.done(nc.vector.tensor_copy(gparts[:, :, q, :], gbf))
                if q < STAT - 1:
                    order.done(nc.vector.tensor_tensor(gate, gate, gparts[:, :, q, :], ALU.subtract))
            nc.vector.nop().then_inc(l_parts, 1)
            for q, tiles in GROUPS:
                w = len(tiles) * 128
                dve.wait_ge(l_gates, q + 1)
                nc.vector.tensor_copy(gates_t[0:GROWS, q * 512:q * 512 + w],
                                      gates_bf[0:GROWS, q * 512:q * 512 + w]).then_inc(l_rows, 1)

            nc.vector.nop().then_inc(m_prod, FREE)
            nc.vector.nop().then_inc(m_out, FREE)
            for b in parities:
                nc.vector.nop().then_inc(m_stored[b], 16)
            with dve.Fori(0, BLOCKS // 2) as gg:
                for gb in parities:
                    for e in range(E):
                        b, n = e % 2, E * gb + e
                        dve.wait_ge(m_act, 2 * E * gg + (n + 1))
                        dve.wait_ge(m_gate, 2 * E * gg + (n + 1))
                        dve.wait_ge(m_used, 2 * E * gg + (n + 1))
                        nc.vector.tensor_tensor(
                            prod_h[:, b, :, :], act_h[:, b, :, :],
                            bank[4 + b][:, 0:BLOCK].unsqueeze(1).broadcast_to([128, HALVES, BLOCK]), ALU.mult)\
                            .then_inc(m_prod, 1)
                    dve.wait_ge(m_y, 2 * gg + (gb + 1))
                    dve.wait_ge(m_stored[gb], 16 * gg + 16)
                    nc.vector.tensor_tensor(y_sb[:, gb, :], bank[6 + gb][:, 0:BLOCK],
                                            x_feat[:, bass.ds((2 * gg + gb) * BLOCK, BLOCK)], ALU.add)\
                        .then_inc(m_out, 1)

        @block.tensor
        def _(pe):
            pe.wait_ge(small_in, 48)
            pe.wait_ge(consts, 4)
            pe.wait_ge(h_ready, 2)
            for t in range(TILES):
                q = t // 4
                if t % 4 == 0 and q >= 2:
                    pe.wait_ge(ht_ready, q - 1)
                last = nc.tensor.transpose(bank[q % 2][:, t % 4 * 128:(t % 4 + 1) * 128], h[:, t, 0:H],
                                           ident[:, :])
                if t % 4 == 3 or t == TILES - 1:
                    last.then_inc(ht_psum, 1)
            pe.wait_ge(gatw_in, 16 * (1 + HEADS))
            for i in range(HEADS):
                last = nc.tensor.matmul(bank[2][:, 2 * i:2 * i + 2], gat_wt_sb[:, i, :], att_vec[:, i, :],
                                        start=True, stop=True)
            last.then_inc(v_psum, 1)
            pe.wait_ge(v_ready, 1)
            pe.wait_ge(ht_ready, -(-TILES // 4))
            for t in range(TILES):
                last = nc.tensor.matmul(bank[3][:, t * SCORES:(t + 1) * SCORES], h_t[:, t * 128:(t + 1) * 128],
                                        w_att[:, :], start=True, stop=True)
            last.then_inc(u_psum, 1)

            def clear(out, free=None):
                m = out.shape[0]
                return nc.tensor.matmul(out, zero_bf[:, 0:m], zero_bf[:, 0:out.shape[1]], start=True, stop=False)

            def close(out):
                m = out.shape[0]
                return nc.tensor.matmul(out, zero_bf[:, 0:m], zero_bf[:, 0:out.shape[1]], start=False, stop=True)

            pe.wait_ge(u_ready, 1)
            for c, (c0, w) in enumerate(CHUNKS):
                if c >= 2:
                    pe.wait_ge(a_kept, 2 * (c - 1))
                sums, parts = bank[c % 2][:, 0:w], bank[2 + c % 2][0:32, 0:w]
                clear(sums)
                last = clear(parts)
                if c == 0:
                    last.then_inc(a_used, FREE)
                with pe.Fori(0, TILES // 2) as p:
                    for b in parities:
                        n = TILES * c + b
                        pe.wait_ge(a_tile, 4 * p + 2 * (n + 1))
                        nc.tensor.matmul(sums, h_tile[:, b, 0:H],
                                         cols[:, bass.ds(2 * p + b, 1), 0:w].squeeze(1), start=False, stop=False)
                        pe.wait_ge(a_mask, 2 * p + (n + 1))
                        nc.tensor.matmul(parts, u_tile[:, b, 0:UW], masks[:, b, 0, 0:w], start=False, stop=False)
                        nc.tensor.matmul(parts, u_tile[:, b, UW:2 * UW], masks[:, b, 1, 0:w], start=False,
                                         stop=False).then_inc(a_used, 1)
                close(sums)
                close(parts).then_inc(a_sums, 1)
            pe.wait_ge(a_kept, 2 * NCH)
            for c, (c0, w) in enumerate(CHUNKS):
                if c >= 2:
                    pe.wait_ge(s_ready, c - 1)
                nc.tensor.matmul(bank[4 + c % 2][0:32, 0:w], sum_parts[:, :], score_parts[:, c0:c0 + w],
                                 start=True, stop=True).then_inc(s_psum, 1)
            pe.wait_ge(s_ready, NCH)
            for q in range(HEADS * NCH):
                i, (c0, w) = q % HEADS, CHUNKS[q // HEADS]
                if q >= 2:
                    pe.wait_ge(b_ready, q - 1)
                nc.tensor.matmul(bank[6 + q % 2][:, 0:w], pick_score[:, i, :], scores[:, c0:c0 + w],
                                 start=True, stop=True).then_inc(b_psum, 1)
            for t in range(TILES):
                last = nc.tensor.matmul(bank[3][:, t * SCORES:(t + 1) * SCORES], scores[:, t * 128:(t + 1) * 128],
                                        ident[0:32, 0:SCORES], start=True, stop=True)
            last.then_inc(c_psum, 1)
            pe.wait_ge(f_ready, 1)
            signed = pe.value_load(flag[0:1, 0:1])
            with pe.If(signed > 0):
                pe.wait_ge(b_ready, HEADS * NCH)
                for head in range(HEADS):
                    if head > 0:
                        pe.wait_ge(r_max["signed"], TILES * head)
                    for q in range(2 * NCH):
                        c0, w = CHUNKS[q // 2]
                        if head > 0 or q >= 2:
                            pe.wait_ge(q_ready, 2 * NCH * head + q - 1)
                        nc.tensor.matmul(bank[6 + q % 2][:, 0:w], pick_score[:, HEADS * (q % 2) + head, :],
                                         scores[:, c0:c0 + w], start=True, stop=True).then_inc(q_psum, 1)
            for q in range(2 * HEADS * NCH):
                w = CHUNKS[q // (2 * HEADS)][1]
                column = minus_ones if q % (2 * HEADS) < HEADS else ones
                pe.wait_ge(n_spread, q + 1)
                if q >= 2:
                    pe.wait_ge(n_ready, q - 1)
                nc.tensor.matmul(bank[q % 2][:, 0:w], column[:, :],
                                 spread[:, q % 2, 0:w // 128, :].rearrange("p t c -> p (t c)"),
                                 start=True, stop=True).then_inc(n_psum, 1)
            pe.wait_ge(n_ready, 2 * HEADS * NCH)

            def sum_heads(v):
                for c, (c0, w) in enumerate(CHUNKS):
                    if c >= 2:
                        pe.wait_ge(g_kept, HEADS * (c - 1))
                    sums = [bank[3 * (c % 2) + i][:, 0:w] for i in range(HEADS)]
                    for out in sums:
                        last = clear(out)
                    if c == 0:
                        last.then_inc(g_mm, FREE)
                    with pe.Fori(0, TILES // 2) as p:
                        for b in parities:
                            pe.wait_ge(g_tile, 2 * p + (TILES * c + b + 1))
                            pe.wait_ge(g_w, 2 * p + (TILES * c + b + 1 + FREE))
                            for i in range(HEADS):
                                last = nc.tensor.matmul(sums[i], h_tile[:, b, 0:H],
                                                        wadj[:, b if v == "plain" else 0, i, 0:w],
                                                        start=False, stop=False)
                            last.then_inc(g_mm, 1)
                    for out in sums:
                        last = close(out)
                    last.then_inc(g_sums, 1)

            with pe.If(signed > 0):
                sum_heads("signed")
            with pe.Else():
                sum_heads("plain")

            nc.tensor.nop().then_inc(by_pe, START)
            pe.wait_ge(g_kept, HEADS * NCH)
            pe.wait_ge(t_ready, 3)
            with pe.Fori(0, BLOCKS // 2) as gg:
                for b in parities:
                    here = bass.ds((2 * gg + b) * BLOCK, BLOCK)
                    at = Steps(pe, "pe", 2 * gg + b)
                    attention = gru_tmp[:, b, 0, :]

                    def both(out, gru, a, inp):
                        wih, whh = gru_w[gru]
                        nc.tensor.matmul(out[:, 0:BLOCK], wih[:, a * H:(a + 1) * H], inp, start=True, stop=False)
                        return nc.tensor.matmul(out[:, 0:BLOCK], whh[:, a * H:(a + 1) * H], h_t[:, here],
                                                start=False, stop=True)

                    def single(out, w, inp):
                        return nc.tensor.matmul(out[:, 0:BLOCK], w[:, 2 * H:3 * H], inp, start=True, stop=True)

                    at.after(by_act, "act", "edge gates", back=1)
                    both(bank[1], 0, 0, support[:, here])
                    at.step(both(bank[2], 0, 1, support[:, here]), by_pe, "edge gates")
                    at.after(by_dve, "dve", "node candidate", back=1)
                    for i in range(HEADS):
                        last = nc.tensor.matmul(bank[0][:, 0:BLOCK], gat_w_sb[:, i, :], heads[:, i, here],
                                                start=(i == 0), stop=(i == HEADS - 1))
                    at.step(last, by_pe, "heads")
                    single(bank[3], wih_e, support[:, here])
                    at.step(single(bank[4], whh_e, h_t[:, here]), by_pe, "edge candidate")
                    at.after(by_act, "act", "node gates", back=1)
                    at.after(by_act, "act", "attention")
                    both(bank[5], 1, 0, attention)
                    both(bank[6], 1, 1, attention)
                    single(bank[7], wih_n, attention)
                    at.step(single(bank[0], whh_n, h_t[:, here]), by_pe, "node")
                    at.end()

            pe.wait_ge(by_dve, signalled("dve", BLOCKS, 0))
            for q, tiles in GROUPS:
                for t in tiles:
                    last = nc.tensor.transpose(bank[q][:, (t - tiles[0]) * 128:(t - tiles[0] + 1) * 128],
                                               x_feat[:, t * 128:(t + 1) * 128], ident[:, :])
                last.then_inc(n_turned, 1)
            pe.wait_ge(n_normed, 1)
            for q, tiles in GROUPS:
                for t in tiles:
                    last = nc.tensor.transpose(bank[q][:, (t - tiles[0]) * 128:(t - tiles[0] + 1) * 128],
                                               x_nm[:, t, :], ident[:, :])
                last.then_inc(n_back, 1)
            for q, tiles in GROUPS:
                pe.wait_ge(n_input, q + 1)
                for t in tiles:
                    last = nc.tensor.matmul(bank[7][:, t * E:(t + 1) * E], xn[:, t * 128:(t + 1) * 128], wr_sb,
                                            start=True, stop=True)
            last.then_inc(l_psum, 1)
            pe.wait_ge(l_parts, 1)
            for q, tiles in GROUPS:
                for t in tiles:
                    last = nc.tensor.transpose(bank[q][0:GROWS, (t - tiles[0]) * 128:(t - tiles[0] + 1) * 128],
                                               gparts[:, t].rearrange("p q e -> p (q e)"), ident[:, :])
                last.then_inc(l_turned, 1)

            pe.wait_ge(l_rows, len(GROUPS))
            nc.tensor.nop().then_inc(m_used, FREE)
            with pe.Fori(0, BLOCKS // 2) as gg:
                for gb in parities:
                    here = bass.ds((2 * gg + gb) * BLOCK, BLOCK)
                    y = bank[6 + gb][:, 0:BLOCK]
                    pe.wait_ge(m_out, 2 * gg + (gb + 1))
                    nc.tensor.matmul(y, b2_sb[0:GROWS, :], gates_t[0:GROWS, here], start=True, stop=False)

                    def down(e):
                        pe.wait_ge(m_prod, 2 * E * gg + (E * gb + e + 1 + FREE))
                        for a in range(HALVES):
                            last = nc.tensor.matmul(y, w2_sb[:, e, a, :], prod_h[:, e % 2, a, :], start=False,
                                                    stop=False)
                        last.then_inc(m_used, 1)
                        return last

                    for e in range(E):
                        b, n = e % 2, E * gb + e
                        pe.wait_ge(m_prod, 2 * E * gg + (n + 1))
                        for a in range(HALVES):
                            last = nc.tensor.matmul(bank[2 * b + a][:, 0:BLOCK],
                                                    w1_sb[:, e, a * 128:(a + 1) * 128], xn[:, here],
                                                    start=True, stop=True)
                        last.then_inc(m_hid, 1)
                        nc.tensor.matmul(bank[4 + b][:, 0:BLOCK], pick_bf[0:GROWS, e, :], gates_bf[0:GROWS, here],
                                         start=True, stop=True).then_inc(m_gate, 1)
                        if e >= 1:
                            down(e - 1)
                    down(E - 1)
                    close(y).then_inc(m_y, 1)


def kernel(**inputs):
    import concourse.bacc as bacc
    from concourse.bass_utils import run_bass_kernel_spmd

    def arr(name):
        return np.ascontiguousarray(inputs[name])

    x, adj = arr("x"), arr("adj")
    x_pad = np.zeros((NP, H), x.dtype)
    x_pad[:N] = x
    rows = np.zeros((NP, NP), adj.dtype)
    rows[:N, :N] = adj
    ident, sum_parts, pick_score, pick_expert, iota = host_constants()
    data = [("x", x_pad), ("x_t", x_pad.T), ("adj_rows", rows), ("adj_cols", rows.T), ("diag", rows.diagonal()),
            ("ident", ident), ("sum_parts", sum_parts), ("pick_score", pick_score),
            ("pick_expert", pick_expert), ("iota", iota), ("gat_w", arr("L0_gnn_gat_W")),
            ("gat_w_t", arr("L0_gnn_gat_W").transpose(0, 2, 1)), ("gat_a", arr("L0_gnn_gat_a")),
            ("edge_wih_t", arr("L0_gnn_edge_Wih").T), ("edge_whh_t", arr("L0_gnn_edge_Whh").T),
            ("edge_bih", arr("L0_gnn_edge_bih")), ("edge_bhh", arr("L0_gnn_edge_bhh")),
            ("node_wih_t", arr("L0_gnn_node_Wih").T), ("node_whh_t", arr("L0_gnn_node_Whh").T),
            ("node_bih", arr("L0_gnn_node_bih")), ("node_bhh", arr("L0_gnn_node_bhh")),
            ("gamma", arr("L0_ffn_gamma")), ("beta", arr("L0_ffn_beta")), ("wr", arr("L0_ffn_Wr")),
            ("br", arr("L0_ffn_br")), ("w1", arr("L0_ffn_W1")), ("b1", arr("L0_ffn_b1")),
            ("w2", arr("L0_ffn_W2")), ("b2", arr("L0_ffn_b2"))]
    nc = bacc.Bacc("TRN2", target_bir_lowering=False, num_devices=1)
    arrays, args = {}, []
    for name, a in data:
        a = np.ascontiguousarray(a)
        arrays[f"{name}_dram"] = a
        args.append(nc.dram_tensor(f"{name}_dram", a.shape, mybir.dt.from_np(a.dtype),
                                   kind="ExternalInput").ap())
    out = nc.dram_tensor("out_dram", (H, NP), mybir.dt.float32, kind="ExternalOutput").ap()
    graph_layer_kernel(nc, *args, out)
    result = run_bass_kernel_spmd(nc, [arrays], core_ids=[0])
    return np.ascontiguousarray(result.results[0]["out_dram"][:, :N].T)
```

```python
from contextlib import ExitStack

import concourse.bass as bass
from concourse import mybir
import numpy as np

N = 3327
H = 128
HEADS = 3
TILES = -(-N // 128)
NP = TILES * 128
CHUNK = 512
CHUNKS = [(c, min(CHUNK, NP - c)) for c in range(0, NP, CHUNK)]
PARTS = ((0, 12), (12, TILES))
THIRDS = ((0, 8), (8, 16), (16, TILES))
SLOT = 8
ROWS = 3
SLOTS = 4
ALPHA = 0.2
NEG_INF = -9e15
LOWEST = -3e38
EPS = 1e-5
E = 8
HID = 256
HALVES = HID // 128
BLOCK = 416
BLOCKS = NP // BLOCK
SCORES = 2 * HEADS
STAT = 3
UW = 32
HE = H + SCORES + HEADS
GROWS = STAT * E
FREE = 2


def host_constants():
    ident = np.eye(128, dtype=np.float32)
    sum_parts = np.zeros((32, 32), np.float32)
    for q in range(STAT):
        for r in range(SCORES):
            sum_parts[1 + SCORES * q + r, r] = 1.0
    pick_score = np.zeros((32, SCORES, 128), np.float32)
    for r in range(SCORES):
        pick_score[r, r, :] = -1.0
    pick_expert = np.zeros((32, E, 128), np.float32)
    for q in range(STAT):
        for e in range(E):
            pick_expert[E * q + e, e, :] = 1.0
    iota = np.tile(np.arange(-E, 0, dtype=np.float32), (128, 1))
    return ident, sum_parts, pick_score, pick_expert, iota


class InOrder:

    def __init__(self, engine, semaphore):
        self.engine, self.semaphore, self.value = engine, semaphore, 0

    def done(self, instruction):
        instruction.then_inc(self.semaphore, 1)
        self.value = self.value + 1
        self.engine.wait_ge(self.semaphore, self.value)


GRU = {
    "pe": ["edge gates", "edge candidate", "heads", "node"],
    "act": ["edge gates", "attention", "node gates", "edge tanh", "node tanh"],
    "dve": ["edge candidate", "node candidate", "x"],
    "settled": 10,
}


START = 10


def signalled(who, g, steps, back=0):
    each = GRU[who] if who == "settled" else len(GRU[who])
    return g * each + (START + steps - back * each)


def apart(engine, waits):
    engine.sem_inc(waits, 1)


def tiles_by_four(engine, first, end, body):
    rounds = (end - first) // SLOTS
    with engine.Fori(0, rounds) as p:
        for k in range(SLOTS):
            body(SLOTS * p + (first + k), k)
    for t in range(first + rounds * SLOTS, end):
        body(t, t % SLOTS)


class Steps:

    def __init__(self, engine, who, g, own=None):
        self.engine, self.who, self.g, self.own = engine, who, g, own
        self.signals, self.chain = [], 0

    def after(self, semaphore, who, name, back=0):
        self.engine.wait_ge(semaphore, signalled(who, self.g, GRU[who].index(name) + 1, back))

    def step(self, instruction, semaphore, name):
        self.signals.append(name)
        instruction.then_inc(semaphore, 1)

    def settled(self, instruction):
        self.chain += 1
        instruction.then_inc(self.own, 1)
        self.engine.wait_ge(self.own, signalled("settled", self.g, self.chain))

    def end(self):
        assert self.signals == GRU[self.who], self.signals
        assert self.own is None or self.chain == GRU["settled"], self.chain


def graph_layer_kernel(nc, x, x_t, adj_rows, adj_cols, diag, ident_in, sum_parts_in, pick_score_in,
                       pick_expert_in, iota_in, gat_w, gat_w_t, gat_a, edge_wih_t, edge_whh_t, edge_bih,
                       edge_bhh, node_wih_t, node_whh_t, node_bih, node_bhh, gamma, beta, wr, br, w1, b1,
                       w2, b2, out_t, scores_dram, stats_dram):
    f32, bf16, i32 = mybir.dt.float32, mybir.dt.bfloat16, mybir.dt.int32
    ALU = mybir.AluOpType
    ACT = mybir.ActivationFunctionType
    AX = mybir.AxisListType
    ctx = ExitStack()
    with ctx:
        def sb(name, shape, dt=f32):
            return ctx.enter_context(nc.sbuf_tensor(name, shape, dt))

        def sem(name):
            return ctx.enter_context(nc.semaphore(name))

        psum = ctx.enter_context(nc.psum_tensor("psum", [128, 8 * 512], f32))
        bank = [psum[:, b * 512:(b + 1) * 512] for b in range(8)]

        h = sb("h", [128, TILES, HE])
        h_t = sb("h_t", [128, NP])
        support = sb("support", [128, NP])
        big = sb("big", [128, TILES * CHUNK])
        rowbuf = sb("rowbuf", [128, HEADS, NP])
        heads = sb("heads", [128, HEADS, NP])
        work = sb("work", [128, 12 * CHUNK])
        h_tile = sb("h_tile", [128, 2, H])
        u_tile = sb("u_tile", [128, SLOTS, 2 * UW], bf16)
        node_w = sb("node_w", [128, 2, 3 * H])
        u_parts = sb("u_parts", [128, TILES, 2 * UW], bf16)
        ident = sb("ident", [128, 128])
        off_diag = sb("off_diag", [128, 128])
        zero_bf = sb("zero_bf", [128, 512], bf16)
        bn = sb("bn", [128, TILES, 6])
        stats = sb("stats", [128, 6, TILES])
        neg_max = sb("neg_max", [128, HEADS, TILES])
        denom = sb("denom", [128, HEADS, TILES])
        inv_denom = sb("inv_denom", [128, HEADS, TILES])
        row_max = sb("row_max", [128, 3])
        table_out = sb("table_out", [128, 1])
        by_row = sb("by_row", [HEADS * TILES, 2, 128])
        sum_parts = sb("sum_parts", [32, 32])
        att_vec = sb("att_vec", [128, HEADS, 2])
        w_att = sb("w_att", [128, SCORES])
        row_min = sb("row_min", [128, 2, HEADS])
        minus_count = sb("minus_count", [1, len(CHUNKS)])
        flag_f = sb("flag_f", [1, 1])
        flag = sb("flag", [1, 1], i32)

        pick_score = node_w[0:32, :, :].rearrange("p k f -> p (k f)").rearrange("p (r c) -> p r c", r=SCORES)
        h_feat = h[:, :, 0:H]
        x_nodes = support[:, :].rearrange("p (t f) -> p t f", f=H)
        gat_wt_sb = heads[:, 1, 0:HEADS * H].rearrange("p (i f) -> p i f", i=HEADS)
        NU = TILES * SCORES
        u_all = heads[:, 2, 0:NU].rearrange("p (t i s) -> p t i s", i=HEADS, s=2)
        u_f32 = heads[:, 2, NU:2 * NU].rearrange("p (t i s) -> p t i s", i=HEADS, s=2)
        u_part = heads[:, 2, 2 * NU:3 * NU].bitcast(bf16)[:, 0:NU]\
            .rearrange("p (t i s) -> p t i s", i=HEADS, s=2)
        score_parts = heads[0:32, 0, :]
        scores = heads[0:32, 1, :]
        scaled = heads[0:32, 2, 0:2 * CHUNK].rearrange("p (b c) -> p b c", b=2)
        cols = big[:, :].rearrange("p (t c) -> p t c", t=TILES)
        masks = work[:, 0:SLOTS * CHUNK].bitcast(bf16).rearrange("p (b m c) -> p b m c", b=SLOTS, m=2)
        row = [support[:, :]] + [big[:, i * NP:(i + 1) * NP] for i in range(2)]
        masked = [big[:, (2 + i) * NP:(3 + i) * NP] for i in range(2)]
        edge_mask = row[1]
        masked_minus = work[:, 0:NP]
        RING = 2 * SLOT + 2
        ring = big[:, 0:RING * CHUNK].rearrange("p (t c) -> p t c", t=RING)
        ring_h = heads[:, :, :].rearrange("p i n -> p (i n)")[:, 0:RING * CHUNK]\
            .rearrange("p (t c) -> p t c", t=RING)
        wadj = big[:, RING * CHUNK:(RING + 2 * HEADS) * CHUNK].rearrange("p (b i c) -> p b i c", b=2, i=HEADS)
        wexp = work[:, :].rearrange("p (b i c) -> p b i c", b=SLOTS, i=HEADS)

        def carve(buffer, widths):
            views, at = [], 0
            for width in widths:
                views.append(buffer[:, at:at + width])
                at += width
            assert at <= buffer.shape[-1], (at, buffer.shape)
            return views

        (x_feat, xn, w1_f, w2_f) = carve(
            big[:, 0:RING * CHUNK + 2 * HEADS * CHUNK], [NP, NP, E * HID, E * HID])
        (wih_n, whh_n) = (node_w[:, k, :] for k in range(2))
        (wih_e, whh_e) = carve(big[:, (RING + 2 * HEADS) * CHUNK:], [3 * H] * 2)
        pick32 = xn[:, 0:E * 128].rearrange("p (e c) -> p e c", e=E)
        w1_sb = w1_f.rearrange("p (e f) -> p e f", e=E)
        w2_sb = w2_f.rearrange("p (e a d) -> p e a d", e=E, a=HALVES)
        gru_w = ((wih_e, whh_e), (wih_n, whh_n))
        (diag_bc, gates_t, gates_half, pick_f) = carve(
            rowbuf[:, :, :].rearrange("p i n -> p (i n)"), [NP, NP, NP // 2, E * 128 // 2])
        gates_bf = gates_half.bitcast(bf16)
        pick_bf = pick_f.bitcast(bf16).rearrange("p (e c) -> p e c", e=E)
        (gw_f, bias_in_f, bias_f, gamma_sb, beta_sb, wr_sb, br_bc, b1_f, b2_sb, iota) = carve(
            u_parts[:, :, :].rearrange("p t c -> p (t c)").bitcast(f32),
            [HEADS * H, 12, 6, 1, 1, E, E, E * HALVES, H, E])
        gat_w_sb = gw_f.rearrange("p (i f) -> p i f", i=HEADS)
        bias_in = bias_in_f.rearrange("p (g a) -> p g a", g=4)
        bias = bias_f.rearrange("p (g a) -> p g a", g=2)
        b1_sb = b1_f.rearrange("p (e a) -> p e a", e=E)
        gru_tmp = work[:, 0:2 * 7 * BLOCK].rearrange("p (b k n) -> p b k n", b=2, k=7)
        x_nm = heads[:, 2, :].rearrange("p (t f) -> p t f", f=H)
        RW = TILES * E
        (logit, rest, hot1, hot2, spare_f, gate, gbf_f, gparts_f, small_f) = carve(
            work[:, 0:4096], [RW] * 6 + [RW // 2, STAT * RW, 6 * TILES])
        logit, rest, hot1, hot2, picked, gate = (
            v.rearrange("p (t e) -> p t e", e=E) for v in (logit, rest, hot1, hot2, spare_f, gate))
        gbf = gbf_f.bitcast(bf16).rearrange("p (t e) -> p t e", e=E)
        gparts = gparts_f.rearrange("p (t q e) -> p t q e", q=STAT, e=E)
        first, second, where, gap, w_first, w_second = (small_f[:, k * TILES:(k + 1) * TILES] for k in range(6))
        act_f = work[:, 4096:4096 + 4 * BLOCK]
        act_h = act_f.rearrange("p (b a n) -> p b a n", b=2, a=HALVES)
        prod_h = heads[:, 0, 0:4 * BLOCK].rearrange("p (b a n) -> p b a n", b=2, a=HALVES)
        y_sb = heads[:, 1, 0:2 * BLOCK].rearrange("p (b n) -> p b n", b=2)

        x_in = [sem("x_in0"), sem("x_in1")]
        small_in, gatw_in, consts = sem("small_in"), sem("gatw_in"), sem("consts")
        dve_order, pool_order = sem("dve_order"), sem("pool_order")
        h_ready, ht_psum, ht_ready = sem("h_ready"), sem("ht_psum"), sem("ht_ready")
        var_ready, root_ready = sem("var_ready"), sem("root_ready")
        v_psum, v_ready, u_clear, u_psum, u_ready = (sem(n) for n in (
            "v_psum", "v_ready", "u_clear", "u_psum", "u_ready"))
        a_in = [sem("a_in0"), sem("a_in1")]
        a_clear, a_tile, a_mask, a_used, a_kept = (sem(f"a_{n}") for n in (
            "clear", "tile", "mask", "used", "kept"))
        s_psum, s_scaled, s_ready, s_stored = sem("s_psum"), sem("s_scaled"), sem("s_ready"), sem("s_stored")
        b_psum, b_ready, c_psum, c_ready, f_ready = (sem("b_psum"), sem("b_ready"), sem("c_psum"),
                                                     sem("c_ready"), sem("f_ready"))
        PATHS = ("plain", "signed")
        r_in = [sem(f"r_in{i}") for i in range(ROWS)]
        r_in_signed, r_free_signed = sem("r_in_signed"), sem("r_free_signed")
        r_max, r_exp, r_order = ({v: sem(f"{n}_{v}") for v in PATHS} for n in ("r_max", "r_exp", "r_order"))
        q_ready = sem("q_ready")
        h_in = [sem(f"h_in{i}") for i in range(3)]
        h_clear, h_copied, h_used, h_sums, h_kept = (sem(f"h_{n}") for n in (
            "clear", "copied", "used", "sums", "kept"))
        rows_done = sem("rows_done")
        k_ready, k_psum, k_rows, k_stored = (sem(f"k_{n}") for n in ("ready", "psum", "rows", "stored"))
        k_in = [sem("k_in0"), sem("k_in1")]
        d_stored, d_in = sem("d_stored"), sem("d_in")
        g_in = [sem(f"g_in{i}") for i in range(3)]
        g_y, g_e, g_w, g_mm, g_kept = (sem(f"g_{n}") for n in ("y", "e", "w", "mm", "kept"))
        g_clear, g_relu, g_order_dve, g_tile = (sem(f"g_{n}") for n in ("clear", "relu", "order_dve", "tile"))
        early_in, pick_in, pick_ready, late_in, t_ready = (sem(n) for n in (
            "early_in", "pick_in", "pick_ready", "late_in", "t_ready"))
        biases_in = sem("biases_in")
        dense_in = sem("dense_in")
        by_pe, by_act, by_dve, dense_order = sem("by_pe"), sem("by_act"), sem("by_dve"), sem("dense_order")
        n_turned, n_normed, n_back, n_input = (sem(f"n_{n}") for n in ("turned", "normed", "back", "input"))
        l_psum, l_gap, l_weights, l_parts, l_turned, l_gates, l_rows = (
            sem(f"l_{n}") for n in ("psum", "gap", "weights", "parts", "turned", "gates", "rows"))
        m_hid, m_gate, m_act, m_prod, m_used, m_out = (
            sem(f"m_{n}") for n in ("hid", "gate", "act", "prod", "used", "out"))
        m_stored = [sem("m_stored0"), sem("m_stored1")]

        dve_waits, pool_waits = sem("dve_waits"), sem("pool_waits")

        NCH = len(CHUNKS)
        EARLY_LOADS = 12
        parities = range(2)
        GROUPS = [(q, range(4 * q, min(4 * q + 4, TILES))) for q in range(-(-TILES // 4))]

        def stretches(c):
            for third, (t0, t1) in enumerate(THIRDS):
                yield t0, t0 + SLOT, (3 * c + third) % 2 * SLOT
            yield THIRDS[2][0] + SLOT, TILES, 2 * SLOT

        block = ctx.enter_context(nc.Block())

        @block.sync
        def _(sp):
            for k, (t0, t1) in enumerate(((0, 8), (8, TILES))):
                sp.dma_start(x_nodes[:, t0:t1, :], x[t0 * 128:t1 * 128, :].rearrange("(t p) f -> p t f", p=128))\
                    .then_inc(x_in[k], 16)
            for dst, src in ((ident[:, :], ident_in), (sum_parts[:, :], sum_parts_in),
                             (pick_score[:, :, :], pick_score_in)):
                sp.dma_start(dst, src).then_inc(small_in, 16)
            sp.dma_start(gat_wt_sb, gat_w_t.rearrange("i p f -> p i f")).then_inc(gatw_in, 16)
            for i in range(HEADS):
                sp.dma_start(att_vec[:, i, :], gat_a[i].rearrange("(s p) o -> p (s o)", p=128),
                             allow_slow_non_contiguous=True).then_inc(gatw_in, 16)

            for c, (c0, w) in enumerate(CHUNKS):
                for part, (t0, t1) in enumerate(PARTS):
                    if c > 0:
                        sp.wait_ge(a_used, TILES * (c - 1) + t1 + SLOTS)
                    src = adj_cols[t0 * 128:t1 * 128, c0:c0 + w].rearrange("(t p) c -> p t c", p=128)
                    sp.dma_start(cols[:, t0:t1, 0:w], src).then_inc(a_in[part], 16)

            def load_third(c, third, to, used, credit, loaded):
                c0, w = CHUNKS[c]
                t0, t1 = THIRDS[third]
                n = 3 * c + third
                if n >= 2:
                    sp.wait_ge(used, TILES * ((n - 2) // 3) + THIRDS[(n - 2) % 3][1] + credit)
                for a, b, at in ((t0, t0 + SLOT, n % 2 * SLOT), (t0 + SLOT, t1, 2 * SLOT)):
                    if a < b:
                        sp.dma_start(to[:, at:at + b - a, 0:w], adj_cols[a * 128:b * 128, c0:c0 + w]
                                     .rearrange("(t p) c -> p t c", p=128)).then_inc(loaded[third], 16)

            sp.wait_ge(h_ready, len(GROUPS))
            sp.dma_start(row[0], adj_rows[0:128, :]).then_inc(r_in[0], 16)
            sp.wait_ge(a_used, TILES * NCH + SLOTS)
            for t in range(1, ROWS):
                sp.dma_start(row[t], adj_rows[t * 128:(t + 1) * 128, :]).then_inc(r_in[t], 16)
            sp.wait_ge(f_ready, 1)
            signed = sp.value_load(flag[0:1, 0:1])
            sp.wait_ge(c_psum, NCH)
            sp.wait_ge(b_ready, HEADS * NCH)
            with sp.If(signed > 0):
                sp.wait_ge(s_ready, NCH)
                sp.dma_start(scores_dram, scores[0:SCORES, :]).then_inc(s_stored, 16)
                sp.wait_ge(s_stored, 16)
                for c in range(NCH):
                    for third in range(3):
                        load_third(c, third, ring_h, h_used, FREE, h_in)
                for t in range(ROWS):
                    sp.wait_ge(r_in[t], 16)
                for head in range(HEADS):
                    if head > 0:
                        sp.wait_ge(r_max["signed"], TILES * head)
                    for s in parities:
                        sp.dma_start(rowbuf[:, s, :], scores_dram[HEADS * s + head].partition_broadcast(128))\
                            .then_inc(q_ready, 16)
                    with sp.Fori(0, TILES) as t:
                        sp.wait_ge(r_free_signed, TILES * head + t + 1)
                        sp.dma_start(row[0], adj_rows[bass.ds(t * 128, 128), :]).then_inc(r_in_signed, 16)
            with sp.Else():
                for t in range(TILES):
                    if t >= ROWS:
                        sp.wait_ge(r_max["plain"], HEADS * (t + 1))
                        sp.dma_start(row[t % ROWS], adj_rows[t * 128:(t + 1) * 128, :])\
                            .then_inc(r_in[t % ROWS], 16)
                    if t % 4 < 3:
                        load_third(t // 4, t % 4, ring_h, h_used, FREE, h_in)
                load_third(NCH - 1, 2, ring_h, h_used, FREE, h_in)
            early = (
                (gat_w_sb, gat_w.rearrange("i p f -> p i f")), (wr_sb, wr), (br_bc, br.partition_broadcast(128)),
                (gamma_sb, gamma.rearrange("(p a) -> p a", a=1)), (beta_sb, beta.rearrange("(p a) -> p a", a=1)),
                (b1_sb, b1.rearrange("e (a p) -> p e a", p=128)), (iota, iota_in),
                (wih_n, node_wih_t), (whh_n, node_whh_t),
                (b2_sb[0:E, :], b2), (b2_sb[E:2 * E, :], b2), (b2_sb[2 * E:3 * E, :], b2))
            assert len(early) == EARLY_LOADS
            for k, src in enumerate((edge_bih, edge_bhh, node_bih, node_bhh)):
                sp.dma_start(bias_in[:, k, :], src.rearrange("(a p) -> p a", p=128),
                             allow_slow_non_contiguous=True).then_inc(biases_in, 16)
            for dst, src in early:
                sp.dma_start(dst, src, allow_slow_non_contiguous=True).then_inc(early_in, 16)
            sp.wait_ge(rows_done, 1)

            def to_all(k, i0, out, first, end):
                return sp.dma_start(out[:, :, first:end],
                                    stats_dram[i0:i0 + HEADS, first:end].partition_broadcast(128)).then_inc(k, 16)

            sp.wait_ge(k_rows, 1)
            sp.dma_start(stats_dram[0:HEADS, :].rearrange("i (t p) -> (i t) p", p=128), by_row[:, 0, :])\
                .then_inc(k_stored, 16)
            for c, (c0, w) in enumerate(CHUNKS):
                for third, (t0, t1) in enumerate(THIRDS):
                    n = 3 * c + third
                    if n == 1:
                        sp.wait_ge(k_stored, 16)
                        to_all(k_in[0], 0, rowbuf, 0, CHUNK)
                        sp.wait_ge(k_rows, 2)
                        sp.dma_start(stats_dram[HEADS:2 * HEADS, :].rearrange("i (t p) -> (i t) p", p=128),
                                     by_row[:, 1, :]).then_inc(d_stored, 16)
                    if n == 3:
                        to_all(k_in[1], 0, rowbuf, CHUNK, NP)
                        sp.wait_ge(d_stored, 16)
                        sp.wait_ge(h_sums, 1)
                        to_all(d_in, HEADS, heads, 0, NP)
                        sp.dma_start(wih_e, edge_wih_t).then_inc(early_in, 16)
                        sp.dma_start(whh_e, edge_whh_t).then_inc(early_in, 16)
                    load_third(c, third, ring, g_w, SLOTS, g_in)
            sp.wait_ge(g_w, TILES * NCH + SLOTS)
            for dst, src in ((x_feat, x_t), (diag_bc, diag.partition_broadcast(128))):
                sp.dma_start(dst, src).then_inc(late_in, 16)
            sp.wait_ge(g_mm, TILES * NCH + FREE)
            sp.dma_start(pick32[0:32, :, :], pick_expert_in).then_inc(pick_in, 16)
            sp.dma_start(w1_sb, w1.rearrange("e d f -> d e f")).then_inc(dense_in, 16)
            sp.dma_start(w2_sb, w2.rearrange("e (a p) d -> p e a d", p=128)).then_inc(dense_in, 16)
            with sp.Fori(0, BLOCKS // 2) as g:
                for b in parities:
                    sp.wait_ge(m_out, 2 * g + b + 1 + FREE)
                    sp.dma_start(out_t[:, bass.ds((2 * g + b) * BLOCK, BLOCK)], y_sb[:, b, :])\
                        .then_inc(m_stored[b], 16)
            for b in parities:
                sp.wait_ge(m_stored[b], 16 * (BLOCKS // 2 + 1))

        @block.gpsimd
        def _(pool):
            order = InOrder(pool, pool_order)
            nc.gpsimd.memset(zero_bf[:, :], 0.0).then_inc(consts, 1)
            order.done(nc.gpsimd.memset(off_diag[:, :], 1.0))
            nc.gpsimd.affine_select(out=off_diag[:, :], in_=off_diag[:, :], compare_op=ALU.not_equal,
                                    fill=0.0, base=0, pattern=[[-1, 128]], channel_multiplier=1)\
                .then_inc(consts, 1)

            def clear_diagonal(c, t, tile):
                c0, w = CHUNKS[c]
                if c0 <= t * 128 < c0 + w:
                    crossed = tile[:, t * 128 - c0:t * 128 - c0 + 128]
                    order.done(nc.gpsimd.affine_select(
                        out=crossed, in_=crossed, compare_op=ALU.not_equal, fill=0.0, base=0,
                        pattern=[[-1, 128]], channel_multiplier=1))

            pool.wait_ge(u_ready, 1)
            for c, (c0, w) in enumerate(CHUNKS):
                for part, (t0, t1) in enumerate(PARTS):
                    pool.wait_ge(a_in[part], 16 * (c + 1))
                    for t in range(t0, t1):
                        clear_diagonal(c, t, cols[:, t, :])
                    nc.gpsimd.nop().then_inc(a_clear, 1)

                    def copy_vectors(t, k):
                        n = TILES * c
                        pool.wait_ge(a_used, t + (n + 1))
                        nc.gpsimd.tensor_copy(u_tile[:, (n + k) % SLOTS, :],
                                              u_parts[:, bass.ds(t, 1), :].squeeze(1)).then_inc(a_tile, 1)

                    tiles_by_four(pool, t0, t1, copy_vectors)

            def feed(to, loaded, cleared, used, copied):
                for c in range(NCH):
                    for third, (t0, t1) in enumerate(THIRDS):
                        at = (3 * c + third) % 2 * SLOT
                        pool.wait_ge(loaded[third], (32 if third == 2 else 16) * (c + 1))
                        for t in range(t0, t1):
                            clear_diagonal(c, t, to[:, at + t - t0 if t < t0 + SLOT else SLOT + t - t0, :])
                        nc.gpsimd.nop().then_inc(cleared, 1)
                        with pool.Fori(0, (t1 - t0) // 2) as p:
                            for b in parities:
                                t = 2 * p + (t0 + b)
                                pool.wait_ge(used, TILES * c + 1 + t)
                                nc.gpsimd.tensor_copy(h_tile[:, b, 0:H], h[:, bass.ds(t, 1), 0:H].squeeze(1))\
                                    .then_inc(copied, 1)

            pool.wait_ge(h_ready, len(GROUPS))
            feed(ring_h, h_in, h_clear, h_used, h_copied)
            pool.wait_ge(h_used, TILES * NCH + FREE)
            feed(ring, g_in, g_clear, g_mm, g_tile)
            pool.wait_ge(pick_in, 16)
            nc.gpsimd.tensor_copy(pick_bf[0:32, :, :], pick32[0:32, :, :]).then_inc(pick_ready, 1)

        @block.scalar
        def _(act):
            def root(k):
                act.wait_ge(var_ready, k + 1)
                nc.scalar.activation(stats[:, 1, :], stats[:, 0, :], ACT.Sqrt).then_inc(root_ready, 1)

            def load_table(function):
                nc.scalar.activation(table_out[:, :], zero_bf[:, 0:1], function)

            root(0)
            for q in range(-(-TILES // 4)):
                n = min(4, TILES - 4 * q) * 128
                act.wait_ge(ht_psum, q + 1)
                nc.scalar.activation(h_t[:, q * 512:q * 512 + n], bank[q % 2][:, 0:n], ACT.Copy)\
                    .then_inc(ht_ready, 1)
            for c in range(NCH + 1):
                if c < NCH:
                    c0, w = CHUNKS[c]
                    act.wait_ge(a_used, TILES * (c + 1) + SLOTS)
                    nc.scalar.activation(score_parts[:, c0:c0 + w], bank[c % 2][0:32, 0:w], ACT.Copy)\
                        .then_inc(a_kept, 1)
                    act.wait_ge(s_psum, c + 1)
                    if c >= 2:
                        act.wait_ge(s_ready, c - 1)
                    nc.scalar.activation(scaled[:, c % 2, 0:w], bank[2 + c % 2][0:32, 0:w], ACT.Copy,
                                         scale=ALPHA).then_inc(s_scaled, 1)
                if c >= 1:
                    c0, w = CHUNKS[c - 1]
                    for i in range(HEADS):
                        q = HEADS * (c - 1) + i
                        act.wait_ge(b_psum, q + 1)
                        nc.scalar.activation(rowbuf[:, i, c0:c0 + w], bank[4 + q % 2][:, 0:w], ACT.Copy)\
                            .then_inc(b_ready, 1)
            act.wait_ge(consts, 2)
            act.wait_ge(f_ready, 1)
            signed = act.value_load(flag[0:1, 0:1])

            def denominators_plain():
                nc.scalar.nop().then_inc(r_exp["plain"], HEADS + 1)
                load_table(ACT.Exp)
                with act.Fori(0, TILES // 2) as p:
                    for b in parities:
                        for i in range(HEADS):
                            k, n = (HEADS * b + i) % 2, HEADS * b + i
                            act.wait_ge(r_max["plain"], 2 * HEADS * p + (ROWS * HEADS + n + 1))
                            nc.scalar.activation(masked[k], masked[k], ACT.Exp, bias=row_min[:, b, i:i + 1],
                                                 scale=-1.0, accum_out=denom[:, i, bass.ds(2 * p + b, 1)])\
                                .then_inc(r_exp["plain"], 1)
                        nc.scalar.activation(neg_max[:, :, bass.ds(2 * p + b, 1)].squeeze(2), row_min[:, b, :],
                                             ACT.Copy).then_inc(r_exp["plain"], 1)
                act.wait_ge(r_exp["plain"], (HEADS + 1) * (TILES + 1))

            def denominators_signed():
                nc.scalar.nop().then_inc(r_exp["signed"], FREE)
                for head in range(HEADS):
                    with act.Fori(0, TILES // 2) as p:
                        for b in parities:
                            act.wait_ge(r_max["signed"], 2 * p + (TILES * head + b + 1))
                            nc.scalar.activation(masked[b], masked[b], ACT.Exp,
                                                 bias=neg_max[:, head, bass.ds(2 * p + b, 1)],
                                                 accum_out=denom[:, head, bass.ds(2 * p + b, 1)])\
                                .then_inc(r_exp["signed"], 1)
                act.wait_ge(r_exp["signed"], HEADS * TILES + FREE)

            with act.If(signed > 0):
                denominators_signed()
            with act.Else():
                denominators_plain()
            nc.scalar.nop().then_inc(rows_done, 1)
            act.wait_ge(k_psum, 1)
            nc.scalar.activation(by_row[:, 0, :], bank[7][0:HEADS * TILES, 0:128], ACT.Copy, scale=-1.0)\
                .then_inc(k_rows, 1)
            act.wait_ge(h_sums, 1)
            for q in range(NCH):
                c0, w = CHUNKS[q]
                nc.scalar.activation(support[:, c0:c0 + w], bank[q][:, 0:w], ACT.Copy).then_inc(h_kept, 1)
            act.wait_ge(k_psum, 2)
            nc.scalar.activation(by_row[:, 1, :], bank[7][0:HEADS * TILES, 128:256], ACT.Copy).then_inc(k_rows, 1)

            LAST = HEADS - 1

            def exponentials(v):
                for c, (c0, w) in enumerate(CHUNKS):
                    if v == "signed":
                        with act.Fori(0, TILES) as t:
                            act.wait_ge(g_y, t + (TILES * c + 1))
                            place = wexp[:, 0:2, :, 0:w].rearrange("p b i c -> p (b i) c")
                            nc.scalar.activation(place, place, ACT.Exp, scale=-1.0).then_inc(g_e, 1)
                        continue

                    def tile(t, k):
                        n = TILES * c
                        slot = (n + k) % SLOTS
                        place = wexp[:, slot, LAST, 0:w]
                        act.wait_ge(g_w, t + (n + 1))
                        nc.scalar.activation(place, rowbuf[:, LAST, c0:c0 + w], ACT.Relu,
                                             bias=h[:, bass.ds(t, 1), H + SCORES + LAST]).then_inc(g_relu, 1)
                        act.wait_ge(g_y, t + (n + 1))
                        both = wexp[:, slot, 0:LAST, 0:w]
                        nc.scalar.activation(both, both, ACT.Exp, scale=-1.0)
                        act.wait_ge(g_relu, t + (n + 1))
                        nc.scalar.activation(place, place, ACT.Exp, scale=-1.0).then_inc(g_e, 1)

                    if c < 2:
                        act.wait_ge(k_in[c], 16)
                    tiles_by_four(act, 0, TILES, tile)

            with act.If(signed > 0):
                exponentials("signed")
            with act.Else():
                exponentials("plain")

            load_table(ACT.Sigmoid)
            act.wait_ge(t_ready, 2)
            nc.scalar.nop().then_inc(by_act, START)
            with act.Fori(0, BLOCKS // 2) as gg:
                for b in parities:
                    at = Steps(act, "act", 2 * gg + b)
                    att, e_r, e_z, _, n_r, n_z, _ = (gru_tmp[:, b, k, :] for k in range(7))
                    at.after(by_dve, "dve", "x", back=2)
                    at.after(by_pe, "pe", "edge gates")
                    nc.scalar.activation(e_r, bank[6][:, 0:BLOCK], ACT.Sigmoid, bias=bias[:, 0, 0:1])
                    at.step(nc.scalar.activation(e_z, bank[3][:, 0:BLOCK], ACT.Sigmoid, bias=bias[:, 0, 1:2]),
                            by_act, "edge gates")
                    at.after(by_pe, "pe", "heads")
                    at.step(nc.scalar.activation(att, bank[7][:, 0:BLOCK], ACT.Copy), by_act, "attention")
                    at.after(by_pe, "pe", "node")
                    nc.scalar.activation(n_r, bank[1][:, 0:BLOCK], ACT.Sigmoid, bias=bias[:, 1, 0:1])
                    at.step(nc.scalar.activation(n_z, bank[2][:, 0:BLOCK], ACT.Sigmoid, bias=bias[:, 1, 1:2]),
                            by_act, "node gates")
                    at.after(by_dve, "dve", "edge candidate")
                    at.step(nc.scalar.activation(e_r, e_r, ACT.Tanh), by_act, "edge tanh")
                    at.after(by_dve, "dve", "node candidate")
                    at.step(nc.scalar.activation(n_r, n_r, ACT.Tanh), by_act, "node tanh")
                    at.end()

            root(1)
            root(2)
            act.wait_ge(pick_ready, 1)
            for q, tiles in GROUPS:
                w = len(tiles) * 128
                act.wait_ge(n_back, q + 1)
                nc.scalar.activation(xn[:, q * 512:q * 512 + w], bank[q][:, 0:w], ACT.Identity, bias=beta_sb,
                                     scale=gamma_sb).then_inc(n_input, 1)
            act.wait_ge(l_gap, 1)
            nc.scalar.activation(w_first, gap, ACT.Sigmoid)
            nc.scalar.activation(w_second, gap, ACT.Sigmoid, scale=-1.0).then_inc(l_weights, 1)
            load_table(ACT.Gelu)
            for q, tiles in GROUPS:
                w = len(tiles) * 128
                act.wait_ge(l_turned, q + 1)
                nc.scalar.activation(gates_bf[0:GROWS, q * 512:q * 512 + w], bank[q][0:GROWS, 0:w], ACT.Copy)\
                    .then_inc(l_gates, 1)

            with act.Fori(0, BLOCKS) as g:
                for e in range(E):
                    b = e % 2
                    act.wait_ge(m_hid, g * E + (e + 1))
                    act.wait_ge(m_prod, g * E + (e + 1))
                    for a in range(HALVES):
                        last = nc.scalar.activation(act_h[:, b, a, :], bank[2 * b + a][:, 0:BLOCK], ACT.Gelu,
                                                    bias=b1_sb[:, e, a:a + 1])
                    last.then_inc(m_act, 1)

        @block.vector
        def _(dve):
            order = InOrder(dve, dve_order)

            roots = []

            def normalise(source, out, done, wait_for, twice=False):
                for q, tiles in GROUPS:
                    wait_for(q)
                    for t in tiles:
                        last = nc.vector.bn_stats(bn[:, t, :], source(t))
                order.done(last)
                mean, inv, value, spare, variance, again = (stats[:, k, :] for k in (2, 1, 0, 3, 4, 5))
                nc.vector.tensor_tensor(mean, bn[:, :, 1], bn[:, :, 4], ALU.add)
                order.done(nc.vector.tensor_tensor(variance, bn[:, :, 2], bn[:, :, 5], ALU.add))
                nc.vector.tensor_tensor(spare, bn[:, :, 1], bn[:, :, 4], ALU.subtract)
                order.done(nc.vector.tensor_scalar(variance, variance, 1.0 / H, None, ALU.mult))
                order.done(nc.vector.tensor_tensor(spare, spare, spare, ALU.mult))
                nc.vector.tensor_scalar(mean, mean, 0.5, None, ALU.mult)
                order.done(nc.vector.scalar_tensor_tensor(out=variance, in0=spare, scalar=0.25, in1=variance,
                                                          op0=ALU.mult, op1=ALU.add))

                def inverse_root():
                    nc.vector.tensor_scalar(value, variance, EPS, None, ALU.add).then_inc(var_ready, 1)
                    roots.append(1)
                    dve.wait_ge(root_ready, len(roots))
                    order.done(nc.vector.reciprocal(inv, inv))
                    order.done(nc.vector.tensor_tensor(spare, inv, inv, ALU.mult))
                    order.done(nc.vector.tensor_tensor(spare, spare, value, ALU.mult))
                    order.done(nc.vector.tensor_scalar(spare, spare, -0.5, 1.5, ALU.mult, ALU.add))
                    order.done(nc.vector.tensor_tensor(inv, inv, spare, ALU.mult))

                inverse_root()
                if twice:
                    order.done(nc.vector.tensor_tensor(variance, variance, inv, ALU.mult))
                    nc.vector.tensor_copy(again, inv)
                    order.done(nc.vector.tensor_tensor(variance, variance, inv, ALU.mult))
                    inverse_root()
                    order.done(nc.vector.tensor_tensor(inv, inv, again, ALU.mult))
                for q, tiles in GROUPS:
                    for t in tiles:
                        last = nc.vector.tensor_scalar(out[:, t, :], source(t), mean[:, t:t + 1], inv[:, t:t + 1],
                                                       ALU.subtract, ALU.mult)
                    last.then_inc(done, 1)

            nc.vector.memset(u_parts[:, :, :], 0.0).then_inc(u_clear, 1)
            normalise(lambda t: x_nodes[:, t, :], h_feat, h_ready, lambda q: dve.wait_ge(x_in[q >= 2], 16))
            dve.wait_ge(v_psum, 1)
            nc.vector.tensor_copy(w_att[:, :], bank[2][:, 0:SCORES]).then_inc(v_ready, 1)
            dve.wait_ge(u_clear, 1)
            order.done(nc.vector.memset(u_parts[:, :, UW:UW + 1], 1.0))
            dve.wait_ge(u_psum, 1)
            order.done(nc.vector.tensor_copy(heads[:, 2, 0:NU], bank[3][:, 0:NU]))
            for q in range(STAT):
                order.done(nc.vector.tensor_copy(u_part, u_all))
                for s in range(2):
                    for m in range(2):
                        at = UW * m + 1 + SCORES * q + HEADS * s
                        nc.vector.tensor_copy(u_parts[:, :, at:at + HEADS], u_part[:, :, :, s ^ m])
                order.done(nc.vector.tensor_copy(u_f32, u_part))
                if q < STAT - 1:
                    order.done(nc.vector.tensor_tensor(u_all, u_all, u_f32, ALU.subtract))
            nc.vector.nop().then_inc(u_ready, 1)

            for c in range(NCH + 1):
                if c < NCH:
                    w = CHUNKS[c][1]

                    def make_masks(t, k):
                        n = TILES * c
                        place = (n + k) % SLOTS
                        dve.wait_ge(a_used, t + (n + 1))
                        tile = cols[:, bass.ds(t, 1), 0:w].squeeze(1)
                        nc.vector.tensor_scalar(masks[:, place, 0, 0:w], tile, 0.0, None, ALU.is_gt)
                        nc.vector.tensor_scalar(masks[:, place, 1, 0:w], tile, 0.0, None, ALU.is_lt)\
                            .then_inc(a_mask, 1)

                    for part, (t0, t1) in enumerate(PARTS):
                        dve.wait_ge(a_clear, 2 * c + part + 1)
                        tiles_by_four(dve, t0, t1, make_masks)
                if c >= 1:
                    c0, w = CHUNKS[c - 1]
                    dve.wait_ge(s_scaled, c)
                    nc.vector.tensor_tensor(scores[:, c0:c0 + w], scaled[:, (c - 1) % 2, 0:w],
                                            bank[2 + (c - 1) % 2][0:32, 0:w], ALU.max).then_inc(s_ready, 1)
                    order.done(nc.vector.tensor_reduce(minus_count[:, c - 1:c], score_parts[0:1, c0:c0 + w], AX.X,
                                                       ALU.max))
            order.done(nc.vector.tensor_reduce(flag_f[:, :], minus_count[:, :], AX.X, ALU.max))
            nc.vector.tensor_copy(flag[:, :], flag_f[:, :]).then_inc(f_ready, 1)
            dve.wait_ge(f_ready, 1)
            signed = dve.value_load(flag[0:1, 0:1])

            def scores_by_node():
                dve.wait_ge(c_psum, NCH)
                by_node = bank[6][:, 0:NU].rearrange("p (t r) -> p t r", r=SCORES)
                nc.vector.tensor_copy(h[:, :, H:H + SCORES], by_node)
                nc.vector.tensor_scalar(h[:, :, H + SCORES:HE], by_node[:, :, 0:HEADS], -1.0, None, ALU.mult)\
                    .then_inc(c_ready, 1)

            def maxima_plain():
                step = r_order["plain"]
                nc.vector.nop().then_inc(r_max["plain"], ROWS * HEADS)
                EACH = 6

                def clear_row(p, j):
                    b, turn = j % ROWS, j // ROWS
                    dve.wait_ge(r_in[b], 32 * p + 16 * (turn + 1))
                    crossed = row[b][:, bass.ds((EACH * p + j) * 128, 128)]
                    nc.vector.tensor_tensor(crossed, crossed, off_diag[:, :], ALU.mult).then_inc(step, 1)

                def mask_row(p, j):
                    b = j % ROWS
                    dve.wait_ge(step, 2 * EACH * p + (2 * j + 1))
                    nc.vector.tensor_scalar(row[b], row[b], 0.0, -NEG_INF, ALU.is_le, ALU.mult).then_inc(step, 1)

                def take(p, j, last=False):
                    ahead = (p, j + 1) if j < EACH - 1 else (p + 1, 0)
                    dve.wait_ge(step, 2 * EACH * p + (2 * j + 2))
                    for i in range(HEADS):
                        dve.wait_ge(r_exp["plain"], (HEADS + 1) * EACH * p + ((HEADS + 1) * j + (2, 3, 5)[i]))
                        apart(dve, dve_waits)
                        nc.vector.tensor_tensor_reduce(
                            out=masked[(HEADS * j + i) % 2], in0=row[j % ROWS], in1=rowbuf[:, i, :], scale=1.0,
                            scalar=-LOWEST, op0=ALU.add, op1=ALU.min, accum_out=row_min[:, j % 2, i:i + 1])\
                            .then_inc(r_max["plain"], 1)
                        if not last and i < 2:
                            (clear_row, mask_row)[i](*ahead)

                clear_row(0, 0)
                mask_row(0, 0)
                scores_by_node()
                dve.wait_ge(b_ready, HEADS * NCH)
                with dve.Fori(0, TILES // EACH) as p:
                    for j in range(EACH):
                        take(p, j)
                for j in range(TILES % EACH):
                    take(TILES // EACH, j, last=j == TILES % EACH - 1)

            def maxima_signed():
                scores_by_node()
                step = r_order["signed"]
                nc.vector.nop().then_inc(r_free_signed, 1)
                EACH = 7
                for head in range(HEADS):
                    dve.wait_ge(q_ready, 32 * (head + 1))
                    with dve.Fori(0, TILES // 2) as p:
                        for b in parities:
                            n = TILES * head + b
                            at = EACH * n
                            dve.wait_ge(r_in_signed, 32 * p + 16 * (n + 1))
                            crossed = row[0][:, bass.ds((2 * p + b) * 128, 128)]
                            nc.vector.tensor_tensor(crossed, crossed, off_diag[:, :], ALU.mult).then_inc(step, 1)
                            dve.wait_ge(step, 2 * EACH * p + (at + 1))
                            nc.vector.tensor_scalar(edge_mask, row[0], 0.0, NEG_INF, ALU.is_le, ALU.mult)\
                                .then_inc(step, 1)
                            dve.wait_ge(step, 2 * EACH * p + (at + 2))
                            dve.wait_ge(r_exp["signed"], 2 * p + (n + 1))
                            apart(dve, dve_waits)
                            nc.vector.tensor_tensor_reduce(
                                out=masked[b], in0=edge_mask, in1=rowbuf[:, 0, :], scale=1.0, scalar=LOWEST,
                                op0=ALU.add, op1=ALU.max, accum_out=row_max[:, 0:1]).then_inc(step, 1)
                            dve.wait_ge(step, 2 * EACH * p + (at + 3))
                            nc.vector.tensor_scalar(edge_mask, row[0], 0.0, NEG_INF, ALU.is_ge, ALU.mult)\
                                .then_inc(step, 1)
                            dve.wait_ge(step, 2 * EACH * p + (at + 4))
                            apart(dve, dve_waits)
                            nc.vector.tensor_tensor_reduce(
                                out=masked_minus, in0=edge_mask, in1=rowbuf[:, 1, :], scale=1.0, scalar=LOWEST,
                                op0=ALU.add, op1=ALU.max, accum_out=row_max[:, 1:2]).then_inc(step, 1)
                            dve.wait_ge(step, 2 * EACH * p + (at + 5))
                            nc.vector.tensor_tensor(masked[b], masked[b], masked_minus, ALU.max)\
                                .then_inc(step, 1)
                            nc.vector.tensor_tensor(row_max[:, 2:3], row_max[:, 0:1], row_max[:, 1:2], ALU.max)\
                                .then_inc(step, 1)
                            dve.wait_ge(step, 2 * EACH * p + (at + 7))
                            apart(dve, r_free_signed)
                            nc.vector.tensor_scalar(neg_max[:, head, bass.ds(2 * p + b, 1)],
                                                    row_max[:, 2:3], -1.0, None, ALU.mult)\
                                .then_inc(r_max["signed"], 1)

            with dve.If(signed > 0):
                maxima_signed()
                dve.wait_ge(r_max["signed"], HEADS * TILES)
            with dve.Else():
                maxima_plain()

            dve.wait_ge(rows_done, 1)
            order.done(nc.vector.tensor_scalar(inv_denom[:, :, :], denom[:, :, :], float(HEADS), None, ALU.mult))
            nc.vector.reciprocal(inv_denom[:, :, :], inv_denom[:, :, :]).then_inc(k_ready, 1)
            dve.wait_ge(biases_in, 64)
            for c in range(2):
                nc.vector.tensor_tensor(bias[:, c, :], bias_in[:, 2 * c, :], bias_in[:, 2 * c + 1, :], ALU.add)\
                    .then_inc(t_ready, 1)

            def keep(c):
                c0, w = CHUNKS[c]
                dve.wait_ge(g_mm, TILES * (c + 1) + FREE)
                if c == 0:
                    dve.wait_ge(d_in, 16)
                for i in range(HEADS):
                    nc.vector.tensor_tensor(heads[:, i, c0:c0 + w], heads[:, i, c0:c0 + w],
                                            bank[3 * (c % 2) + i][:, 0:w], ALU.mult).then_inc(g_kept, 1)

            def products_signed():
                nc.vector.nop().then_inc(g_w, SLOTS)
                for c, (c0, w) in enumerate(CHUNKS):
                    if c < 2:
                        dve.wait_ge(k_in[c], 16)
                    for first, end, at in stretches(c):
                        dve.wait_ge(g_clear, 3 * c + min(first // SLOT, 2) + 1)
                        with dve.Fori(0, end - first) as p:
                            n, t = TILES * c + first, p + first
                            for s in parities:
                                for i in range(HEADS):
                                    last = nc.vector.tensor_scalar(
                                        wexp[:, s, i, 0:w], rowbuf[:, i, c0:c0 + w],
                                        h[:, bass.ds(t, 1), H + HEADS * s + i], 0.0, ALU.subtract, ALU.max)
                            last.then_inc(g_y, 1)
                            dve.wait_ge(g_e, p + (n + 1))
                            dve.wait_ge(g_mm, p + (n + 2))
                            for s, part in enumerate((ALU.max, ALU.min)):
                                for i in range(HEADS):
                                    last = nc.vector.scalar_tensor_tensor(
                                        out=wadj[:, s, i, 0:w], in0=ring[:, bass.ds(p + at, 1), 0:w].squeeze(1),
                                        scalar=0.0, in1=wexp[:, s, i, 0:w], op0=part, op1=ALU.mult)
                            last.then_inc(g_order_dve, 1)
                            dve.wait_ge(g_order_dve, p + (n + 1))
                            nc.vector.tensor_tensor(wadj[:, 0, :, 0:w], wadj[:, 0, :, 0:w],
                                                    wadj[:, 1, :, 0:w], ALU.add).then_inc(g_w, 1)
                    keep(c)

            def products_plain():
                nc.vector.nop().then_inc(g_w, SLOTS)

                def distance(c, t, k):
                    c0, w = CHUNKS[c]
                    n = TILES * c
                    dve.wait_ge(g_w, t + (n + 1))
                    for i in range(HEADS - 1):
                        last = nc.vector.tensor_scalar(wexp[:, (n + k) % SLOTS, i, 0:w], rowbuf[:, i, c0:c0 + w],
                                                       h[:, bass.ds(t, 1), H + i], 0.0, ALU.subtract, ALU.max)
                    last.then_inc(g_y, 1)

                def product(c, t, k, place):
                    c0, w = CHUNKS[c]
                    n = TILES * c
                    dve.wait_ge(g_e, t + (n + 1))
                    dve.wait_ge(g_mm, t + (n + 1))
                    nc.vector.tensor_tensor(wadj[:, k % 2, :, 0:w], wexp[:, (n + k) % SLOTS, :, 0:w],
                                            ring[:, bass.ds(place, 1), 0:w].broadcast_to([128, HEADS, w]),
                                            ALU.mult).then_inc(g_w, 1)

                dve.wait_ge(k_in[0], 16)
                distance(0, 0, 0)
                for c in range(NCH):
                    for first, end, at in stretches(c):
                        if c > 0 and first == SLOT:
                            keep(c - 1)
                        dve.wait_ge(g_clear, 3 * c + min(first // SLOT, 2) + 1)
                        if end - first < SLOTS:
                            for t in range(first, end):
                                if t + 1 < TILES:
                                    distance(c, t + 1, t + 1)
                                elif c + 1 < NCH:
                                    if c == 0:
                                        dve.wait_ge(k_in[1], 16)
                                    distance(c + 1, 0, 0)
                                product(c, t, t, at + t - first)
                            continue
                        with dve.Fori(0, (end - first) // SLOTS) as p:
                            for k in range(SLOTS):
                                distance(c, SLOTS * p + (first + k + 1), k + 1)
                                product(c, SLOTS * p + (first + k), k, SLOTS * p + (at + k))
                keep(NCH - 1)

            with dve.If(signed > 0):
                products_signed()
            with dve.Else():
                products_plain()

            nc.vector.nop().then_inc(by_dve, START)
            nc.vector.nop().then_inc(dense_order, START)
            with dve.Fori(0, BLOCKS // 2) as gg:
                for b in parities:
                    here = bass.ds((2 * gg + b) * BLOCK, BLOCK)
                    at = Steps(dve, "dve", 2 * gg + b, dense_order)
                    _, e_r, e_z, e_out, n_r, n_z, n_out = (gru_tmp[:, b, k, :] for k in range(7))

                    def candidate(gru, reset, bank_in, bank_hn, name):
                        at.settled(nc.vector.scalar_tensor_tensor(
                            out=reset, in0=bank_hn[:, 0:BLOCK], scalar=bias_in[:, 2 * gru + 1, 2:3], in1=reset,
                            op0=ALU.add, op1=ALU.mult))
                        at.step(nc.vector.scalar_tensor_tensor(
                            out=reset, in0=bank_in[:, 0:BLOCK], scalar=bias_in[:, 2 * gru, 2:3], in1=reset,
                            op0=ALU.add, op1=ALU.add), by_dve, name + " candidate")

                    def mix(out, update, cand, name):
                        at.after(by_act, "act", name + " tanh")
                        at.settled(nc.vector.tensor_tensor(out, h_t[:, here], cand, ALU.subtract))
                        at.settled(nc.vector.tensor_tensor(out, out, update, ALU.mult))
                        at.settled(nc.vector.tensor_tensor(out, out, cand, ALU.add))

                    at.after(by_act, "act", "edge gates")
                    at.after(by_pe, "pe", "edge candidate")
                    candidate(0, e_r, bank[4], bank[5], "edge")
                    at.after(by_act, "act", "node gates")
                    candidate(1, n_r, bank[7], bank[0], "node")
                    mix(e_out, e_z, e_r, "edge")
                    mix(n_out, n_z, n_r, "node")
                    at.settled(nc.vector.tensor_tensor(e_out, e_out, n_out, ALU.add))
                    dve.wait_ge(late_in, 32)
                    at.settled(nc.vector.tensor_tensor(e_out, e_out, diag_bc[:, here], ALU.mult))
                    at.step(nc.vector.tensor_tensor(x_feat[:, here], x_feat[:, here], e_out, ALU.add), by_dve, "x")
                    at.end()

            normalise(lambda t: bank[t // 4][:, t % 4 * 128:(t % 4 + 1) * 128], x_nm, n_normed,
                      lambda q: dve.wait_ge(n_turned, q + 1), twice=True)

            wide = [128, TILES, E]
            codes = iota.unsqueeze(1).broadcast_to(wide)

            def spread_out(value):
                return value.unsqueeze(2).broadcast_to(wide)

            def largest(values, best, hot):
                order.done(nc.vector.tensor_reduce(best, values, AX.X, ALU.max))
                order.done(nc.vector.tensor_tensor(picked, values, spread_out(best), ALU.is_equal))
                order.done(nc.vector.tensor_tensor(picked, picked, codes, ALU.mult))
                order.done(nc.vector.tensor_reduce(where, picked, AX.X, ALU.min))
                order.done(nc.vector.tensor_tensor(hot, codes, spread_out(where), ALU.is_equal))

            dve.wait_ge(l_psum, 1)
            order.done(nc.vector.tensor_tensor(logit, bank[7][:, 0:RW].rearrange("p (t e) -> p t e", e=E),
                                               br_bc.unsqueeze(1).broadcast_to(wide), ALU.add))
            largest(logit, first, hot1)
            order.done(nc.vector.scalar_tensor_tensor(out=rest, in0=hot1, scalar=LOWEST, in1=logit, op0=ALU.mult,
                                                      op1=ALU.add))
            largest(rest, second, hot2)
            nc.vector.tensor_tensor(gap, first, second, ALU.subtract).then_inc(l_gap, 1)
            dve.wait_ge(l_weights, 1)
            nc.vector.tensor_tensor(hot1, hot1, spread_out(w_first), ALU.mult)
            order.done(nc.vector.tensor_tensor(hot2, hot2, spread_out(w_second), ALU.mult))
            order.done(nc.vector.tensor_tensor(gate, hot1, hot2, ALU.add))
            for q in range(STAT):
                order.done(nc.vector.tensor_copy(gbf, gate))
                order.done(nc.vector.tensor_copy(gparts[:, :, q, :], gbf))
                if q < STAT - 1:
                    order.done(nc.vector.tensor_tensor(gate, gate, gparts[:, :, q, :], ALU.subtract))
            nc.vector.nop().then_inc(l_parts, 1)
            for q, tiles in GROUPS:
                w = len(tiles) * 128
                dve.wait_ge(l_gates, q + 1)
                nc.vector.tensor_copy(gates_t[0:GROWS, q * 512:q * 512 + w],
                                      gates_bf[0:GROWS, q * 512:q * 512 + w])\
                    .then_inc(l_rows, 1 if q < len(GROUPS) - 1 else BLOCKS - q)

            nc.vector.nop().then_inc(m_prod, FREE)
            nc.vector.nop().then_inc(m_out, FREE)
            for b in parities:
                nc.vector.nop().then_inc(m_stored[b], 16)
            with dve.Fori(0, BLOCKS // 2) as gg:
                for gb in parities:
                    for e in range(E):
                        b, n = e % 2, E * gb + e
                        dve.wait_ge(m_act, 2 * E * gg + (n + 1))
                        dve.wait_ge(m_gate, 2 * E * gg + (n + 1))
                        dve.wait_ge(m_used, 2 * E * gg + (n + 1))
                        nc.vector.tensor_tensor(
                            prod_h[:, b, :, :], act_h[:, b, :, :],
                            bank[4 + b][:, 0:BLOCK].unsqueeze(1).broadcast_to([128, HALVES, BLOCK]), ALU.mult)\
                            .then_inc(m_prod, 1)
                    dve.wait_ge(m_used, 2 * E * gg + (E * (gb + 1) + FREE))
                    dve.wait_ge(m_stored[gb], 16 * gg + 16)
                    nc.vector.tensor_tensor(y_sb[:, gb, :], bank[6 + gb][:, 0:BLOCK],
                                            x_feat[:, bass.ds((2 * gg + gb) * BLOCK, BLOCK)], ALU.add)\
                        .then_inc(m_out, 1)

        @block.tensor
        def _(pe):
            pe.wait_ge(small_in, 48)
            pe.wait_ge(consts, 2)
            pe.wait_ge(gatw_in, 16 * (1 + HEADS))
            for i in range(HEADS):
                last = nc.tensor.matmul(bank[2][:, 2 * i:2 * i + 2], gat_wt_sb[:, i, :], att_vec[:, i, :],
                                        start=True, stop=True)
            last.then_inc(v_psum, 1)
            for q in range(len(GROUPS) + 1):
                if q < len(GROUPS):
                    pe.wait_ge(h_ready, q + 1)
                    if q >= 2:
                        pe.wait_ge(ht_ready, q - 1)
                    for t in GROUPS[q][1]:
                        last = nc.tensor.transpose(bank[q % 2][:, t % 4 * 128:(t % 4 + 1) * 128], h[:, t, 0:H],
                                                   ident[:, :])
                    last.then_inc(ht_psum, 1)
                if q == 1:
                    pe.wait_ge(v_ready, 1)
                if q >= 1:
                    pe.wait_ge(ht_ready, q)
                    for t in GROUPS[q - 1][1]:
                        last = nc.tensor.matmul(bank[3][:, t * SCORES:(t + 1) * SCORES],
                                                h_t[:, t * 128:(t + 1) * 128], w_att[:, :], start=True, stop=True)
            last.then_inc(u_psum, 1)

            def clear(out):
                m = out.shape[0]
                return nc.tensor.matmul(out, zero_bf[:, 0:m], zero_bf[:, 0:out.shape[1]], start=True, stop=False)

            def close(out):
                m = out.shape[0]
                return nc.tensor.matmul(out, zero_bf[:, 0:m], zero_bf[:, 0:out.shape[1]], start=False, stop=True)

            pe.wait_ge(u_ready, 1)
            for c in range(NCH + 2):
                if 1 <= c <= NCH:
                    c0, w = CHUNKS[c - 1]
                    pe.wait_ge(a_kept, c)
                    if c >= 3:
                        pe.wait_ge(s_ready, c - 2)
                    nc.tensor.matmul(bank[2 + (c - 1) % 2][0:32, 0:w], sum_parts[:, :],
                                     score_parts[:, c0:c0 + w], start=True, stop=True).then_inc(s_psum, 1)
                if c >= 2:
                    c0, w = CHUNKS[c - 2]
                    pe.wait_ge(s_ready, c - 1)
                    for i in range(HEADS):
                        q = HEADS * (c - 2) + i
                        if q >= 2:
                            pe.wait_ge(b_ready, q - 1)
                        nc.tensor.matmul(bank[4 + q % 2][:, 0:w], pick_score[:, i, :], scores[:, c0:c0 + w],
                                         start=True, stop=True).then_inc(b_psum, 1)
                    for t in range(c0 // 128, (c0 + w) // 128):
                        last = nc.tensor.matmul(bank[6][:, t * SCORES:(t + 1) * SCORES],
                                                scores[:, t * 128:(t + 1) * 128], ident[0:32, 0:SCORES],
                                                start=True, stop=True)
                    last.then_inc(c_psum, 1)
                if c < NCH:
                    w = CHUNKS[c][1]
                    parts = bank[c % 2][0:32, 0:w]
                    if c == 0:
                        nc.tensor.nop().then_inc(a_used, SLOTS)

                    def add_up(t, k, first=False, last=False):
                        n = TILES * c
                        place = (n + k) % SLOTS
                        pe.wait_ge(a_tile, t + (n + 1))
                        pe.wait_ge(a_mask, t + (n + 1))
                        nc.tensor.matmul(parts, u_tile[:, place, 0:UW], masks[:, place, 0, 0:w], start=first,
                                         stop=False)
                        done = nc.tensor.matmul(parts, u_tile[:, place, UW:2 * UW], masks[:, place, 1, 0:w],
                                                start=False, stop=last)
                        done.then_inc(a_used, 1)
                        return done

                    for t in range(SLOTS):
                        add_up(t, t, first=t == 0)
                    tiles_by_four(pe, SLOTS, TILES - 1, add_up)
                    add_up(TILES - 1, (TILES - 1) % SLOTS, last=True)
            pe.wait_ge(f_ready, 1)
            signed = pe.value_load(flag[0:1, 0:1])
            pe.wait_ge(c_ready, 1)
            pe.wait_ge(b_ready, HEADS * NCH)
            for c, (c0, w) in enumerate(CHUNKS):
                last = clear(bank[c][:, 0:w])
                if c == 0:
                    last.then_inc(h_used, FREE)
                for first, end, at in stretches(c):
                    with pe.Fori(0, (end - first) // 2) as p:
                        for b in parities:
                            pe.wait_ge(h_copied, 2 * p + (TILES * c + first + b + 1))
                            nc.tensor.matmul(bank[c][:, 0:w], h_tile[:, b, 0:H],
                                             ring_h[:, bass.ds(2 * p + (at + b), 1), 0:w].squeeze(1), start=False,
                                             stop=False).then_inc(h_used, 1)
                last = close(bank[c][:, 0:w])
            last.then_inc(h_sums, 1)
            pe.wait_ge(rows_done, 1)
            nc.tensor.transpose(bank[7][0:HEADS * TILES, 0:128], neg_max[:, :, :].rearrange("p i t -> p (i t)"),
                                ident[:, :]).then_inc(k_psum, 1)
            pe.wait_ge(h_kept, NCH)
            pe.wait_ge(k_ready, 1)
            nc.tensor.transpose(bank[7][0:HEADS * TILES, 128:256], inv_denom[:, :, :].rearrange("p i t -> p (i t)"),
                                ident[:, :]).then_inc(k_psum, 1)

            def sum_heads(v):
                for c, (c0, w) in enumerate(CHUNKS):
                    if c >= 2:
                        pe.wait_ge(g_kept, HEADS * (c - 1))
                    sums = [bank[3 * (c % 2) + i][:, 0:w] for i in range(HEADS)]
                    if c == 0:
                        nc.tensor.nop().then_inc(g_mm, FREE)

                    def add_pair(p, first=False, last=False):
                        for b in parities:
                            pe.wait_ge(g_tile, 2 * p + (TILES * c + b + 1))
                            pe.wait_ge(g_w, 2 * p + (TILES * c + b + 1 + SLOTS))
                            for i in range(HEADS):
                                done = nc.tensor.matmul(sums[i], h_tile[:, b, 0:H],
                                                        wadj[:, b if v == "plain" else 0, i, 0:w],
                                                        start=first and b == 0, stop=last and b == 1)
                            done.then_inc(g_mm, 1)

                    add_pair(0, first=True)
                    with pe.Fori(1, TILES // 2 - 1) as p:
                        add_pair(p)
                    add_pair(TILES // 2 - 1, last=True)

            with pe.If(signed > 0):
                sum_heads("signed")
            with pe.Else():
                sum_heads("plain")

            nc.tensor.nop().then_inc(by_pe, START)
            pe.wait_ge(g_kept, HEADS * (NCH - 1))
            pe.wait_ge(early_in, 16 * (EARLY_LOADS + 2))
            with pe.Fori(0, BLOCKS // 2) as gg:
                for b in parities:
                    here = bass.ds((2 * gg + b) * BLOCK, BLOCK)
                    at = Steps(pe, "pe", 2 * gg + b)
                    attention = gru_tmp[:, b, 0, :]

                    def both(out, gru, a, inp):
                        wih, whh = gru_w[gru]
                        nc.tensor.matmul(out[:, 0:BLOCK], wih[:, a * H:(a + 1) * H], inp, start=True, stop=False)
                        return nc.tensor.matmul(out[:, 0:BLOCK], whh[:, a * H:(a + 1) * H], h_t[:, here],
                                                start=False, stop=True)

                    def single(out, w, inp):
                        return nc.tensor.matmul(out[:, 0:BLOCK], w[:, 2 * H:3 * H], inp, start=True, stop=True)

                    at.after(by_act, "act", "edge gates", back=1)
                    both(bank[6], 0, 0, support[:, here])
                    at.step(both(bank[3], 0, 1, support[:, here]), by_pe, "edge gates")
                    at.after(by_dve, "dve", "edge candidate", back=1)
                    single(bank[4], wih_e, support[:, here])
                    at.step(single(bank[5], whh_e, h_t[:, here]), by_pe, "edge candidate")
                    at.after(by_dve, "dve", "node candidate", back=1)
                    pe.wait_ge(g_kept, HEADS * NCH)
                    for i in range(HEADS):
                        last = nc.tensor.matmul(bank[7][:, 0:BLOCK], gat_w_sb[:, i, :], heads[:, i, here],
                                                start=(i == 0), stop=(i == HEADS - 1))
                    at.step(last, by_pe, "heads")
                    single(bank[0], whh_n, h_t[:, here])
                    at.after(by_act, "act", "node gates", back=1)
                    at.after(by_act, "act", "attention")
                    both(bank[1], 1, 0, attention)
                    both(bank[2], 1, 1, attention)
                    at.step(single(bank[7], wih_n, attention), by_pe, "node")
                    at.end()

            pe.wait_ge(by_dve, signalled("dve", BLOCKS, 0))
            for q, tiles in GROUPS:
                for t in tiles:
                    last = nc.tensor.transpose(bank[q][:, (t - tiles[0]) * 128:(t - tiles[0] + 1) * 128],
                                               x_feat[:, t * 128:(t + 1) * 128], ident[:, :])
                last.then_inc(n_turned, 1)
            for q in range(len(GROUPS) + 1):
                if q < len(GROUPS):
                    tiles = GROUPS[q][1]
                    pe.wait_ge(n_normed, q + 1)
                    for t in tiles:
                        last = nc.tensor.transpose(bank[q][:, (t - tiles[0]) * 128:(t - tiles[0] + 1) * 128],
                                                   x_nm[:, t, :], ident[:, :])
                    last.then_inc(n_back, 1)
                if q >= 1:
                    pe.wait_ge(n_input, q)
                    for t in GROUPS[q - 1][1]:
                        last = nc.tensor.matmul(bank[7][:, t * E:(t + 1) * E], xn[:, t * 128:(t + 1) * 128], wr_sb,
                                                start=True, stop=True)
            last.then_inc(l_psum, 1)
            pe.wait_ge(l_parts, 1)
            for q, tiles in GROUPS:
                for t in tiles:
                    last = nc.tensor.transpose(bank[q][0:GROWS, (t - tiles[0]) * 128:(t - tiles[0] + 1) * 128],
                                               gparts[:, t].rearrange("p q e -> p (q e)"), ident[:, :])
                last.then_inc(l_turned, 1)

            pe.wait_ge(pick_ready, 1)
            pe.wait_ge(dense_in, 32)
            nc.tensor.nop().then_inc(m_used, FREE)

            def hidden(gg, n):
                gb, e = n // E, n % E
                b = e % 2
                here = bass.ds((2 * gg + gb) * BLOCK, BLOCK)
                pe.wait_ge(m_prod, 2 * E * gg + (n + 1))
                for a in range(HALVES):
                    last = nc.tensor.matmul(bank[2 * b + a][:, 0:BLOCK], w1_sb[:, e, a * 128:(a + 1) * 128],
                                            xn[:, here], start=True, stop=True)
                last.then_inc(m_hid, 1)
                if e == 0:
                    pe.wait_ge(l_rows, 2 * gg + (gb + 1))
                nc.tensor.matmul(bank[4 + b][:, 0:BLOCK], pick_bf[0:GROWS, e, :], gates_bf[0:GROWS, here],
                                 start=True, stop=True).then_inc(m_gate, 1)

            def down(gg, n):
                gb, e = n // E, n % E
                y = bank[6 + gb][:, 0:BLOCK]
                if e == 0:
                    pe.wait_ge(m_out, 2 * gg + (gb + 1))
                    nc.tensor.matmul(y, b2_sb[0:GROWS, :], gates_t[0:GROWS, bass.ds((2 * gg + gb) * BLOCK, BLOCK)],
                                     start=True, stop=False)
                pe.wait_ge(m_prod, 2 * E * gg + (n + 1 + FREE))
                for a in range(HALVES):
                    last = nc.tensor.matmul(y, w2_sb[:, e, a, :], prod_h[:, e % 2, a, :], start=False,
                                            stop=e == E - 1 and a == HALVES - 1)
                last.then_inc(m_used, 1)

            def experts(gg, last):
                for n in range(2 * E):
                    if n + 1 < 2 * E:
                        hidden(gg, n + 1)
                    elif not last:
                        hidden(gg + 1, 0)
                    down(gg, n)

            hidden(0, 0)
            with pe.Fori(0, BLOCKS // 2 - 1) as gg:
                experts(gg, last=False)
            experts(BLOCKS // 2 - 1, last=True)


def kernel(**inputs):
    import concourse.bacc as bacc
    from concourse.bass_utils import run_bass_kernel_spmd

    def arr(name):
        return np.ascontiguousarray(inputs[name])

    x, adj = arr("x"), arr("adj")
    x_pad = np.zeros((NP, H), x.dtype)
    x_pad[:N] = x
    rows = np.zeros((NP, NP), adj.dtype)
    rows[:N, :N] = adj
    ident, sum_parts, pick_score, pick_expert, iota = host_constants()
    data = [("x", x_pad), ("x_t", x_pad.T), ("adj_rows", rows), ("adj_cols", rows.T), ("diag", rows.diagonal()),
            ("ident", ident), ("sum_parts", sum_parts), ("pick_score", pick_score),
            ("pick_expert", pick_expert), ("iota", iota), ("gat_w", arr("L0_gnn_gat_W")),
            ("gat_w_t", arr("L0_gnn_gat_W").transpose(0, 2, 1)), ("gat_a", arr("L0_gnn_gat_a")),
            ("edge_wih_t", arr("L0_gnn_edge_Wih").T), ("edge_whh_t", arr("L0_gnn_edge_Whh").T),
            ("edge_bih", arr("L0_gnn_edge_bih")), ("edge_bhh", arr("L0_gnn_edge_bhh")),
            ("node_wih_t", arr("L0_gnn_node_Wih").T), ("node_whh_t", arr("L0_gnn_node_Whh").T),
            ("node_bih", arr("L0_gnn_node_bih")), ("node_bhh", arr("L0_gnn_node_bhh")),
            ("gamma", arr("L0_ffn_gamma")), ("beta", arr("L0_ffn_beta")), ("wr", arr("L0_ffn_Wr")),
            ("br", arr("L0_ffn_br")), ("w1", arr("L0_ffn_W1")), ("b1", arr("L0_ffn_b1")),
            ("w2", arr("L0_ffn_W2")), ("b2", arr("L0_ffn_b2"))]
    nc = bacc.Bacc("TRN2", target_bir_lowering=False, num_devices=1)
    arrays, args = {}, []
    for name, a in data:
        a = np.ascontiguousarray(a)
        arrays[f"{name}_dram"] = a
        args.append(nc.dram_tensor(f"{name}_dram", a.shape, mybir.dt.from_np(a.dtype),
                                   kind="ExternalInput").ap())
    out = nc.dram_tensor("out_dram", (H, NP), mybir.dt.float32, kind="ExternalOutput").ap()
    scratch = [nc.dram_tensor(name, (SCORES, NP), mybir.dt.float32, kind="Internal").ap()
               for name in ("scores_dram", "stats_dram")]
    graph_layer_kernel(nc, *args, out, *scratch)
    result = run_bass_kernel_spmd(nc, [arrays], core_ids=[0])
    return np.ascontiguousarray(result.results[0]["out_dram"][:, :N].T)
```
